# Optimizing a Trainium2 kernel written in Bass

```python
import numpy as np
import jax
import jax.numpy as jnp

def _softmax(x, axis=-1):
    return jax.nn.softmax(x, axis=axis)

def _gelu(x):
    return jax.nn.gelu(x, approximate=True)

def _silu(x):
    return jax.nn.silu(x)

def _sigmoid(x):
    return jax.nn.sigmoid(x)

def _layernorm(x, axis=-1, eps=1e-05):
    m = jnp.mean(x, axis=axis, keepdims=True)
    v = jnp.var(x, axis=axis, keepdims=True)
    return (x - m) / jnp.sqrt(v + eps)

def _scatter_add(tgt, idx, src, axis=0):
    return tgt.at[idx].add(src)

def _segment_sum(src, seg, n):
    return jax.ops.segment_sum(src, seg, n)
kernel_name = 'mk_perceiver_d4_seqx_r8_3ca508'

def setup_inputs(seed: int=0):
    np.random.seed(seed)
    _w = jnp.asarray

    def _rec_inputs():
        import jax
        import jax.numpy as jnp
        _rk = jax.random.key(seed)
        x = -0.0003929 + 0.9999 * jax.random.normal(jax.random.fold_in(_rk, 1), (1, 128, 512), jnp.float32)
        _lenS = 128 - jax.random.randint(jax.random.fold_in(_rk, 7), (1,), 0, max(1, 128 // 4) + 1, jnp.int32)
        _lenS2 = 2048 - jax.random.randint(jax.random.fold_in(_rk, 8), (1,), 0, max(1, 2048 // 4) + 1, jnp.int32)
        _ctx_4096P = jax.random.normal(jax.random.fold_in(_rk, 11), (1, 16, 512), jnp.float32)
        _ctx_4096c = jax.random.dirichlet(jax.random.fold_in(_rk, 511), 0.3 * jnp.ones((16,), jnp.float32), (1, 2048))
        _ctx_4096t = jnp.einsum('bsk,bkd->bsd', _ctx_4096c, _ctx_4096P)
        _ctx_4096t = _ctx_4096t * jax.lax.rsqrt(jnp.mean(jnp.square(_ctx_4096t)) + 1e-12) * 0.953939
        ctx_4096 = 2.81802e-05 + 1.00001 * (_ctx_4096t + 0.3 * jax.random.normal(jax.random.fold_in(_rk, 611), (1, 2048, 512), jnp.float32))
        _validS = jnp.arange(128)[None, :] < _lenS[:, None]
        _validS2 = jnp.arange(2048)[None, :] < _lenS2[:, None]
        _causal = jnp.tril(jnp.ones((128, 128), dtype=bool))
        mask_BxSxS2_ff0 = jnp.where(jnp.ones((1, 128, 2048), dtype=bool), 0.0, -1000000000.0).astype(jnp.float32)
        mask_SxS2_bk0 = jnp.logical_not(jnp.broadcast_to(_validS2[0:1, :], (128, 2048)))
        mask_1x1xSxS2_ff0 = jnp.where(jnp.ones((1, 1, 128, 2048), dtype=bool), 0.0, -1000000000.0).astype(jnp.float32)
        return (x, ctx_4096, mask_BxSxS2_ff0, mask_SxS2_bk0, mask_1x1xSxS2_ff0)
    x, ctx_4096, mask_BxSxS2_ff0, mask_SxS2_bk0, mask_1x1xSxS2_ff0 = _rec_inputs()

    def _L0_xattn_setup():
        import jax, jax.numpy as jnp
        import numpy as np
        BS, SEQ, D_MODEL = (4, 128, 512)
        N_Q_HEADS, N_KV_HEADS, D_K, D_V = (32, 8, 128, 128)
        ROPE_BASE = 10000.0

        def _rotate_half(x):
            x1, x2 = jnp.split(x, 2, axis=-1)
            return jnp.concatenate([-x2, x1], axis=-1)

        def _apply_rope(x, pos0):
            d = x.shape[-1]
            seq = x.shape[2]
            inv_freq = 1.0 / ROPE_BASE ** (jnp.arange(0, d, 2, dtype=jnp.float32) / d)
            pos = (pos0 + jnp.arange(seq)).astype(jnp.float32)
            ang = pos[:, None] * inv_freq[None, :]
            cos = jnp.concatenate([jnp.cos(ang), jnp.cos(ang)], axis=-1)
            sin = jnp.concatenate([jnp.sin(ang), jnp.sin(ang)], axis=-1)
            return x * cos[None, None] + _rotate_half(x) * sin[None, None]
        key = jax.random.key(seed)
        ks = jax.random.split(key, 8)
        w_scale = 0.02
        return {'query': jax.random.normal(ks[0], (BS, SEQ, D_MODEL), dtype=jnp.float32), 'key': jax.random.normal(ks[1], (BS, SEQ, D_MODEL), dtype=jnp.float32), 'value': jax.random.normal(ks[2], (BS, SEQ, D_MODEL), dtype=jnp.float32), 'mask': jnp.zeros((BS, SEQ, SEQ), dtype=jnp.float32), 'wq': jax.random.normal(ks[3], (D_MODEL, N_Q_HEADS * D_K), dtype=jnp.float32) * w_scale, 'wk': jax.random.normal(ks[4], (D_MODEL, N_KV_HEADS * D_K), dtype=jnp.float32) * w_scale, 'wv': jax.random.normal(ks[5], (D_MODEL, N_KV_HEADS * D_V), dtype=jnp.float32) * w_scale, 'wo': jax.random.normal(ks[6], (N_Q_HEADS * D_V, D_MODEL), dtype=jnp.float32) * w_scale, 'curr_seq_pos': 0}
    _L0_xattn_all = _L0_xattn_setup()
    _L0_xattn_in = {k: v for k, v in _L0_xattn_all.items() if k in ('wq', 'wk', 'wv', 'wo')}
    del _L0_xattn_all

    def _L0_attn_setup():
        import jax, jax.numpy as jnp
        import numpy as np
        HIDDEN = 512
        NUM_HEADS = 32
        HEAD_DIM = HIDDEN // NUM_HEADS
        THRESH = 0.001
        key = jax.random.key(seed)
        ks = jax.random.split(key, 9)
        w_std = 0.02
        x = jax.random.normal(ks[0], (4, 512, HIDDEN), dtype=jnp.float32)
        Wq = jax.random.normal(ks[1], (HIDDEN, HIDDEN), dtype=jnp.float32) * w_std
        bq = jax.random.normal(ks[2], (HIDDEN,), dtype=jnp.float32) * w_std
        Wk = jax.random.normal(ks[3], (HIDDEN, HIDDEN), dtype=jnp.float32) * w_std
        bk = jax.random.normal(ks[4], (HIDDEN,), dtype=jnp.float32) * w_std
        Wv = jax.random.normal(ks[5], (HIDDEN, HIDDEN), dtype=jnp.float32) * w_std
        bv = jax.random.normal(ks[6], (HIDDEN,), dtype=jnp.float32) * w_std
        Wo = jax.random.normal(ks[7], (HIDDEN, HIDDEN), dtype=jnp.float32) * w_std
        bo = jax.random.normal(ks[8], (HIDDEN,), dtype=jnp.float32) * w_std
        return {'x': x, 'Wq': Wq, 'bq': bq, 'Wk': Wk, 'bk': bk, 'Wv': Wv, 'bv': bv, 'Wo': Wo, 'bo': bo}
    _L0_attn_all = _L0_attn_setup()
    _L0_attn_in = {k: v for k, v in _L0_attn_all.items() if k in ('Wq', 'bq', 'Wk', 'bk', 'Wv', 'bv', 'Wo', 'bo')}
    del _L0_attn_all

    def _L0_ffn_setup():
        import jax, jax.numpy as jnp
        import numpy as np
        LORA_RANK = 16
        LORA_ALPHA = 16
        LORA_SCALE = LORA_ALPHA / LORA_RANK
        key = jax.random.key(seed)
        k1, k2, k3, k4, k5 = jax.random.split(key, 5)
        B, S, D_IN, D_OUT, N_LORA, R = (8, 256, 512, 512, 3, LORA_RANK)
        std = 1.0 / np.sqrt(D_IN)
        x = jax.random.normal(k1, (B, S, D_IN), dtype=jnp.float32)
        weight = jax.random.truncated_normal(k2, -3.0, 3.0, (D_OUT, D_IN), dtype=jnp.float32) * std
        bias = jax.random.normal(k3, (D_OUT,), dtype=jnp.float32) * 0.01
        lora_A = jax.random.normal(k4, (N_LORA, R, D_IN), dtype=jnp.float32) * std
        lora_B = jax.random.normal(k5, (N_LORA, D_OUT, R), dtype=jnp.float32) * 0.02
        lora_start_indices = jnp.arange(4, dtype=jnp.int64) * 2
        return {'x': x, 'weight': weight, 'bias': bias, 'lora_A': lora_A, 'lora_B': lora_B, 'lora_start_indices': lora_start_indices}
    _L0_ffn_all = _L0_ffn_setup()
    _L0_ffn_in = {k: v for k, v in _L0_ffn_all.items() if k in ('weight', 'bias', 'lora_A', 'lora_B', 'lora_start_indices')}
    del _L0_ffn_all

    def _L1_xattn_setup():
        import jax, jax.numpy as jnp
        import numpy as np
        EPS = 1e-06

        def rmsnorm(x, w):
            xf = x.astype(jnp.float32)
            var = jnp.mean(xf * xf, axis=-1, keepdims=True)
            return (xf * jax.lax.rsqrt(var + EPS)).astype(x.dtype) * w
        key = jax.random.key(seed)
        ks = jax.random.split(key, 6)
        B, T, S, Dt, Df = (4, 128, 72, 512, 512)
        text = jax.random.normal(ks[0], (B, T, Dt), dtype=jnp.float32)
        features = jax.random.normal(ks[1], (B, S, Df), dtype=jnp.float32)
        lim_q = float(np.sqrt(6.0 / (Dt + Df)))
        lim_k = float(np.sqrt(6.0 / (Df + Df)))
        Wq_w = jax.random.uniform(ks[2], (Df, Dt), minval=-lim_q, maxval=lim_q, dtype=jnp.float32)
        Wk_w = jax.random.uniform(ks[3], (Df, Df), minval=-lim_k, maxval=lim_k, dtype=jnp.float32)
        bq = 1.0 / np.sqrt(Dt)
        bk = 1.0 / np.sqrt(Df)
        Wq_b = jax.random.uniform(ks[4], (Df,), minval=-bq, maxval=bq, dtype=jnp.float32)
        Wk_b = jax.random.uniform(ks[5], (Df,), minval=-bk, maxval=bk, dtype=jnp.float32)
        fn_w = jnp.ones((Df,), dtype=jnp.float32)
        qn_w = jnp.ones((Df,), dtype=jnp.float32)
        kn_w = jnp.ones((Df,), dtype=jnp.float32)
        return {'text': text, 'features': features, 'Wq_w': Wq_w, 'Wq_b': Wq_b, 'Wk_w': Wk_w, 'Wk_b': Wk_b, 'fn_w': fn_w, 'qn_w': qn_w, 'kn_w': kn_w}
    _L1_xattn_all = _L1_xattn_setup()
    _L1_xattn_in = {k: v for k, v in _L1_xattn_all.items() if k in ('Wq_w', 'Wq_b', 'Wk_w', 'Wk_b', 'fn_w', 'qn_w', 'kn_w')}
    del _L1_xattn_all

    def _L1_attn_setup():
        import jax, jax.numpy as jnp
        import numpy as np
        B, S, HID = (1, 256, 512)
        H, NOPE, ROPE, VD = (32, 128, 64, 128)
        QKD = NOPE + ROPE
        Q_RANK, KV_RANK = (192, 64)
        IDX_H, IDX_D, TOPK = (16, 128, 128)
        EPS, THETA = (1e-05, 10000.0)

        def rmsnorm(x, w):
            return x * jax.lax.rsqrt(jnp.mean(x * x, axis=-1, keepdims=True) + EPS) * w

        def rope_interleaved(x, pos):
            d = x.shape[-1]
            inv_freq = 1.0 / THETA ** (jnp.arange(0, d, 2, dtype=jnp.float32) / d)
            ang = pos[:, None] * inv_freq[None, :]
            cos, sin = (jnp.cos(ang), jnp.sin(ang))
            x2 = x.reshape(*x.shape[:-1], d // 2, 2)
            x0, x1 = (x2[..., 0], x2[..., 1])
            return jnp.stack([x0 * cos - x1 * sin, x1 * cos + x0 * sin], axis=-1).reshape(x.shape)
        key = jax.random.key(seed)
        ks = jax.random.split(key, 12)
        s = 0.02
        return {'hidden_states': jax.random.normal(ks[0], (B, S, HID), jnp.float32), 'q_a_w': jax.random.normal(ks[1], (HID, Q_RANK), jnp.float32) * s, 'q_a_norm_w': jnp.ones((Q_RANK,), jnp.float32), 'q_b_w': jax.random.normal(ks[2], (Q_RANK, H * QKD), jnp.float32) * s, 'kv_a_w': jax.random.normal(ks[3], (HID, KV_RANK + ROPE), jnp.float32) * s, 'kv_a_norm_w': jnp.ones((KV_RANK,), jnp.float32), 'kv_b_w': jax.random.normal(ks[4], (KV_RANK, H * (NOPE + VD)), jnp.float32) * s, 'o_w': jax.random.normal(ks[5], (H * VD, HID), jnp.float32) * s, 'idx_wq_w': jax.random.normal(ks[6], (HID, IDX_H * IDX_D), jnp.float32) * s, 'idx_wk_w': jax.random.normal(ks[7], (HID, IDX_D), jnp.float32) * s, 'idx_weights_w': jax.random.normal(ks[8], (HID, IDX_H), jnp.float32) * s}
    _L1_attn_all = _L1_attn_setup()
    _L1_attn_in = {k: v for k, v in _L1_attn_all.items() if k in ('q_a_w', 'q_a_norm_w', 'q_b_w', 'kv_a_w', 'kv_a_norm_w', 'kv_b_w', 'o_w', 'idx_wq_w', 'idx_wk_w', 'idx_weights_w')}
    del _L1_attn_all

    def _L1_ffn_setup():
        import jax, jax.numpy as jnp
        import numpy as np
        B, S, D_IN, D_OUT = (2, 256, 512, 512)
        E, K, R = (8, 2, 16)
        SCALING = 32.0 / 16.0
        key = jax.random.key(seed)
        ks = jax.random.split(key, 6)
        x = jax.random.normal(ks[0], (B, S, D_IN), dtype=jnp.float32)
        gate_w = jax.random.normal(ks[1], (E, D_IN), dtype=jnp.float32) * 0.02
        base_w = jax.random.normal(ks[2], (D_OUT, D_IN), dtype=jnp.float32) * 0.02
        base_b = jax.random.normal(ks[3], (D_OUT,), dtype=jnp.float32) * 0.02
        lora_A = jax.random.normal(ks[4], (E, R, D_IN), dtype=jnp.float32) * 0.02
        lora_B = jax.random.normal(ks[5], (E, D_OUT, R), dtype=jnp.float32) * 0.02
        return {'x': x, 'gate_w': gate_w, 'base_w': base_w, 'base_b': base_b, 'lora_A': lora_A, 'lora_B': lora_B}
    _L1_ffn_all = _L1_ffn_setup()
    _L1_ffn_in = {k: v for k, v in _L1_ffn_all.items() if k in ('gate_w', 'base_w', 'base_b', 'lora_A', 'lora_B')}
    del _L1_ffn_all

    def _L2_xattn_setup():
        import jax, jax.numpy as jnp
        import numpy as np
        N_HEAD = 32
        D_MODEL = 512
        N_KV_GROUPS = 8
        D_HEAD = D_MODEL // N_HEAD
        H_PER_G = N_HEAD // N_KV_GROUPS
        KV_DIM = N_KV_GROUPS * D_HEAD
        B, S = (2, 256)
        key = jax.random.key(seed)
        ks = jax.random.split(key, 8)
        q = jax.random.normal(ks[0], (B, S, D_MODEL), dtype=jnp.float32)
        k = jax.random.normal(ks[1], (B, S, D_MODEL), dtype=jnp.float32)
        v = jax.random.normal(ks[2], (B, S, D_MODEL), dtype=jnp.float32)
        mask = jnp.tril(jnp.ones((S, S), dtype=bool))
        w_q = jax.random.uniform(ks[3], (D_MODEL, D_MODEL), dtype=jnp.float32) * 0.02
        w_k = jax.random.uniform(ks[4], (KV_DIM, D_MODEL), dtype=jnp.float32) * 0.02
        w_v = jax.random.uniform(ks[5], (KV_DIM, D_MODEL), dtype=jnp.float32) * 0.02
        w_out = jax.random.uniform(ks[6], (D_MODEL, D_MODEL), dtype=jnp.float32) * 0.02
        return {'q': q, 'k': k, 'v': v, 'w_q': w_q, 'w_k': w_k, 'w_v': w_v, 'w_out': w_out, 'mask': mask}
    _L2_xattn_all = _L2_xattn_setup()
    _L2_xattn_in = {k: v for k, v in _L2_xattn_all.items() if k in ('w_q', 'w_k', 'w_v', 'w_out')}
    del _L2_xattn_all

    def _L2_attn_setup():
        import jax, jax.numpy as jnp
        import numpy as np
        H = 512
        NH = 32
        QR = 192
        KVR = 64
        RD = 64
        ND = 128
        VD = 128
        QK = RD + ND
        EPS = 1e-06
        THETA = 10000.0
        B, S = (2, 128)

        def rmsnorm(x, w):
            norm = jnp.sqrt(jnp.sum(x * x, axis=-1, keepdims=True)) * x.shape[-1] ** (-0.5)
            return x / (norm + EPS) * w

        def rope_cos_sin(seq_len):
            inv_freq = 1.0 / THETA ** (jnp.arange(0, RD, 2, dtype=jnp.float32) / RD)
            t = jnp.arange(seq_len, dtype=jnp.float32)
            freqs = jnp.outer(t, inv_freq)
            emb = jnp.concatenate([freqs, freqs], -1)
            return (jnp.cos(emb), jnpp_cos_sin_dummy() if False else jnp.sin(emb))

        def rotate_half(x):
            x1, x2 = jnp.split(x, 2, axis=-1)
            return jnp.concatenate([-x2, x1], axis=-1)
        key = jax.random.key(seed)
        ks = jax.random.split(key, 8)
        sc = 0.02
        return {'hidden_states': jax.random.normal(ks[0], (B, S, H), jnp.float32), 'w_qa': jax.random.normal(ks[1], (H, QR), jnp.float32) * sc, 'g_qa': jnp.ones((QR,), jnp.float32), 'w_qb': jax.random.normal(ks[2], (QR, NH * QK), jnp.float32) * sc, 'w_kva': jax.random.normal(ks[3], (H, KVR + RD), jnp.float32) * sc, 'g_kva': jnp.ones((KVR,), jnp.float32), 'w_kvb': jax.random.normal(ks[4], (KVR, NH * (ND + VD)), jnp.float32) * sc, 'w_o': jax.random.normal(ks[5], (NH * VD, H), jnp.float32) * sc}
    _L2_attn_all = _L2_attn_setup()
    _L2_attn_in = {k: v for k, v in _L2_attn_all.items() if k in ('w_qa', 'g_qa', 'w_qb', 'w_kva', 'g_kva', 'w_kvb', 'w_o')}
    del _L2_attn_all

    def _L2_ffn_setup():
        import jax, jax.numpy as jnp
        import numpy as np
        import math
        B, S, IN, OUT = (4, 256, 512, 512)
        E, R, K = (8, 64, 128)
        SCALE = 64.0 / 64.0
        MULTIPLIER = 1.0
        key = jax.random.key(seed)
        ks = jax.random.split(key, 6)
        return {'x': jax.random.normal(ks[0], (B, S, IN), jnp.float32), 'W_org': jax.random.normal(ks[1], (OUT, IN), jnp.float32) * 0.02, 'lora_down': jax.random.normal(ks[2], (E, IN, R), jnp.float32) * 0.02, 'lora_up': jax.random.normal(ks[3], (E, R, OUT), jnp.float32) * 0.02, 'lora_keys': jax.random.normal(ks[4], (E, K), jnp.float32), 'Wq': jax.random.normal(ks[5], (K, IN), jnp.float32) * 0.02}
    _L2_ffn_all = _L2_ffn_setup()
    _L2_ffn_in = {k: v for k, v in _L2_ffn_all.items() if k in ('W_org', 'lora_down', 'lora_up', 'lora_keys', 'Wq')}
    del _L2_ffn_all

    def _L3_xattn_setup():
        import jax, jax.numpy as jnp
        import numpy as np
        NUM_HEADS = 32
        NUM_KV_HEADS = 8
        HEAD_DIM = 128
        HIDDEN = 512
        EPS = 1e-05

        def rmsnorm(x, w, eps=EPS):
            xf = x.astype(jnp.float32)
            var = jnp.mean(xf * xf, axis=-1, keepdims=True)
            return w * (xf * jax.lax.rsqrt(var + eps)).astype(x.dtype)
        key = jax.random.key(seed)
        ks = jax.random.split(key, 10)
        B, Q, KV = (1, 128, 6404)
        s = 1.0 / np.sqrt(HIDDEN)
        return {'hidden_states': jax.random.normal(ks[0], (B, Q, HIDDEN), jnp.float32), 'cross_attention_states': jax.random.normal(ks[1], (B, KV, HIDDEN), jnp.float32), 'attention_mask': jnp.zeros((B, 1, Q, KV), jnp.float32), 'q_proj_w': jax.random.normal(ks[2], (NUM_HEADS * HEAD_DIM, HIDDEN), jnp.float32) * s, 'k_proj_w': jax.random.normal(ks[3], (NUM_KV_HEADS * HEAD_DIM, HIDDEN), jnp.float32) * s, 'v_proj_w': jax.random.normal(ks[4], (NUM_KV_HEADS * HEAD_DIM, HIDDEN), jnp.float32) * s, 'o_proj_w': jax.random.normal(ks[5], (HIDDEN, NUM_HEADS * HEAD_DIM), jnp.float32) * s, 'q_norm_w': jnp.ones((HEAD_DIM,), jnp.float32), 'k_norm_w': jnp.ones((HEAD_DIM,), jnp.float32)}
    _L3_xattn_all = _L3_xattn_setup()
    _L3_xattn_in = {k: v for k, v in _L3_xattn_all.items() if k in ('q_proj_w', 'k_proj_w', 'v_proj_w', 'o_proj_w', 'q_norm_w', 'k_norm_w')}
    del _L3_xattn_all

    def _L3_attn_setup():
        import jax, jax.numpy as jnp
        import numpy as np
        H = 512
        D = H // 4
        key = jax.random.key(seed)
        k1, k2, k3, k4, k5 = jax.random.split(key, 5)
        x = jax.random.normal(k1, (4, 512, H), dtype=jnp.float32)
        s_in = 1.0 / np.sqrt(H)
        Wqkv = jax.random.normal(k2, (H, 3 * D), dtype=jnp.float32) * s_in
        bqkv = jax.random.normal(k3, (3 * D,), dtype=jnp.float32) * 0.01
        Wo = jax.random.normal(k4, (D, H), dtype=jnp.float32) * (1.0 / np.sqrt(D))
        bo = jax.random.normal(k5, (H,), dtype=jnp.float32) * 0.01
        return {'x': x, 'Wqkv': Wqkv, 'bqkv': bqkv, 'Wo': Wo, 'bo': bo}
    _L3_attn_all = _L3_attn_setup()
    _L3_attn_in = {k: v for k, v in _L3_attn_all.items() if k in ('Wqkv', 'bqkv', 'Wo', 'bo')}
    del _L3_attn_all

    def _L3_ffn_setup():
        import jax, jax.numpy as jnp
        import numpy as np
        IN_F = 512
        OUT_F = 512
        C = 32
        NCL = 32
        SUB = IN_F // C
        CLS = OUT_F // NCL
        SIGMA = 10.0
        THRESH = 0.5

        def _expand(codes, codebooks):
            w = codebooks[jnp.arange(codes.shape[0])[:, None], codes]
            return jnp.transpose(w, (1, 0, 2)).reshape(codes.shape[1], -1)
        key = jax.random.key(seed)
        ks = jax.random.split(key, 6)
        x = jax.random.normal(ks[0], (4, 256, IN_F), dtype=jnp.float32)
        codebooks = jax.random.normal(ks[1], (C, 32, SUB), dtype=jnp.float32) * 0.025
        centroids = jax.random.randint(ks[2], (NCL, C), 0, 32, dtype=jnp.int32)
        codes = jnp.repeat(centroids, CLS, axis=0)
        n_pert = max(1, round(0.25 * C))
        psel = jax.random.randint(ks[3], (OUT_F, n_pert), 0, C, dtype=jnp.int32)
        prep = jax.random.randint(ks[4], (OUT_F, n_pert), 0, 32, dtype=jnp.int32)
        rows = jnp.arange(OUT_F)[:, None]
        codes = codes.at[rows, psel].set(prep)
        bound = 1.0 / np.sqrt(IN_F)
        bias = jax.random.uniform(ks[5], (OUT_F,), dtype=jnp.float32, minval=-bound, maxval=bound)
        ln_weight = jnp.ones((NCL,), dtype=jnp.float32) * SIGMA
        return {'x': x, 'codebooks': codebooks, 'bias': bias, 'ln_weight': ln_weight, 'codes': codes.T.astype(jnp.int32), 'centroids': centroids.T.astype(jnp.int32)}
    _L3_ffn_all = _L3_ffn_setup()
    _L3_ffn_in = {k: v for k, v in _L3_ffn_all.items() if k in ('codebooks', 'bias', 'ln_weight', 'codes', 'centroids')}
    del _L3_ffn_all
    return {'x': x, 'ctx_4096': ctx_4096, 'mask_BxSxS2_ff0': mask_BxSxS2_ff0, 'mask_SxS2_bk0': mask_SxS2_bk0, 'mask_1x1xSxS2_ff0': mask_1x1xSxS2_ff0, 'L0_xattn_wq': _L0_xattn_in['wq'], 'L0_xattn_wk': _L0_xattn_in['wk'], 'L0_xattn_wv': _L0_xattn_in['wv'], 'L0_xattn_wo': _L0_xattn_in['wo'], 'L0_attn_Wq': _L0_attn_in['Wq'], 'L0_attn_bq': _L0_attn_in['bq'], 'L0_attn_Wk': _L0_attn_in['Wk'], 'L0_attn_bk': _L0_attn_in['bk'], 'L0_attn_Wv': _L0_attn_in['Wv'], 'L0_attn_bv': _L0_attn_in['bv'], 'L0_attn_Wo': _L0_attn_in['Wo'], 'L0_attn_bo': _L0_attn_in['bo'], 'L0_ffn_weight': _L0_ffn_in['weight'], 'L0_ffn_bias': _L0_ffn_in['bias'], 'L0_ffn_lora_A': _L0_ffn_in['lora_A'], 'L0_ffn_lora_B': _L0_ffn_in['lora_B'], 'L0_ffn_lora_start_indices': _L0_ffn_in['lora_start_indices'], 'L1_xattn_Wq_w': _L1_xattn_in['Wq_w'], 'L1_xattn_Wq_b': _L1_xattn_in['Wq_b'], 'L1_xattn_Wk_w': _L1_xattn_in['Wk_w'], 'L1_xattn_Wk_b': _L1_xattn_in['Wk_b'], 'L1_xattn_fn_w': _L1_xattn_in['fn_w'], 'L1_xattn_qn_w': _L1_xattn_in['qn_w'], 'L1_xattn_kn_w': _L1_xattn_in['kn_w'], 'L1_attn_q_a_w': _L1_attn_in['q_a_w'], 'L1_attn_q_a_norm_w': _L1_attn_in['q_a_norm_w'], 'L1_attn_q_b_w': _L1_attn_in['q_b_w'], 'L1_attn_kv_a_w': _L1_attn_in['kv_a_w'], 'L1_attn_kv_a_norm_w': _L1_attn_in['kv_a_norm_w'], 'L1_attn_kv_b_w': _L1_attn_in['kv_b_w'], 'L1_attn_o_w': _L1_attn_in['o_w'], 'L1_attn_idx_wq_w': _L1_attn_in['idx_wq_w'], 'L1_attn_idx_wk_w': _L1_attn_in['idx_wk_w'], 'L1_attn_idx_weights_w': _L1_attn_in['idx_weights_w'], 'L1_ffn_gate_w': _L1_ffn_in['gate_w'], 'L1_ffn_base_w': _L1_ffn_in['base_w'], 'L1_ffn_base_b': _L1_ffn_in['base_b'], 'L1_ffn_lora_A': _L1_ffn_in['lora_A'], 'L1_ffn_lora_B': _L1_ffn_in['lora_B'], 'L2_xattn_w_q': _L2_xattn_in['w_q'], 'L2_xattn_w_k': _L2_xattn_in['w_k'], 'L2_xattn_w_v': _L2_xattn_in['w_v'], 'L2_xattn_w_out': _L2_xattn_in['w_out'], 'L2_attn_w_qa': _L2_attn_in['w_qa'], 'L2_attn_g_qa': _L2_attn_in['g_qa'], 'L2_attn_w_qb': _L2_attn_in['w_qb'], 'L2_attn_w_kva': _L2_attn_in['w_kva'], 'L2_attn_g_kva': _L2_attn_in['g_kva'], 'L2_attn_w_kvb': _L2_attn_in['w_kvb'], 'L2_attn_w_o': _L2_attn_in['w_o'], 'L2_ffn_W_org': _L2_ffn_in['W_org'], 'L2_ffn_lora_down': _L2_ffn_in['lora_down'], 'L2_ffn_lora_up': _L2_ffn_in['lora_up'], 'L2_ffn_lora_keys': _L2_ffn_in['lora_keys'], 'L2_ffn_Wq': _L2_ffn_in['Wq'], 'L3_xattn_q_proj_w': _L3_xattn_in['q_proj_w'], 'L3_xattn_k_proj_w': _L3_xattn_in['k_proj_w'], 'L3_xattn_v_proj_w': _L3_xattn_in['v_proj_w'], 'L3_xattn_o_proj_w': _L3_xattn_in['o_proj_w'], 'L3_xattn_q_norm_w': _L3_xattn_in['q_norm_w'], 'L3_xattn_k_norm_w': _L3_xattn_in['k_norm_w'], 'L3_attn_Wqkv': _L3_attn_in['Wqkv'], 'L3_attn_bqkv': _L3_attn_in['bqkv'], 'L3_attn_Wo': _L3_attn_in['Wo'], 'L3_attn_bo': _L3_attn_in['bo'], 'L3_ffn_codebooks': _L3_ffn_in['codebooks'], 'L3_ffn_bias': _L3_ffn_in['bias'], 'L3_ffn_ln_weight': _L3_ffn_in['ln_weight'], 'L3_ffn_codes': _L3_ffn_in['codes'], 'L3_ffn_centroids': _L3_ffn_in['centroids']}

def reference(x, ctx_4096, mask_BxSxS2_ff0, mask_SxS2_bk0, mask_1x1xSxS2_ff0, L0_xattn_wq, L0_xattn_wk, L0_xattn_wv, L0_xattn_wo, L0_attn_Wq, L0_attn_bq, L0_attn_Wk, L0_attn_bk, L0_attn_Wv, L0_attn_bv, L0_attn_Wo, L0_attn_bo, L0_ffn_weight, L0_ffn_bias, L0_ffn_lora_A, L0_ffn_lora_B, L0_ffn_lora_start_indices, L1_xattn_Wq_w, L1_xattn_Wq_b, L1_xattn_Wk_w, L1_xattn_Wk_b, L1_xattn_fn_w, L1_xattn_qn_w, L1_xattn_kn_w, L1_attn_q_a_w, L1_attn_q_a_norm_w, L1_attn_q_b_w, L1_attn_kv_a_w, L1_attn_kv_a_norm_w, L1_attn_kv_b_w, L1_attn_o_w, L1_attn_idx_wq_w, L1_attn_idx_wk_w, L1_attn_idx_weights_w, L1_ffn_gate_w, L1_ffn_base_w, L1_ffn_base_b, L1_ffn_lora_A, L1_ffn_lora_B, L2_xattn_w_q, L2_xattn_w_k, L2_xattn_w_v, L2_xattn_w_out, L2_attn_w_qa, L2_attn_g_qa, L2_attn_w_qb, L2_attn_w_kva, L2_attn_g_kva, L2_attn_w_kvb, L2_attn_w_o, L2_ffn_W_org, L2_ffn_lora_down, L2_ffn_lora_up, L2_ffn_lora_keys, L2_ffn_Wq, L3_xattn_q_proj_w, L3_xattn_k_proj_w, L3_xattn_v_proj_w, L3_xattn_o_proj_w, L3_xattn_q_norm_w, L3_xattn_k_norm_w, L3_attn_Wqkv, L3_attn_bqkv, L3_attn_Wo, L3_attn_bo, L3_ffn_codebooks, L3_ffn_bias, L3_ffn_ln_weight, L3_ffn_codes, L3_ffn_centroids):
    import jax
    import jax.numpy as jnp

    def _L0_xattn_ref(query, key, value, mask, wq, wk, wv, wo, curr_seq_pos):
        import jax, jax.numpy as jnp
        import numpy as np
        BS, SEQ, D_MODEL = (4, 128, 512)
        N_Q_HEADS, N_KV_HEADS, D_K, D_V = (32, 8, 128, 128)
        ROPE_BASE = 10000.0

        def _rotate_half(x):
            x1, x2 = jnp.split(x, 2, axis=-1)
            return jnp.concatenate([-x2, x1], axis=-1)

        def _apply_rope(x, pos0):
            d = x.shape[-1]
            seq = x.shape[2]
            inv_freq = 1.0 / ROPE_BASE ** (jnp.arange(0, d, 2, dtype=jnp.float32) / d)
            pos = (pos0 + jnp.arange(seq)).astype(jnp.float32)
            ang = pos[:, None] * inv_freq[None, :]
            cos = jnp.concatenate([jnp.cos(ang), jnp.cos(ang)], axis=-1)
            sin = jnp.concatenate([jnp.sin(ang), jnp.sin(ang)], axis=-1)
            return x * cos[None, None] + _rotate_half(x) * sin[None, None]
        bs, sq, _ = query.shape
        n_groups = N_Q_HEADS // N_KV_HEADS
        q = (query @ wq).reshape(bs, sq, N_Q_HEADS, D_K).transpose((0, 2, 1, 3))
        sk = key.shape[1]
        k = (key @ wk).reshape(bs, sk, N_KV_HEADS, 1, D_K)
        k = jnp.repeat(k, n_groups, axis=3).reshape(bs, sk, N_Q_HEADS, D_K).transpose((0, 2, 1, 3))
        v = (value @ wv).reshape(bs, sk, N_KV_HEADS, 1, D_V)
        v = jnp.repeat(v, n_groups, axis=3).reshape(bs, sk, N_Q_HEADS, D_V).transpose((0, 2, 1, 3))
        scale = jnp.sqrt(jnp.float32(D_K))
        q = _apply_rope(q, curr_seq_pos)
        k = _apply_rope(k, curr_seq_pos)
        raw = jnp.einsum('bhqd,bhkd->bhqk', q, k) / scale
        masked = raw + mask[:bs, None, curr_seq_pos:curr_seq_pos + sq, :sk]
        attn = jax.nn.softmax(masked, axis=-1)
        out = jnp.einsum('bhqk,bhkd->bhqd', attn, v)
        out = out.transpose((0, 2, 1, 3)).reshape(bs, sq, N_Q_HEADS * D_V)
        return out @ wo

    def _L0_attn_ref(x, Wq, bq, Wk, bk, Wv, bv, Wo, bo):
        import jax, jax.numpy as jnp
        import numpy as np
        HIDDEN = 512
        NUM_HEADS = 32
        HEAD_DIM = HIDDEN // NUM_HEADS
        THRESH = 0.001
        B, S, Hd = x.shape
        H, D = (NUM_HEADS, HEAD_DIM)
        q = (x @ Wq.T + bq).reshape(B, S, H, D)
        k = (x @ Wk.T + bk).reshape(B, S, H, D)
        v = (x @ Wv.T + bv).reshape(B, S, H, D)
        inv_sqrt_d = np.float32(1.0 / np.sqrt(D))
        scores = jnp.einsum('bshd,bsgd->bshg', q, k) * inv_sqrt_d
        scores = jnp.where(scores > THRESH, scores, -jnp.inf)
        attn = jax.nn.softmax(scores, axis=-1)
        out = jnp.einsum('bshg,bsgd->bshd', attn, v).reshape(B, S, Hd)
        return out @ Wo.T + bo

    def _L0_ffn_ref(x, weight, bias, lora_A, lora_B, lora_start_indices):
        import jax, jax.numpy as jnp
        import numpy as np
        LORA_RANK = 16
        LORA_ALPHA = 16
        LORA_SCALE = LORA_ALPHA / LORA_RANK
        y = jnp.einsum('bsd,od->bso', x, weight) + bias
        B = x.shape[0]
        seg = jnp.searchsorted(lora_start_indices, jnp.arange(B), side='right') - 1
        adapter_idx = jnp.clip(seg - 1, 0, lora_A.shape[0] - 1)
        A = lora_A[adapter_idx]
        Bw = lora_B[adapter_idx]
        lo = jnp.einsum('bsr,bor->bso', jnp.einsum('bsd,brd->bsr', x, A), Bw) * LORA_SCALE
        use_lora = (seg > 0)[:, None, None]
        return y + jnp.where(use_lora, lo, jnp.zeros((), dtype=y.dtype))

    def _L1_xattn_ref(text, features, Wq_w, Wq_b, Wk_w, Wk_b, fn_w, qn_w, kn_w):
        import jax, jax.numpy as jnp
        import numpy as np
        EPS = 1e-06

        def rmsnorm(x, w):
            xf = x.astype(jnp.float32)
            var = jnp.mean(xf * xf, axis=-1, keepdims=True)
            return (xf * jax.lax.rsqrt(var + EPS)).astype(x.dtype) * w
        features_n = rmsnorm(features, fn_w)
        Q = jnp.einsum('btd,fd->btf', text, Wq_w) + Wq_b
        K = jnp.einsum('bsd,fd->bsf', features_n, Wk_w) + Wk_b
        Q = rmsnorm(Q, qn_w)
        K = rmsnorm(K, kn_w)
        scale = 1.0 / jnp.sqrt(jnp.asarray(K.shape[-1], dtype=Q.dtype))
        scores = jnp.einsum('btf,bsf->bts', Q, K) * scale
        attn = jax.nn.softmax(scores, axis=-1)
        attended = jnp.einsum('bts,bsf->btf', attn, features_n)
        return attended

    def _L1_attn_ref(hidden_states, q_a_w, q_a_norm_w, q_b_w, kv_a_w, kv_a_norm_w, kv_b_w, o_w, idx_wq_w, idx_wk_w, idx_weights_w):
        import jax, jax.numpy as jnp
        import numpy as np
        B, S, HID = (1, 256, 512)
        H, NOPE, ROPE, VD = (32, 128, 64, 128)
        QKD = NOPE + ROPE
        Q_RANK, KV_RANK = (192, 64)
        IDX_H, IDX_D, TOPK = (16, 128, 128)
        EPS, THETA = (1e-05, 10000.0)

        def rmsnorm(x, w):
            return x * jax.lax.rsqrt(jnp.mean(x * x, axis=-1, keepdims=True) + EPS) * w

        def rope_interleaved(x, pos):
            d = x.shape[-1]
            inv_freq = 1.0 / THETA ** (jnp.arange(0, d, 2, dtype=jnp.float32) / d)
            ang = pos[:, None] * inv_freq[None, :]
            cos, sin = (jnp.cos(ang), jnp.sin(ang))
            x2 = x.reshape(*x.shape[:-1], d // 2, 2)
            x0, x1 = (x2[..., 0], x2[..., 1])
            return jnp.stack([x0 * cos - x1 * sin, x1 * cos + x0 * sin], axis=-1).reshape(x.shape)
        b, s, _ = hidden_states.shape
        pos = jnp.arange(s, dtype=jnp.float32)
        q_lat = rmsnorm(hidden_states @ q_a_w, q_a_norm_w)
        q = (q_lat @ q_b_w).reshape(b, s, H, QKD).transpose(0, 2, 1, 3)
        q_nope, q_pe = (q[..., :NOPE], q[..., NOPE:])
        ckv = hidden_states @ kv_a_w
        kv_lat, k_pe = (ckv[..., :KV_RANK], ckv[..., KV_RANK:])
        kv = (rmsnorm(kv_lat, kv_a_norm_w) @ kv_b_w).reshape(b, s, H, NOPE + VD).transpose(0, 2, 1, 3)
        k_nope, v = (kv[..., :NOPE], kv[..., NOPE:])
        q_pe = rope_interleaved(q_pe, pos)
        k_pe = rope_interleaved(k_pe[:, None, :, :], pos)
        scores = (jnp.einsum('bhqd,bhkd->bhqk', q_nope, k_nope) + jnp.einsum('bhqd,bhkd->bhqk', q_pe, k_pe)) * QKD ** (-0.5)
        iq = (hidden_states @ idx_wq_w).reshape(b, s, IDX_H, IDX_D)
        ik = hidden_states @ idx_wk_w
        iw = hidden_states @ idx_weights_w * IDX_H ** (-0.5)
        idx_scores = jnp.einsum('bqn,bnqk->bqk', iw, jax.nn.relu(jnp.einsum('bqnd,bkd->bnqk', iq, ik))) * IDX_D ** (-0.5)
        causal = pos[:, None] >= pos[None, :]
        idx_scores = jnp.where(causal, idx_scores, -jnp.inf)
        _, topk_idx = jax.lax.top_k(idx_scores, TOPK)
        bi = jnp.arange(b)[:, None, None]
        qi = jnp.arange(s)[None, :, None]
        topk_mask = jnp.zeros((b, s, s), bool).at[bi, qi, topk_idx].set(True)
        mask = topk_mask & causal
        scores = jnp.where(mask[:, None], scores, -jnp.inf)
        attn = jax.nn.softmax(scores, axis=-1)
        out = jnp.einsum('bhqk,bhkd->bqhd', attn, v).reshape(b, s, H * VD)
        return out @ o_w

    def _L1_ffn_ref(x, gate_w, base_w, base_b, lora_A, lora_B):
        import jax, jax.numpy as jnp
        import numpy as np
        B, S, D_IN, D_OUT = (2, 256, 512, 512)
        E, K, R = (8, 2, 16)
        SCALING = 32.0 / 16.0
        gate_logits = jnp.einsum('bsd,ed->bse', x, gate_w)
        weights, selected = jax.lax.top_k(gate_logits, K)
        weights = jax.nn.softmax(weights.astype(jnp.float32), axis=2).astype(x.dtype)
        result = jnp.einsum('bsd,od->bso', x, base_w) + base_b
        w_full = jnp.sum(jax.nn.one_hot(selected, E, dtype=x.dtype) * weights[..., None], axis=2)
        low = jnp.einsum('bsd,erd->ebsr', x, lora_A)
        lora_out = jnp.einsum('ebsr,eor,bse->bso', low, lora_B, w_full)
        result = result + SCALING * lora_out
        return result

    def _L2_xattn_ref(q, k, v, w_q, w_k, w_v, w_out, mask):
        import jax, jax.numpy as jnp
        import numpy as np
        N_HEAD = 32
        D_MODEL = 512
        N_KV_GROUPS = 8
        D_HEAD = D_MODEL // N_HEAD
        H_PER_G = N_HEAD // N_KV_GROUPS
        KV_DIM = N_KV_GROUPS * D_HEAD
        B, S = (2, 256)
        b, n, _ = q.shape
        s = k.shape[1]
        query = q @ w_q.T
        key = k @ w_k.T
        value = v @ w_v.T
        query = query.reshape(b, n, N_HEAD, D_HEAD).transpose(0, 2, 1, 3)
        query = query.reshape(b, N_KV_GROUPS, H_PER_G, n, D_HEAD)
        key = key.reshape(b, s, N_KV_GROUPS, D_HEAD).transpose(0, 2, 1, 3)
        value = value.reshape(b, s, N_KV_GROUPS, D_HEAD).transpose(0, 2, 1, 3)
        scores = jnp.einsum('bghnd,bgsd->bghns', query, key) / D_HEAD ** 0.5
        scores = jnp.where(mask, scores, jnp.finfo(scores.dtype).min)
        attention = jax.nn.softmax(scores, axis=-1)
        out = jnp.einsum('bghns,bgsd->bghnd', attention, value)
        out = out.transpose(0, 3, 1, 2, 4).reshape(b, n, D_MODEL)
        return out @ w_out.T

    def _L2_attn_ref(hidden_states, w_qa, g_qa, w_qb, w_kva, g_kva, w_kvb, w_o):
        import jax, jax.numpy as jnp
        import numpy as np
        H = 512
        NH = 32
        QR = 192
        KVR = 64
        RD = 64
        ND = 128
        VD = 128
        QK = RD + ND
        EPS = 1e-06
        THETA = 10000.0
        B, S = (2, 128)

        def rmsnorm(x, w):
            norm = jnp.sqrt(jnp.sum(x * x, axis=-1, keepdims=True)) * x.shape[-1] ** (-0.5)
            return x / (norm + EPS) * w

        def rope_cos_sin(seq_len):
            inv_freq = 1.0 / THETA ** (jnp.arange(0, RD, 2, dtype=jnp.float32) / RD)
            t = jnp.arange(seq_len, dtype=jnp.float32)
            freqs = jnp.outer(t, inv_freq)
            emb = jnp.concatenate([freqs, freqs], -1)
            return (jnp.cos(emb), jnpp_cos_sin_dummy() if False else jnp.sin(emb))

        def rotate_half(x):
            x1, x2 = jnp.split(x, 2, axis=-1)
            return jnp.concatenate([-x2, x1], axis=-1)
        b, s, _ = hidden_states.shape
        q_c = rmsnorm(hidden_states @ w_qa, g_qa)
        q = (q_c @ w_qb).reshape(b, s, NH, QK).transpose(0, 2, 1, 3)
        q_nope, q_rope = (q[..., :ND], q[..., ND:])
        kv = hidden_states @ w_kva
        k_c, k_rope = (kv[..., :KVR], kv[..., KVR:])
        k_c = rmsnorm(k_c, g_kva)
        kst = (k_c @ w_kvb).reshape(b, s, NH, ND + VD).transpose(0, 2, 1, 3)
        k_nope, v = (kst[..., :ND], kst[..., ND:])
        inv_freq = 1.0 / THETA ** (jnp.arange(0, RD, 2, dtype=jnp.float32) / RD)
        freqs = jnp.outer(jnp.arange(s, dtype=jnp.float32), inv_freq)
        emb = jnp.concatenate([freqs, freqs], -1)
        cos = jnp.cos(emb)[None, None]
        sin = jnp.sin(emb)[None, None]
        k_rope = k_rope[:, None]
        q_rope = q_rope * cos + rotate_half(q_rope) * sin
        k_rope = k_rope * cos + rotate_half(k_rope) * sin
        k_rope = jnp.broadcast_to(k_rope, (b, NH, s, RD))
        query = jnp.concatenate([q_nope, q_rope], -1)
        key_s = jnp.concatenate([k_nope, k_rope], -1)
        scaling = QK ** (-0.5)
        scores = jnp.einsum('bhqd,bhkd->bhqk', query, key_s) * scaling
        attn = jax.nn.softmax(scores, axis=-1)
        out = jnp.einsum('bhqk,bhkd->bhqd', attn, v)
        out = out.transpose(0, 2, 1, 3).reshape(b, s, NH * VD)
        return out @ w_o

    def _L2_ffn_ref(x, W_org, lora_down, lora_up, lora_keys, Wq):
        import jax, jax.numpy as jnp
        import numpy as np
        import math
        B, S, IN, OUT = (4, 256, 512, 512)
        E, R, K = (8, 64, 128)
        SCALE = 64.0 / 64.0
        MULTIPLIER = 1.0
        base = jnp.einsum('bsi,oi->bso', x, W_org)
        q = jnp.einsum('bi,ki->bk', x.mean(axis=1), Wq)
        scores = jnp.einsum('bk,ek->be', q, lora_keys) / math.sqrt(K)
        coeffs = jax.nn.softmax(scores, axis=-1)
        h = jnp.einsum('bsi,eir->bser', x, lora_down)
        delta = jnp.einsum('be,bser,ero->bso', coeffs, h, lora_up)
        return base + delta * (SCALE * MULTIPLIER)

    def _L3_xattn_ref(hidden_states, cross_attention_states, attention_mask, q_proj_w, k_proj_w, v_proj_w, o_proj_w, q_norm_w, k_norm_w):
        import jax, jax.numpy as jnp
        import numpy as np
        NUM_HEADS = 32
        NUM_KV_HEADS = 8
        HEAD_DIM = 128
        HIDDEN = 512
        EPS = 1e-05

        def rmsnorm(x, w, eps=EPS):
            xf = x.astype(jnp.float32)
            var = jnp.mean(xf * xf, axis=-1, keepdims=True)
            return w * (xf * jax.lax.rsqrt(var + eps)).astype(x.dtype)
        B, Q, _ = hidden_states.shape
        KV = cross_attention_states.shape[1]
        n_rep = NUM_HEADS // NUM_KV_HEADS
        q = (hidden_states @ q_proj_w.T).reshape(B, Q, NUM_HEADS, HEAD_DIM).transpose(0, 2, 1, 3)
        k = (cross_attention_states @ k_proj_w.T).reshape(B, KV, NUM_KV_HEADS, HEAD_DIM).transpose(0, 2, 1, 3)
        v = (cross_attention_states @ v_proj_w.T).reshape(B, KV, NUM_KV_HEADS, HEAD_DIM).transpose(0, 2, 1, 3)
        q = rmsnorm(q, q_norm_w)
        k = jnp.repeat(k, n_rep, axis=1)
        v = jnp.repeat(v, n_rep, axis=1)
        k = rmsnorm(k, k_norm_w)
        scale = 1.0 / np.sqrt(HEAD_DIM)
        scores = jnp.einsum('bhqd,bhkd->bhqk', q, k) * scale + attention_mask
        attn = jax.nn.softmax(scores.astype(jnp.float32), axis=-1).astype(q.dtype)
        out = jnp.einsum('bhqk,bhkd->bhqd', attn, v)
        out = out.transpose(0, 2, 1, 3).reshape(B, Q, NUM_HEADS * HEAD_DIM)
        return out @ o_proj_w.T

    def _L3_attn_ref(x, Wqkv, bqkv, Wo, bo):
        import jax, jax.numpy as jnp
        import numpy as np
        H = 512
        D = H // 4
        B, S, C = x.shape
        d = C // 4
        qkv = jnp.einsum('bsc,cf->bsf', x, Wqkv) + bqkv
        qkv = qkv.reshape(B, S, 3, d)
        q, k, v = (qkv[:, :, 0], qkv[:, :, 1], qkv[:, :, 2])
        scale = 1.0 / jnp.sqrt(jnp.float32(d)).astype(x.dtype)
        attn = jnp.einsum('bqd,bkd->bqk', q, k) * scale
        attn = jax.nn.softmax(attn, axis=-1)
        out = jnp.einsum('bqk,bkd->bqd', attn, v)
        return jnp.einsum('bqd,dc->bqc', out, Wo) + bo

    def _L3_ffn_ref(x, codebooks, bias, ln_weight, codes, centroids):
        import jax, jax.numpy as jnp
        import numpy as np
        IN_F = 512
        OUT_F = 512
        C = 32
        NCL = 32
        SUB = IN_F // C
        CLS = OUT_F // NCL
        SIGMA = 10.0
        THRESH = 0.5

        def _expand(codes, codebooks):
            w = codebooks[jnp.arange(codes.shape[0])[:, None], codes]
            return jnp.transpose(w, (1, 0, 2)).reshape(codes.shape[1], -1)
        shape = x.shape
        x2 = x.reshape(-1, shape[-1])
        cw = _expand(centroids, codebooks)
        dots = x2 @ cw.T
        mu = jnp.mean(dots, axis=-1, keepdims=True)
        var = jnp.var(dots, axis=-1, keepdims=True)
        dots = (dots - mu) * jax.lax.rsqrt(var + 1e-05) * ln_weight
        soft = jax.nn.softmax(dots, axis=-1)
        m = soft > THRESH
        qmask = jnp.any(m, axis=-1)
        cmask = jnp.any(m, axis=0)
        kmask = jnp.repeat(cmask, CLS)
        W = _expand(codes, codebooks)
        y = x2 @ W.T + bias
        y = y * (qmask[:, None] & kmask[None, :]).astype(y.dtype)
        return y.reshape(*shape[:-1], OUT_F)
    x = x + _L0_xattn_ref(_layernorm(x, axis=-1), ctx_4096, ctx_4096, mask_BxSxS2_ff0, L0_xattn_wq, L0_xattn_wk, L0_xattn_wv, L0_xattn_wo, 0)
    x = x + _L0_attn_ref(_layernorm(x, axis=-1), L0_attn_Wq, L0_attn_bq, L0_attn_Wk, L0_attn_bk, L0_attn_Wv, L0_attn_bv, L0_attn_Wo, L0_attn_bo)
    x = x + _L0_ffn_ref(_layernorm(x, axis=-1), L0_ffn_weight, L0_ffn_bias, L0_ffn_lora_A, L0_ffn_lora_B, L0_ffn_lora_start_indices)
    x = x + _L1_xattn_ref(_layernorm(x, axis=-1), ctx_4096, L1_xattn_Wq_w, L1_xattn_Wq_b, L1_xattn_Wk_w, L1_xattn_Wk_b, L1_xattn_fn_w, L1_xattn_qn_w, L1_xattn_kn_w)
    x = x + _L1_attn_ref(_layernorm(x, axis=-1), L1_attn_q_a_w, L1_attn_q_a_norm_w, L1_attn_q_b_w, L1_attn_kv_a_w, L1_attn_kv_a_norm_w, L1_attn_kv_b_w, L1_attn_o_w, L1_attn_idx_wq_w, L1_attn_idx_wk_w, L1_attn_idx_weights_w)
    x = x + _L1_ffn_ref(_layernorm(x, axis=-1), L1_ffn_gate_w, L1_ffn_base_w, L1_ffn_base_b, L1_ffn_lora_A, L1_ffn_lora_B)
    x = x + _L2_xattn_ref(_layernorm(x, axis=-1), ctx_4096, ctx_4096, L2_xattn_w_q, L2_xattn_w_k, L2_xattn_w_v, L2_xattn_w_out, mask_SxS2_bk0)
    x = x + _L2_attn_ref(_layernorm(x, axis=-1), L2_attn_w_qa, L2_attn_g_qa, L2_attn_w_qb, L2_attn_w_kva, L2_attn_g_kva, L2_attn_w_kvb, L2_attn_w_o)
    x = x + _L2_ffn_ref(_layernorm(x, axis=-1), L2_ffn_W_org, L2_ffn_lora_down, L2_ffn_lora_up, L2_ffn_lora_keys, L2_ffn_Wq)
    x = x + _L3_xattn_ref(_layernorm(x, axis=-1), ctx_4096, mask_1x1xSxS2_ff0, L3_xattn_q_proj_w, L3_xattn_k_proj_w, L3_xattn_v_proj_w, L3_xattn_o_proj_w, L3_xattn_q_norm_w, L3_xattn_k_norm_w)
    x = x + _L3_attn_ref(_layernorm(x, axis=-1), L3_attn_Wqkv, L3_attn_bqkv, L3_attn_Wo, L3_attn_bo)
    x = x + _L3_ffn_ref(_layernorm(x, axis=-1), L3_ffn_codebooks, L3_ffn_bias, L3_ffn_ln_weight, L3_ffn_codes, L3_ffn_centroids)
    return x

_drawn_inputs = setup_inputs


def setup_inputs(seed=0):
    import zlib

    import numpy as np

    out = dict(_drawn_inputs(seed))
    spreads = {'L1_xattn_fn_w': (1.0, 0.2),
     'L1_xattn_qn_w': (1.0, 0.6),
     'L1_xattn_kn_w': (1.0, 0.6),
     'L1_attn_q_a_norm_w': (1.0, 0.6),
     'L1_attn_kv_a_norm_w': (1.0, 0.6),
     'L2_attn_g_qa': (1.0, 0.6),
     'L2_attn_g_kva': (1.0, 0.6),
     'L3_xattn_q_norm_w': (1.0, 0.2),
     'L3_xattn_k_norm_w': (1.0, 0.2),
     'L3_ffn_ln_weight': (10.0, 0.2)}
    factors = {'L0_xattn_wq': 4.721,
     'L0_xattn_wk': 3.791,
     'L0_attn_bq': 16.831,
     'L0_attn_bv': 25.635,
     'L0_attn_bo': 3.178,
     'L1_xattn_Wq_b': 8.0,
     'L1_xattn_Wk_b': 39.525,
     'L1_attn_q_a_w': 4.557,
     'L1_attn_q_b_w': 8.0,
     'L2_xattn_w_q': 8.0,
     'L2_xattn_w_k': 14.734,
     'L2_attn_w_qa': 22.289,
     'L2_attn_w_qb': 15.486,
     'L2_ffn_lora_up': 2.868,
     'L2_ffn_lora_keys': 6.242,
     'L2_ffn_Wq': 5.81,
     'L3_attn_bqkv': 4.264,
     'L3_ffn_bias': 8.0,
     'L0_attn_bk': 5.489,
     'L1_ffn_base_b': 2.901,
     'L2_xattn_w_out': 3.263,
     'L3_attn_bo': 5.624}
    for name, (base, spread) in spreads.items():
        noise = np.random.default_rng([zlib.crc32(name.encode()), seed]).standard_normal(out[name].shape)
        drawn = base * np.exp(spread * noise) if base else spread * noise
        out[name] = jnp.asarray(drawn.astype(out[name].dtype))
    for name, factor in factors.items():
        out[name] = (out[name] * factor).astype(out[name].dtype)
    return out
```

```python
from contextlib import ExitStack

import numpy as np

import concourse.bass as bass
from concourse import mybir
from concourse.alu_op_type import AluOpType as ALU

ACT = mybir.ActivationFunctionType
AX = mybir.AxisListType
F32 = mybir.dt.float32
I32 = mybir.dt.int32
U8 = mybir.dt.uint8

P = 128
D = 512
CT = D // P
SK = 2048
KT = SK // P
NC = SK // 512
HD = 128
NH = 32
NG = 8
HG = NH // NG
LOWEST = float(np.finfo(np.float32).min)


class Steps:

    def __init__(self, eng, sem, base=0):
        self.eng, self.sem, self.base, self.n = eng, sem, base, 0

    def then(self, ins):
        self.n += 1
        ins.then_inc(self.sem, 1)
        self.eng.wait_ge(self.sem, self.base + self.n)


class Core:

    def __init__(self, nc, ctx):
        self.nc = nc
        sb = lambda name, shape, dt=F32: ctx.enter_context(nc.sbuf_tensor(name, shape, dt))
        self.x = sb("x", [P, D])
        self.xn_t = sb("xn_t", [P, CT, P])
        self.ctx_t = sb("ctx_t", [P, CT, SK])
        self.ident = sb("ident", [P, P])
        self.ones = sb("ones", [P, P])
        self.eps5 = sb("eps5", [P, 1])
        self.zero = sb("zero", [P, 1])
        self.eps6 = sb("eps6", [P, 1])
        self.bank = [ctx.enter_context(nc.psum_tensor(f"bank{i}", [P, 512], F32)) for i in range(8)]


class Stage:

    def __init__(self, core, name):
        self.core, self.name = core, name
        self.ctx = ExitStack()
        self.sems = []

    def __enter__(self):
        return self

    def sb(self, name, shape, dt=F32):
        return self.ctx.enter_context(self.core.nc.sbuf_tensor(f"{self.name}_{name}", shape, dt))

    def sem(self, name):
        s = self.ctx.enter_context(self.core.nc.semaphore(f"{self.name}_{name}"))
        self.sems.append(s)
        return s

    def __exit__(self, *exc):
        if exc[0] is None:
            nc = self.core.nc
            with nc.Block() as block:
                @block.gpsimd
                def _(pool):
                    for s in self.sems:
                        pool.sem_clear(s)
        return self.ctx.__exit__(*exc)


def layer_norm(core, name):
    nc = core.nc
    with Stage(core, name) as st:
        xn = st.sb("xn", [P, D])
        stats = st.sb("stats", [P, 6])
        mean_var = st.sb("mean_var", [P, 2])
        veps = st.sb("veps", [P, 1])
        std = st.sb("std", [P, 1])
        rstd = st.sb("rstd", [P, 1])
        own = st.sem("own")
        var_ready = st.sem("var_ready")
        std_ready = st.sem("std_ready")
        xn_ready = st.sem("xn_ready")
        turned = st.sem("turned")
        with nc.Block() as block:
            @block.vector
            def _(dve):
                steps = Steps(dve, own)
                steps.then(dve.bn_stats(stats[:], core.x[:]))
                steps.then(dve.bn_aggr(mean_var[:], stats[:]))
                dve.tensor_scalar(veps[:], mean_var[:, 1:2], 1e-5, None, ALU.add).then_inc(var_ready, 1)
                dve.wait_ge(std_ready, 1)
                steps.then(dve.reciprocal(rstd[:], std[:]))
                dve.tensor_scalar(xn[:], core.x[:], mean_var[:, 0:1], rstd[:], ALU.subtract,
                                  ALU.mult).then_inc(xn_ready, 1)
                dve.wait_ge(turned, CT)
                dve.tensor_copy(core.xn_t[:], core.bank[0][:].rearrange("p (c q) -> p c q", c=CT))

            @block.scalar
            def _(act):
                act.wait_ge(var_ready, 1)
                act.activation(std[:], veps[:], ACT.Sqrt).then_inc(std_ready, 1)

            @block.tensor
            def _(pe):
                pe.wait_ge(xn_ready, 1)
                for c in range(CT):
                    pe.transpose(core.bank[0][:, c * P:(c + 1) * P], xn[:, c * P:(c + 1) * P],
                                 core.ident[:]).then_inc(turned, 1)


def wide_cross_attention(core, name, wkqv, wo, mask, rotary=None, norm_cols=None):
    nc = core.nc
    SCALE = float(1.0 / np.sqrt(np.float32(HD)))
    PROJ = NC + 1
    with Stage(core, name) as st:
        w_kqv = st.sb("w_kqv", [P, CT, 768])
        w_o = st.sb("w_o", [P, HG, D])
        mask_sb = st.sb("mask", [P, SK])
        k_t = st.sb("k_t", [P, SK])
        q_t = st.sb("q_t", [P, HG * P])
        v_sb = st.sb("v", [P, KT, HD])
        aux = st.sb("aux", [P, 2, 512])
        s_sb = st.sb("s", [P, HG, SK])
        p_t = st.sb("p_t", [P, 4, HG * P])
        part_max = st.sb("part_max", [P, HG, NC])
        neg_max = st.sb("neg_max", [P, HG])
        row_sum = st.sb("row_sum", [P, HG])
        r_sum = st.sb("r_sum", [P, HG])
        diag = st.sb("diag", [P, HG, P])
        o_raw = st.sb("o_raw", [P, HG * P])
        o_t = st.sb("o_t", [P, HG * P])
        if rotary is not None:
            cos_t = st.sb("cos_t", [P, SK])
            sin_t = st.sb("sin_t", [P, SK])
            cos_q = st.sb("cos_q", [P, P])
            sin_q = st.sb("sin_q", [P, P])
        else:
            cols = st.sb("cols", [P, 3])
            rms = st.sb("rms", [P, 512])

        consts_in = st.sem("consts_in")
        w_in = st.sem("w_in")
        wo_in = st.sem("wo_in")
        proj_ready = st.sem("proj_ready")
        proj_read_act = st.sem("proj_read_act")
        proj_read_dve = st.sem("proj_read_dve")
        aux_used = st.sem("aux_used")
        sumsq_ready = st.sem("sumsq_ready")
        rms_ready = st.sem("rms_ready")
        kq_ready = st.sem("kq_ready")
        v_proj = st.sem("v_proj")
        v_ready = st.sem("v_ready")
        s_ready = st.sem("s_ready")
        s_seen = st.sem("s_seen")
        s_read = st.sem("s_read")
        max_ready = st.sem("max_ready")
        exp_ready = st.sem("exp_ready")
        turned = st.sem("turned")
        pt_dve = st.sem("pt_dve")
        pt_act = st.sem("pt_act")
        pv_done = st.sem("pv_done")
        diag_ready = st.sem("diag_ready")
        rinv_ready = st.sem("rinv_ready")
        o_raw_ready = st.sem("o_raw_ready")
        o_ready = st.sem("o_ready")
        wo_done = st.sem("wo_done")
        x_added = st.sem("x_added")
        dve_own = st.sem("dve_own")
        diag_recip = st.sem("diag_recip")
        out_bank, rinv_bank, wo_bank = core.bank[7], core.bank[0], core.bank[1]
        proj_bank = lambda n: core.bank[n % 3]
        ring_bank = lambda n: core.bank[3 + n % 4]

        consts_all = 16 * (5 if rotary is not None else 2)

        with nc.Block() as block:
            @block.sync
            def _(sp):
                sp.dma_start(w_kqv[:], wkqv[0]).then_inc(w_in, 16)
                sp.dma_start(mask_sb[:], mask).then_inc(consts_in, 16)
                if rotary is not None:
                    for t, src in zip((cos_t, sin_t, cos_q, sin_q), rotary):
                        sp.dma_start(t[:], src).then_inc(consts_in, 16)
                else:
                    sp.dma_start(cols[:, 0:2], norm_cols).then_inc(consts_in, 16)
                sp.dma_start(w_o[:], wo[0]).then_inc(wo_in, 16)
                with sp.Fori(1, NG) as g:
                    sp.wait_ge(v_proj, g * 4)
                    sp.dma_start(w_kqv[:], wkqv[g]).then_inc(w_in, 16)
                    sp.wait_ge(wo_done, g)
                    sp.dma_start(w_o[:], wo[g]).then_inc(wo_in, 16)

            @block.tensor
            def _(pe):
                with pe.Fori(0, NG) as g:
                    pe.wait_ge(w_in, g * 16 + 16)

                    def sum_squares(n):
                        pe.wait_ge(proj_read_act, g * PROJ + n + 1)
                        if n > 0:
                            pe.wait_ge(rms_ready, g * PROJ + n)
                        pe.matmul(out_bank[:], core.ones[:], aux[:, n % 2, :], start=True,
                                  stop=True).then_inc(sumsq_ready, 1)

                    for n in range(PROJ):
                        if n < 3:
                            pe.wait_ge(x_added, g + 1)
                            pe.wait_ge(v_ready, g * 4 + 1)
                        else:
                            pe.wait_ge(proj_read_dve, g * PROJ + n - 2)
                        if n < NC:
                            for c in range(CT):
                                mm = pe.matmul(proj_bank(n)[:], w_kqv[:, c, 0:128],
                                               core.ctx_t[:, c, n * 512:(n + 1) * 512],
                                               start=(c == 0), stop=(c == CT - 1))
                        else:
                            for h in range(HG):
                                for c in range(CT):
                                    mm = pe.matmul(proj_bank(n)[:, h * P:(h + 1) * P],
                                                   w_kqv[:, c, 128 + h * HD:128 + (h + 1) * HD],
                                                   core.xn_t[:, c, :], start=(c == 0), stop=(c == CT - 1))
                        mm.then_inc(proj_ready, 1)
                        if rotary is None and n > 0:
                            sum_squares(n - 1)

                    def project_v(n):
                        if n < 3:
                            pe.wait_ge(proj_read_dve, g * PROJ + n + 3)
                        else:
                            pe.wait_ge(v_ready, g * 4 + 2)
                        for j in range(4):
                            kt = 4 * n + j
                            for c in range(CT):
                                mm = pe.matmul(proj_bank(PROJ + n)[:, j * P:(j + 1) * P],
                                               core.ctx_t[:, c, kt * P:(kt + 1) * P],
                                               w_kqv[:, c, 640:768], start=(c == 0), stop=(c == CT - 1))
                        mm.then_inc(v_proj, 1)

                    project_v(0)
                    if rotary is None:
                        sum_squares(PROJ - 1)
                    project_v(1)
                    pe.wait_ge(kq_ready, g * PROJ + PROJ)
                    for h in range(HG):
                        for c in range(NC):
                            n = h * NC + c
                            if n < 4:
                                pe.wait_ge(pt_dve, g * 8 + 1)
                                pe.wait_ge(pt_act, g * 8 + 1)
                            else:
                                pe.wait_ge(s_read, g * 16 + n - 3)
                            pe.matmul(ring_bank(n)[:], q_t[:, h * P:(h + 1) * P],
                                      k_t[:, c * 512:(c + 1) * 512], start=True,
                                      stop=True).then_inc(s_ready, 1)
                    project_v(2)
                    project_v(3)

                    def turn(kt):
                        if kt < 4:
                            pe.wait_ge(s_read, g * 16 + 16)
                            pe.wait_ge(exp_ready, g * 4 + 4)
                        else:
                            pe.wait_ge((pt_act if kt % 2 else pt_dve), g * 8 + (kt - 4) // 2 + 2)
                        for h in range(HG):
                            mm = pe.transpose(ring_bank(kt)[:, h * P:(h + 1) * P],
                                              s_sb[:, h, kt * P:(kt + 1) * P], core.ident[:])
                        mm.then_inc(turned, 1)

                    def weigh(kt):
                        pe.wait_ge((pt_act if kt % 2 else pt_dve), g * 8 + kt // 2 + 2)
                        if kt == 0:
                            pe.wait_ge(v_ready, g * 4 + 5)
                        pe.matmul(out_bank[:], v_sb[:, kt, :], p_t[:, kt % 4, :], start=(kt == 0),
                                  stop=(kt == KT - 1)).then_inc(pv_done, 1)

                    for kt in range(KT + 2):
                        if kt < KT:
                            turn(kt)
                        if kt >= 2:
                            weigh(kt - 2)
                    pe.wait_ge(diag_ready, g * 4 + 4)
                    pe.matmul(rinv_bank[:], core.ones[:], diag[:].rearrange("p h q -> p (h q)"),
                              start=True, stop=True).then_inc(rinv_ready, 1)
                    pe.wait_ge(wo_in, g * 16 + 16)
                    pe.wait_ge(o_ready, g + 1)
                    for h in range(HG):
                        mm = pe.matmul(wo_bank[:], o_t[:, h * P:(h + 1) * P], w_o[:, h, :],
                                       start=(h == 0), stop=(h == HG - 1))
                    mm.then_inc(wo_done, 1)

            @block.scalar
            def _(act):
                act.sem_inc(v_ready, 1)
                act.sem_inc(pt_act, 1)
                with act.Fori(0, NG) as g:
                    for n in range(PROJ):
                        act.wait_ge(proj_ready, g * PROJ + n + 1)
                        src = proj_bank(n)
                        if rotary is not None:
                            if n >= 2:
                                act.wait_ge(aux_used, g * PROJ + n)
                            else:
                                act.wait_ge(aux_used, g * PROJ + 1)
                            act.activation(aux[64:128, n % 2, :], src[0:64, :], ACT.Copy)
                            act.activation(aux[0:64, n % 2, :], src[64:128, :],
                                           ACT.Copy).then_inc(proj_read_act, 1)
                        else:
                            if n >= 2:
                                act.wait_ge(sumsq_ready, g * PROJ + n - 1)
                            act.activation(aux[:, n % 2, :], src[:], ACT.Square,
                                           scale=float(HD ** -0.5)).then_inc(proj_read_act, 1)
                            if n > 0:
                                act.wait_ge(sumsq_ready, g * PROJ + n)
                                act.wait_ge(kq_ready, g * PROJ + n - 1)
                                act.activation(rms[:], out_bank[:], ACT.Sqrt,
                                               bias=core.eps5[:]).then_inc(rms_ready, 1)
                    if rotary is None:
                        act.wait_ge(sumsq_ready, g * PROJ + PROJ)
                        act.wait_ge(kq_ready, g * PROJ + PROJ - 1)
                        act.activation(rms[:], out_bank[:], ACT.Sqrt, bias=core.eps5[:]).then_inc(rms_ready, 1)

                    def keep_v(n):
                        act.wait_ge(v_proj, g * 4 + n + 1)
                        act.activation(v_sb[:, 4 * n:4 * n + 4, :],
                                       proj_bank(PROJ + n)[:].rearrange("p (k d) -> p k d", k=4),
                                       ACT.Copy).then_inc(v_ready, 1)

                    keep_v(0)
                    keep_v(1)
                    for h in range(HG):
                        act.wait_ge(max_ready, g * 4 + h + 1)
                        act.activation(s_sb[:, h, :], s_sb[:, h, :], ACT.Exp, bias=neg_max[:, h:h + 1],
                                       scale=1.0, accum_out=row_sum[:, h:h + 1]).then_inc(exp_ready, 1)
                    keep_v(2)
                    keep_v(3)
                    for kt in range(1, KT, 2):
                        act.wait_ge(turned, g * 16 + kt + 1)
                        if kt >= 4:
                            act.wait_ge(pv_done, g * 16 + kt - 3)
                        act.activation(p_t[:, kt % 4, :], ring_bank(kt)[:], ACT.Copy).then_inc(pt_act, 1)
                    act.wait_ge(pv_done, g * 16 + 16)
                    act.activation(o_raw[:], out_bank[:], ACT.Copy).then_inc(o_raw_ready, 1)

            @block.vector
            def _(dve):
                for one_ahead in (x_added, pt_dve, aux_used):
                    dve.sem_inc(one_ahead, 1)
                dve.wait_ge(consts_in, consts_all)
                own_a_round = 2 * PROJ if rotary is not None else PROJ
                if rotary is None:
                    dve.tensor_scalar(cols[:, 2:3], cols[:, 0:1], SCALE, None, ALU.mult)
                with dve.Fori(0, NG) as g:
                    steps = Steps(dve, dve_own, base=g * own_a_round)
                    for n in range(PROJ):
                        dst = k_t[:, n * 512:(n + 1) * 512] if n < NC else q_t[:]
                        dve.wait_ge(proj_read_act, g * PROJ + n + 1)
                        if rotary is not None:
                            if n < NC:
                                view = lambda t: t
                                cos, sin = (t[:, n * 512:(n + 1) * 512] for t in (cos_t, sin_t))
                            else:
                                view = lambda t: t.rearrange("p (h q) -> p h q", h=HG)
                                cos, sin = (t[:].unsqueeze(1).to_broadcast([P, HG, P]) for t in (cos_q, sin_q))
                            dve.tensor_tensor(view(dst), view(proj_bank(n)[:]), cos,
                                              ALU.mult).then_inc(proj_read_dve, 1)
                            steps.then(dve.tensor_tensor(view(aux[:, n % 2, :]), view(aux[:, n % 2, :]),
                                                         sin, ALU.mult))
                            dve.wait_ge(proj_read_dve, g * PROJ + n + 1)
                            steps.then(dve.tensor_tensor(dst, dst, aux[:, n % 2, :], ALU.add))
                            dve.sem_inc(aux_used, 1)
                            dve.sem_inc(kq_ready, 1)
                        else:
                            weight = cols[:, 1:2] if n < NC else cols[:, 2:3]
                            dve.tensor_scalar(dst, proj_bank(n)[:], weight, None,
                                              ALU.mult).then_inc(proj_read_dve, 1)
                            dve.wait_ge(rms_ready, g * PROJ + n + 1)
                            steps.then(dve.reciprocal(rms[:], rms[:]))
                            dve.wait_ge(proj_read_dve, g * PROJ + n + 1)
                            dve.tensor_tensor(dst, dst, rms[:], ALU.mult).then_inc(kq_ready, 1)
                    assert steps.n == own_a_round
                    for h in range(HG):
                        for c in range(NC):
                            n = h * NC + c
                            dve.wait_ge(s_ready, g * 16 + n + 1)
                            dve.sem_inc(s_seen, 1)
                            dve.tensor_tensor_reduce(
                                s_sb[:, h, c * 512:(c + 1) * 512], ring_bank(n)[:],
                                mask_sb[:, c * 512:(c + 1) * 512], 1.0, LOWEST, ALU.add, ALU.max,
                                part_max[:, h, c:c + 1]).then_inc(s_read, 1)
                        dve.wait_ge(s_read, g * 16 + h * NC + NC)
                        dve.tensor_reduce(neg_max[:, h:h + 1], part_max[:, h, :], AX.X, ALU.max,
                                          negate=True).then_inc(max_ready, 1)
                    for kt in range(0, KT, 2):
                        dve.wait_ge(turned, g * 16 + kt + 1)
                        if kt >= 4:
                            dve.wait_ge(pv_done, g * 16 + kt - 3)
                        dve.tensor_copy(p_t[:, kt % 4, :], ring_bank(kt)[:]).then_inc(pt_dve, 1)
                        if kt == 4:
                            dve.wait_ge(exp_ready, g * 4 + 4)
                            dve.reciprocal(r_sum[:], row_sum[:]).then_inc(diag_recip, 1)
                            dve.wait_ge(diag_recip, g + 1)
                            for h in range(HG):
                                dve.tensor_scalar(diag[:, h, :], core.ident[:], r_sum[:, h:h + 1], None,
                                                  ALU.mult).then_inc(diag_ready, 1)
                    dve.wait_ge(rinv_ready, g + 1)
                    dve.wait_ge(o_raw_ready, g + 1)
                    dve.tensor_tensor(o_t[:], o_raw[:], rinv_bank[:], ALU.mult).then_inc(o_ready, 1)
                    dve.wait_ge(wo_done, g + 1)
                    dve.tensor_tensor(core.x[:], core.x[:], wo_bank[:], ALU.add).then_inc(x_added, 1)


def per_token_head_attention(core, name, w_qkvo, rows):
    nc = core.nc
    H, E = 32, 16
    THRESH = 0.001
    PARTS = 4
    HP = H // PARTS
    with Stage(core, name) as st:
        w = st.sb("w", [P, CT, 4 * D])
        bias = st.sb("bias", [P, 4 * D])
        qkv = st.sb("qkv", [P, 3, D])
        prod = st.sb("prod", [P, 2, HP * H * E])
        s_sb = st.sb("s", [P, H, H])
        keep = st.sb("keep", [P, H, H])
        top = st.sb("top", [P, H])
        total = st.sb("total", [P, H])
        r_total = st.sb("r_total", [P, H])
        o_sb = st.sb("o", [P, H, E])
        o_t = st.sb("o_t", [P, CT, P])
        w_in = st.sem("w_in")
        bias_in = st.sem("bias_in")
        qkv_ready = st.sem("qkv_ready")
        own = st.sem("own")
        qkv_biased = st.sem("qkv_biased")
        prod_ready = st.sem("prod_ready")
        prod_used = st.sem("prod_used")
        shifted = st.sem("shifted")
        exp_ready = st.sem("exp_ready")
        o_ready = st.sem("o_ready")
        o_turned = st.sem("o_turned")
        o_t_ready = st.sem("o_t_ready")
        out_ready = st.sem("out_ready")
        with nc.Block() as block:
            @block.sync
            def _(sp):
                for j in range(4):
                    sp.dma_start(w[:, :, j * D:(j + 1) * D], w_qkvo[:, :, j * D:(j + 1) * D]).then_inc(w_in, 16)
                sp.dma_start(bias[:], rows.to_broadcast([P, 4 * D])).then_inc(bias_in, 16)

            @block.tensor
            def _(pe):
                pe.wait_ge(w_in, 64)
                for j in range(3):
                    for c in range(CT):
                        mm = pe.matmul(core.bank[j][:], core.xn_t[:, c, :], w[:, c, j * D:(j + 1) * D],
                                       start=(c == 0), stop=(c == CT - 1))
                    mm.then_inc(qkv_ready, 1)
                pe.wait_ge(o_ready, 1)
                o_flat = o_sb[:].rearrange("p h e -> p (h e)")
                for c in range(CT):
                    mm = pe.transpose(core.bank[3][:, c * P:(c + 1) * P], o_flat[:, c * P:(c + 1) * P],
                                      core.ident[:])
                mm.then_inc(o_turned, 1)
                pe.wait_ge(o_t_ready, 1)
                for c in range(CT):
                    mm = pe.matmul(core.bank[4][:], o_t[:, c, :], w[:, c, 3 * D:], start=(c == 0),
                                   stop=(c == CT - 1))
                mm.then_inc(out_ready, 1)

            @block.scalar
            def _(act):
                act.wait_ge(shifted, 1)
                act.activation(s_sb[:], s_sb[:], ACT.Exp, scale=float(E ** -0.5)).then_inc(exp_ready, 1)

            @block.vector
            def _(dve):
                steps = Steps(dve, own)
                dve.wait_ge(bias_in, 16)
                for j in range(3):
                    dve.wait_ge(qkv_ready, j + 1)
                    dve.tensor_tensor(qkv[:, j, :], core.bank[j][:], bias[:, j * D:(j + 1) * D],
                                      ALU.add).then_inc(qkv_biased, 1)
                dve.wait_ge(qkv_biased, 3)
                q = qkv[:, 0, :].rearrange("p (h e) -> p h e", h=H)
                k = qkv[:, 1, :].rearrange("p (g e) -> p g e", g=H)
                v = qkv[:, 2, :].rearrange("p (g e) -> p e g", g=H)
                prods = 0

                def multiply(slot, shape, left, right):
                    nonlocal prods
                    if prods >= 2:
                        dve.wait_ge(prod_used, prods - 1)
                    view = prod[:, slot, :].rearrange("p (a b c) -> p a b c", a=shape[0], b=shape[1])
                    dve.tensor_tensor(view, left, right, ALU.mult).then_inc(prod_ready, 1)
                    prods += 1
                    dve.wait_ge(prod_ready, prods)
                    return view

                for i in range(PARTS):
                    shape = [P, HP, H, E]
                    view = multiply(i % 2, shape[1:], k.unsqueeze(1).to_broadcast(shape),
                                    q[:, i * HP:(i + 1) * HP, :].unsqueeze(2).to_broadcast(shape))
                    dve.tensor_reduce(s_sb[:, i * HP:(i + 1) * HP, :], view, AX.X, ALU.add).then_inc(prod_used, 1)
                dve.wait_ge(prod_used, prods)
                dve.tensor_scalar(keep[:], s_sb[:], float(E ** -0.5), THRESH, ALU.mult, ALU.is_gt)
                steps.then(dve.tensor_reduce(top[:], s_sb[:], AX.X, ALU.max))
                dve.tensor_tensor(s_sb[:], s_sb[:], top[:].unsqueeze(2).to_broadcast([P, H, H]),
                                  ALU.subtract).then_inc(shifted, 1)
                dve.wait_ge(exp_ready, 1)
                steps.then(dve.tensor_tensor(s_sb[:], s_sb[:], keep[:], ALU.mult))
                steps.then(dve.tensor_reduce(total[:], s_sb[:], AX.X, ALU.add))
                steps.then(dve.reciprocal(r_total[:], total[:]))
                for i in range(PARTS):
                    shape = [P, HP, E, H]
                    view = multiply(i % 2, shape[1:], v.unsqueeze(1).to_broadcast(shape),
                                    s_sb[:, i * HP:(i + 1) * HP, :].unsqueeze(2).to_broadcast(shape))
                    dve.tensor_reduce(o_sb[:, i * HP:(i + 1) * HP, :], view, AX.X, ALU.add).then_inc(prod_used, 1)
                dve.wait_ge(prod_used, prods)
                dve.tensor_tensor(o_sb[:], o_sb[:], r_total[:].unsqueeze(2).to_broadcast([P, H, E]),
                                  ALU.mult).then_inc(o_ready, 1)
                steps.then(dve.tensor_tensor(core.x[:], core.x[:], bias[:, 3 * D:], ALU.add))
                dve.wait_ge(o_turned, 1)
                dve.tensor_copy(o_t[:], core.bank[3][:].rearrange("p (c q) -> p c q", c=CT)).then_inc(o_t_ready, 1)
                dve.wait_ge(out_ready, 1)
                dve.tensor_tensor(core.x[:], core.x[:], core.bank[4][:], ALU.add)


def adapter_ffn(core, name, w_in_dram, rows, up_dram, adapters, rank, gate=False, starts=None,
                clamp_iota=None):
    nc = core.nc
    R = adapters * rank
    WIDE = R + (adapters if gate else 0)
    with Stage(core, name) as st:
        w = st.sb("w", [P, CT, D + WIDE])
        bias = st.sb("bias", [P, D])
        up = st.sb("up", [R, D])
        low = st.sb("low", [P, WIDE])
        coef = st.sb("coef", [P, adapters])
        first = st.sb("first", [P, adapters])
        second = st.sb("second", [P, adapters])
        rest = st.sb("rest", [P, adapters])
        iota = st.sb("iota", [P, adapters])
        scal = st.sb("scal", [P, 8])
        low_c = st.sb("low_c", [P, R])
        low_t = st.sb("low_t", [R, P])
        start_rows = st.sb("starts", [P, 4], I32)
        reached = st.sb("reached", [P, 4])
        w_in = st.sem("w_in")
        rows_in = st.sem("rows_in")
        own = st.sem("own")
        low_ready = st.sem("low_ready")
        scaled = st.sem("scaled")
        turned = st.sem("turned")
        low_t_ready = st.sem("low_t_ready")
        out_ready = st.sem("out_ready")
        gap_ready = st.sem("gap_ready")
        gap_exp = st.sem("gap_exp")
        with nc.Block() as block:
            @block.sync
            def _(sp):
                sp.dma_start(w[:], w_in_dram).then_inc(w_in, 16)
                sp.dma_start(up[:], up_dram).then_inc(w_in, 16)
                sp.dma_start(bias[:], rows.to_broadcast([P, D])).then_inc(rows_in, 16)
                sp.dma_start(iota[:], clamp_iota.to_broadcast([P, adapters])).then_inc(rows_in, 16)
                if starts is not None:
                    sp.dma_start(start_rows[:], starts.to_broadcast([P, 4])).then_inc(rows_in, 16)

            @block.tensor
            def _(pe):
                pe.wait_ge(w_in, 32)
                for c in range(CT):
                    mm = pe.matmul(core.bank[1][:, 0:WIDE], core.xn_t[:, c, :], w[:, c, D:],
                                   start=(c == 0), stop=(c == CT - 1))
                mm.then_inc(low_ready, 1)
                for c in range(CT):
                    pe.matmul(core.bank[0][:], core.xn_t[:, c, :], w[:, c, 0:D], start=(c == 0), stop=False)
                pe.wait_ge(scaled, 1)
                pe.transpose(core.bank[2][0:R, 0:P], low_c[:], core.ident[:]).then_inc(turned, 1)
                pe.wait_ge(low_t_ready, 1)
                pe.matmul(core.bank[0][:], low_t[:], up[:], start=False, stop=True).then_inc(out_ready, 1)

            @block.scalar
            def _(act):
                if gate:
                    act.wait_ge(gap_ready, 1)
                    act.activation(scal[:, 3:4], scal[:, 2:3], ACT.Exp).then_inc(gap_exp, 1)

            @block.vector
            def _(dve):
                steps = Steps(dve, own)
                dve.wait_ge(rows_in, 16 * (3 if starts is not None else 2))
                steps.then(dve.tensor_tensor(core.x[:], core.x[:], bias[:], ALU.add))
                if not gate:
                    steps.then(dve.tensor_scalar(reached[:], start_rows[:], 0.0, None, ALU.is_le))
                    steps.then(dve.tensor_reduce(scal[:, 0:1], reached[:], AX.X, ALU.add))
                    steps.then(dve.tensor_scalar(scal[:, 1:2], scal[:, 0:1], 2.0, 0.0, ALU.subtract, ALU.max))
                    steps.then(dve.tensor_scalar(scal[:, 2:3], scal[:, 1:2], float(adapters - 1), None, ALU.min))
                    steps.then(dve.tensor_scalar(scal[:, 3:4], scal[:, 0:1], 1.5, None, ALU.is_gt))
                    steps.then(dve.tensor_scalar(coef[:], iota[:], scal[:, 2:3], scal[:, 3:4],
                                                 ALU.is_equal, ALU.mult))
                    dve.wait_ge(low_ready, 1)
                    source = core.bank[1][:, 0:R]
                else:
                    dve.wait_ge(low_ready, 1)
                    steps.then(dve.tensor_copy(low[:], core.bank[1][:, 0:WIDE]))
                    logits = low[:, R:]

                    def pick(dst, values, peak):
                        steps.then(dve.tensor_reduce(peak, values, AX.X, ALU.max))
                        steps.then(dve.tensor_scalar(dst, values, peak, float(adapters), ALU.not_equal, ALU.mult))
                        steps.then(dve.tensor_tensor(dst, dst, iota[:], ALU.add))
                        steps.then(dve.tensor_reduce(scal[:, 6:7], dst, AX.X, ALU.min))
                        steps.then(dve.tensor_scalar(dst, iota[:], scal[:, 6:7], None, ALU.is_equal))

                    pick(first[:], logits, scal[:, 0:1])
                    steps.then(dve.scalar_tensor_tensor(rest[:], first[:], LOWEST, logits, ALU.mult, ALU.add))
                    pick(second[:], rest[:], scal[:, 1:2])
                    dve.tensor_tensor(scal[:, 2:3], scal[:, 1:2], scal[:, 0:1], ALU.subtract).then_inc(gap_ready, 1)
                    dve.wait_ge(gap_exp, 1)
                    steps.then(dve.tensor_scalar(scal[:, 4:5], scal[:, 3:4], 1.0, 0.5, ALU.add, ALU.mult))
                    steps.then(dve.reciprocal(scal[:, 5:6], scal[:, 4:5]))
                    steps.then(dve.tensor_scalar(coef[:], second[:], scal[:, 3:4], None, ALU.mult))
                    steps.then(dve.tensor_tensor(coef[:], coef[:], first[:], ALU.add))
                    steps.then(dve.tensor_scalar(coef[:], coef[:], scal[:, 5:6], None, ALU.mult))
                    source = low[:, 0:R]
                dve.tensor_tensor(low_c[:].rearrange("p (a r) -> p a r", a=adapters),
                                  source.rearrange("p (a r) -> p a r", a=adapters),
                                  coef[:].unsqueeze(2).to_broadcast([P, adapters, rank]),
                                  ALU.mult).then_inc(scaled, 1)
                dve.wait_ge(turned, 1)
                dve.tensor_copy(low_t[:], core.bank[2][0:R, 0:P]).then_inc(low_t_ready, 1)
                dve.wait_ge(out_ready, 1)
                dve.tensor_tensor(core.x[:], core.x[:], core.bank[0][:], ALU.add)


def mixed_adapter_ffn(core, name, w_dram, keys_dram, up_dram):
    nc = core.nc
    A = 8
    with Stage(core, name) as st:
        w = st.sb("w", [P, CT, 2 * D + P])
        keys = st.sb("keys", [P, A])
        up = st.sb("up", [P, CT, D])
        mean = st.sb("mean", [P, CT])
        q_wide = st.sb("q_wide", [P, P])
        coef = st.sb("coef", [P, A])
        coef_col = st.sb("coef_col", [P, CT])
        scal = st.sb("scal", [P, 4])
        h_t = st.sb("h_t", [P, CT, P])
        w_in = st.sem("w_in")
        own = st.sem("own")
        mean_ready = st.sem("mean_ready")
        q_ready = st.sem("q_ready")
        q_wide_ready = st.sem("q_wide_ready")
        scores_ready = st.sem("scores_ready")
        top_ready = st.sem("top_ready")
        exp_ready = st.sem("exp_ready")
        h_ready = st.sem("h_ready")
        h_scaled = st.sem("h_scaled")
        out_ready = st.sem("out_ready")
        with nc.Block() as block:
            @block.sync
            def _(sp):
                sp.dma_start(w[:], w_dram).then_inc(w_in, 16)
                sp.dma_start(keys[:], keys_dram).then_inc(w_in, 16)
                sp.dma_start(up[:], up_dram).then_inc(w_in, 16)

            @block.tensor
            def _(pe):
                pe.wait_ge(w_in, 48)
                pe.wait_ge(mean_ready, 1)
                for c in range(CT):
                    mm = pe.matmul(core.bank[1][:, 0:1], w[:, c, 2 * D:], mean[:, c:c + 1], start=(c == 0),
                                   stop=(c == CT - 1))
                mm.then_inc(q_ready, 1)
                for t in range(CT):
                    for c in range(CT):
                        mm = pe.matmul(core.bank[3][:, t * P:(t + 1) * P], w[:, c, D + t * P:D + (t + 1) * P],
                                       core.xn_t[:, c, :], start=(c == 0), stop=(c == CT - 1))
                mm.then_inc(h_ready, 1)
                pe.wait_ge(q_wide_ready, 1)
                pe.matmul(core.bank[2][:, 0:A], q_wide[:], keys[:], start=True, stop=True).then_inc(scores_ready, 1)
                for c in range(CT):
                    pe.matmul(core.bank[0][:], core.xn_t[:, c, :], w[:, c, 0:D], start=(c == 0), stop=False)
                pe.wait_ge(h_scaled, CT)
                for t in range(CT):
                    mm = pe.matmul(core.bank[0][:], h_t[:, t, :], up[:, t, :], start=False, stop=(t == CT - 1))
                mm.then_inc(out_ready, 1)

            @block.scalar
            def _(act):
                act.wait_ge(top_ready, 1)
                act.activation(coef[:], core.bank[2][:, 0:A], ACT.Exp, bias=scal[:, 1:2],
                               scale=float(P ** -0.5), accum_out=scal[:, 2:3]).then_inc(exp_ready, 1)

            @block.vector
            def _(dve):
                steps = Steps(dve, own)
                steps.then(dve.tensor_reduce(mean[:], core.xn_t[:], AX.X, ALU.add))
                dve.tensor_scalar(mean[:], mean[:], 1.0 / P, None, ALU.mult).then_inc(mean_ready, 1)
                dve.wait_ge(q_ready, 1)
                steps.then(dve.tensor_copy(scal[:, 3:4], core.bank[1][:, 0:1]))
                dve.tensor_scalar(q_wide[:], core.ones[:], scal[:, 3:4], None, ALU.mult).then_inc(q_wide_ready, 1)
                dve.wait_ge(scores_ready, 1)
                steps.then(dve.tensor_reduce(scal[:, 0:1], core.bank[2][:, 0:A], AX.X, ALU.max, negate=True))
                dve.tensor_scalar(scal[:, 1:2], scal[:, 0:1], float(P ** -0.5), None, ALU.mult).then_inc(top_ready, 1)
                dve.wait_ge(exp_ready, 1)
                steps.then(dve.reciprocal(scal[:, 0:1], scal[:, 2:3]))
                steps.then(dve.tensor_scalar(coef[:], coef[:], scal[:, 0:1], None, ALU.mult))
                steps.then(dve.tensor_copy(coef_col[0:64, :], coef[0:64, 0:A:2]))
                steps.then(dve.tensor_copy(coef_col[64:128, :], coef[64:128, 1:A:2]))
                dve.wait_ge(h_ready, 1)
                for t in range(CT):
                    dve.tensor_scalar(h_t[:, t, :], core.bank[3][:, t * P:(t + 1) * P], coef_col[:, t:t + 1],
                                      None, ALU.mult).then_inc(h_scaled, 1)
                dve.wait_ge(out_ready, 1)
                dve.tensor_tensor(core.x[:], core.x[:], core.bank[0][:], ALU.add)


def single_head_attention(core, name, wqkv, wo, qk_cols, rows):
    nc = core.nc
    SCALE = float(HD ** -0.5)
    with Stage(core, name) as st:
        w = st.sb("w", [P, CT, 3 * HD])
        w_o = st.sb("w_o", [P, D])
        cols = st.sb("cols", [P, 2])
        bias = st.sb("bias", [P, HD + D])
        qk_t = st.sb("qk_t", [P, 2, P])
        v_sb = st.sb("v", [P, HD])
        p_sb = st.sb("p", [P, P])
        p_t = st.sb("p_t", [P, P])
        o_t = st.sb("o_t", [P, P])
        scal = st.sb("scal", [P, 4])
        w_in = st.sem("w_in")
        rows_in = st.sem("rows_in")
        own = st.sem("own")
        qk_ready = st.sem("qk_ready")
        v_ready = st.sem("v_ready")
        qk_biased = st.sem("qk_biased")
        v_biased = st.sem("v_biased")
        s_ready = st.sem("s_ready")
        top_ready = st.sem("top_ready")
        exp_ready = st.sem("exp_ready")
        p_ready = st.sem("p_ready")
        p_turned = st.sem("p_turned")
        p_t_ready = st.sem("p_t_ready")
        o_ready = st.sem("o_ready")
        o_t_ready = st.sem("o_t_ready")
        out_ready = st.sem("out_ready")
        with nc.Block() as block:
            @block.sync
            def _(sp):
                sp.dma_start(w[:], wqkv).then_inc(w_in, 16)
                sp.dma_start(w_o[:], wo).then_inc(w_in, 16)
                sp.dma_start(cols[:], qk_cols).then_inc(rows_in, 16)
                sp.dma_start(bias[:], rows.to_broadcast([P, HD + D])).then_inc(rows_in, 16)

            @block.tensor
            def _(pe):
                pe.wait_ge(w_in, 32)
                for j in range(2):
                    for c in range(CT):
                        mm = pe.matmul(core.bank[0][:, j * P:(j + 1) * P], w[:, c, j * HD:(j + 1) * HD],
                                       core.xn_t[:, c, :], start=(c == 0), stop=(c == CT - 1))
                mm.then_inc(qk_ready, 1)
                for c in range(CT):
                    mm = pe.matmul(core.bank[1][:, 0:HD], core.xn_t[:, c, :], w[:, c, 2 * HD:], start=(c == 0),
                                   stop=(c == CT - 1))
                mm.then_inc(v_ready, 1)
                pe.wait_ge(qk_biased, 2)
                pe.matmul(core.bank[2][:, 0:P], qk_t[:, 0, :], qk_t[:, 1, :], start=True,
                          stop=True).then_inc(s_ready, 1)
                pe.wait_ge(p_ready, 1)
                pe.transpose(core.bank[3][:, 0:P], p_sb[:], core.ident[:]).then_inc(p_turned, 1)
                pe.wait_ge(p_t_ready, 1)
                pe.wait_ge(v_biased, 1)
                pe.matmul(core.bank[4][:, 0:P], v_sb[:], p_t[:], start=True, stop=True).then_inc(o_ready, 1)
                pe.wait_ge(o_t_ready, 1)
                pe.matmul(core.bank[5][:], o_t[:], w_o[:], start=True, stop=True).then_inc(out_ready, 1)

            @block.scalar
            def _(act):
                act.wait_ge(top_ready, 1)
                act.activation(p_sb[:], core.bank[2][:, 0:P], ACT.Exp, bias=scal[:, 1:2], scale=SCALE,
                               accum_out=scal[:, 2:3]).then_inc(exp_ready, 1)

            @block.vector
            def _(dve):
                steps = Steps(dve, own)
                dve.wait_ge(rows_in, 32)
                steps.then(dve.tensor_tensor(core.x[:], core.x[:], bias[:, HD:], ALU.add))
                dve.wait_ge(qk_ready, 1)
                for j in range(2):
                    dve.tensor_scalar(qk_t[:, j, :], core.bank[0][:, j * P:(j + 1) * P], cols[:, j:j + 1], None,
                                      ALU.add).then_inc(qk_biased, 1)
                dve.wait_ge(v_ready, 1)
                dve.tensor_tensor(v_sb[:], core.bank[1][:, 0:HD], bias[:, 0:HD], ALU.add).then_inc(v_biased, 1)
                dve.wait_ge(s_ready, 1)
                steps.then(dve.tensor_reduce(scal[:, 0:1], core.bank[2][:, 0:P], AX.X, ALU.max, negate=True))
                dve.tensor_scalar(scal[:, 1:2], scal[:, 0:1], SCALE, None, ALU.mult).then_inc(top_ready, 1)
                dve.wait_ge(exp_ready, 1)
                steps.then(dve.reciprocal(scal[:, 3:4], scal[:, 2:3]))
                dve.tensor_scalar(p_sb[:], p_sb[:], scal[:, 3:4], None, ALU.mult).then_inc(p_ready, 1)
                dve.wait_ge(p_turned, 1)
                dve.tensor_copy(p_t[:], core.bank[3][:, 0:P]).then_inc(p_t_ready, 1)
                dve.wait_ge(o_ready, 1)
                dve.tensor_copy(o_t[:], core.bank[4][:, 0:P]).then_inc(o_t_ready, 1)
                dve.wait_ge(out_ready, 1)
                dve.tensor_tensor(core.x[:], core.x[:], core.bank[5][:], ALU.add)


def codebook_ffn(core, name, books, codes, entry, rows):
    nc = core.nc
    N = 32
    BG = 8
    with Stage(core, name) as st:
        books_sb = st.sb("books", [P, BG, P])
        codes_sb = st.sb("codes", [P, BG, D + N], I32)
        entry_sb = st.sb("entry", [P, 1])
        hot = st.sb("hot", [P, BG, D + N])
        w_t = st.sb("w_t", [P, CT, D + N])
        bias = st.sb("bias", [P, D + N])
        dots = st.sb("dots", [P, N])
        stats = st.sb("stats", [P, 6])
        mean_var = st.sb("mean_var", [P, 2])
        scal = st.sb("scal", [P, 8])
        taken = st.sb("taken", [P, N])
        k_mask = st.sb("k_mask", [P, N])
        y_sb = st.sb("y", [P, D])
        loaded = st.sem("loaded")
        own = st.sem("own")
        hot_ready = st.sem("hot_ready")
        w_ready = st.sem("w_ready")
        w_copied = st.sem("w_copied")
        c_copied = st.sem("c_copied")
        dots_ready = st.sem("dots_ready")
        y_ready = st.sem("y_ready")
        var_ready = st.sem("var_ready")
        std_ready = st.sem("std_ready")
        top_ready = st.sem("top_ready")
        exp_ready = st.sem("exp_ready")
        taken_ready = st.sem("taken_ready")
        count_ready = st.sem("count_ready")
        with nc.Block() as block:
            @block.sync
            def _(sp):
                sp.dma_start(books_sb[:], books).then_inc(loaded, 16)
                sp.dma_start(codes_sb[:], codes).then_inc(loaded, 16)
                sp.dma_start(entry_sb[:], entry).then_inc(loaded, 16)
                sp.dma_start(bias[:], rows.to_broadcast([P, D + N])).then_inc(loaded, 16)

            @block.tensor
            def _(pe):
                for t in range(CT):
                    pe.wait_ge(hot_ready, 2 * t + 2)
                    big, small = core.bank[t % 2], core.bank[2 + t % 2]
                    if t >= 2:
                        pe.wait_ge(w_copied, t - 1)
                        pe.wait_ge(c_copied, t - 1)
                    for j in range(2):
                        pe.matmul(big[:], books_sb[:, 2 * t + j, :], hot[:, 2 * t + j, 0:D], start=(j == 0),
                                  stop=(j == 1))
                    for j in range(2):
                        mm = pe.matmul(small[:, 0:N], books_sb[:, 2 * t + j, :], hot[:, 2 * t + j, D:],
                                       start=(j == 0), stop=(j == 1))
                    mm.then_inc(w_ready, 1)
                pe.wait_ge(w_copied, CT)
                pe.wait_ge(c_copied, CT)
                for c in range(CT):
                    mm = pe.matmul(core.bank[4][:, 0:N], core.xn_t[:, c, :], w_t[:, c, D:], start=(c == 0),
                                   stop=(c == CT - 1))
                mm.then_inc(dots_ready, 1)
                for c in range(CT):
                    mm = pe.matmul(core.bank[5][:], core.xn_t[:, c, :], w_t[:, c, 0:D], start=(c == 0),
                                   stop=(c == CT - 1))
                mm.then_inc(y_ready, 1)
                pe.wait_ge(taken_ready, 1)
                pe.matmul(core.bank[6][:, 0:N], core.ones[:], taken[:], start=True, stop=True).then_inc(count_ready, 1)

            @block.scalar
            def _(act):
                for t in range(CT):
                    act.wait_ge(w_ready, t + 1)
                    act.activation(w_t[:, t, 0:D], core.bank[t % 2][:], ACT.Copy).then_inc(w_copied, 1)
                    act.activation(w_t[:, t, D:], core.bank[2 + t % 2][:, 0:N], ACT.Copy).then_inc(c_copied, 1)
                act.wait_ge(var_ready, 1)
                act.activation(scal[:, 1:2], scal[:, 0:1], ACT.Sqrt).then_inc(std_ready, 1)
                act.wait_ge(top_ready, 1)
                act.activation(dots[:], dots[:], ACT.Exp, bias=scal[:, 3:4], scale=1.0,
                               accum_out=scal[:, 4:5]).then_inc(exp_ready, 1)

            @block.vector
            def _(dve):
                steps = Steps(dve, own)
                dve.wait_ge(loaded, 64)
                for j in range(BG):
                    dve.tensor_scalar(hot[:, j, :], codes_sb[:, j, :], entry_sb[:], None,
                                      ALU.is_equal).then_inc(hot_ready, 1)
                dve.wait_ge(dots_ready, 1)
                steps.then(dve.bn_stats(stats[:], core.bank[4][:, 0:N]))
                steps.then(dve.bn_aggr(mean_var[:], stats[:]))
                dve.tensor_scalar(scal[:, 0:1], mean_var[:, 1:2], 1e-5, None, ALU.add).then_inc(var_ready, 1)
                dve.wait_ge(std_ready, 1)
                steps.then(dve.reciprocal(scal[:, 2:3], scal[:, 1:2]))
                steps.then(dve.tensor_scalar(dots[:], core.bank[4][:, 0:N], mean_var[:, 0:1], scal[:, 2:3],
                                             ALU.subtract, ALU.mult))
                steps.then(dve.tensor_tensor(dots[:], dots[:], bias[:, D:], ALU.mult))
                dve.tensor_reduce(scal[:, 3:4], dots[:], AX.X, ALU.max, negate=True).then_inc(top_ready, 1)
                dve.wait_ge(y_ready, 1)
                steps.then(dve.tensor_tensor(y_sb[:], core.bank[5][:], bias[:, 0:D], ALU.add))
                dve.wait_ge(exp_ready, 1)
                steps.then(dve.reciprocal(scal[:, 5:6], scal[:, 4:5]))
                dve.tensor_scalar(taken[:], dots[:], scal[:, 5:6], 0.5, ALU.mult, ALU.is_gt).then_inc(taken_ready, 1)
                dve.wait_ge(taken_ready, 1)
                steps.then(dve.tensor_reduce(scal[:, 6:7], taken[:], AX.X, ALU.max))
                dve.wait_ge(count_ready, 1)
                steps.then(dve.tensor_scalar(k_mask[:], core.bank[6][:, 0:N], 0.5, scal[:, 6:7], ALU.is_gt,
                                             ALU.mult))
                steps.then(dve.tensor_tensor(y_sb[:].rearrange("p (n o) -> p n o", n=N),
                                             y_sb[:].rearrange("p (n o) -> p n o", n=N),
                                             k_mask[:].unsqueeze(2).to_broadcast([P, N, D // N]), ALU.mult))
                dve.tensor_tensor(core.x[:], core.x[:], y_sb[:], ALU.add)


def feature_cross_attention(core, name, w_qk, context, cols, rows):
    nc = core.nc
    with Stage(core, name) as st:
        w = st.sb("w", [P, CT, 2 * D])
        ctx_sb = st.sb("ctx", [P, KT, D])
        col_sb = st.sb("cols", [P, CT])
        row_sb = st.sb("rows", [P, 5, D])
        junk = st.sb("junk", [P, D])
        sumsq_f = st.sb("sumsq_f", [P, KT])
        rstd_f = st.sb("rstd_f", [P, KT])
        sumsq_k = st.sb("sumsq_k", [P, KT])
        rstd_k = st.sb("rstd_k", [P, KT])
        sumsq_q = st.sb("sumsq_q", [P, 1])
        rstd_q = st.sb("rstd_q", [P, 1])
        q_sb = st.sb("q", [P, D])
        q_t = st.sb("q_t", [P, CT, P])
        k_sb = st.sb("k", [P, KT, D])
        k_t = st.sb("k_t", [P, 2, CT, P])
        s_sb = st.sb("s", [P, SK])
        part_max = st.sb("part_max", [P, NC])
        neg_max = st.sb("neg_max", [P, 1])
        row_sum = st.sb("row_sum", [P, 1])
        r_sum = st.sb("r_sum", [P, 1])
        p_t = st.sb("p_t", [P, KT, P])
        o_sb = st.sb("o", [P, D])
        w_in = st.sem("w_in")
        ctx_in = st.sem("ctx_in")
        rows_in = st.sem("rows_in")
        own = st.sem("own")
        wk_folded = st.sem("wk_folded")
        q_proj = st.sem("q_proj")
        q_biased = st.sem("q_biased")
        q_squared = st.sem("q_squared")
        squared_f = st.sem("squared_f")
        rms_f = st.sem("rms_f")
        rms_q = st.sem("rms_q")
        q_ready = st.sem("q_ready")
        q_turned = st.sem("q_turned")
        q_t_ready = st.sem("q_t_ready")
        k_proj = st.sem("k_proj")
        k_biased = st.sem("k_biased")
        k_squared = st.sem("k_squared")
        rms_k = st.sem("rms_k")
        k_scaled = st.sem("k_scaled")
        k_turned = st.sem("k_turned")
        k_t_ready = st.sem("k_t_ready")
        s_ready = st.sem("s_ready")
        max_ready = st.sem("max_ready")
        exp_ready = st.sem("exp_ready")
        p_turned = st.sem("p_turned")
        p_t_ready = st.sem("p_t_ready")
        o_ready = st.sem("o_ready")
        with nc.Block() as block:
            @block.sync
            def _(sp):
                sp.dma_start(w[:], w_qk).then_inc(w_in, 16)
                sp.dma_start(col_sb[:], cols).then_inc(rows_in, 16)
                sp.dma_start(row_sb[:].rearrange("p r f -> p (r f)"), rows.to_broadcast([P, 5 * D])).then_inc(rows_in, 16)
                sp.dma_start(ctx_sb[:], context).then_inc(ctx_in, 16)

            @block.tensor
            def _(pe):
                pe.wait_ge(w_in, 16)
                for c in range(CT):
                    mm = pe.matmul(core.bank[2][:], core.xn_t[:, c, :], w[:, c, 0:D], start=(c == 0),
                                   stop=(c == CT - 1))
                mm.then_inc(q_proj, 1)
                pe.wait_ge(wk_folded, CT)
                for kt in range(KT):
                    if kt >= 2:
                        pe.wait_ge(k_biased, kt - 1)
                    for c in range(CT):
                        mm = pe.matmul(core.bank[kt % 2][:], core.ctx_t[:, c, kt * P:(kt + 1) * P],
                                       w[:, c, D:], start=(c == 0), stop=(c == CT - 1))
                    mm.then_inc(k_proj, 1)
                pe.wait_ge(q_ready, 1)
                for c in range(CT):
                    mm = pe.transpose(core.bank[3][:, c * P:(c + 1) * P], q_sb[:, c * P:(c + 1) * P], core.ident[:])
                mm.then_inc(q_turned, 1)
                pe.wait_ge(q_t_ready, 1)
                pe.wait_ge(k_biased, KT)

                def turn_k(kt):
                    pe.wait_ge(k_scaled, kt + 1)
                    if kt >= 2:
                        pe.wait_ge(k_t_ready, kt - 1)
                    for c in range(CT):
                        mm = pe.transpose(core.bank[kt % 2][:, c * P:(c + 1) * P],
                                          k_sb[:, kt, c * P:(c + 1) * P], core.ident[:])
                    mm.then_inc(k_turned, 1)

                turn_k(0)
                for kt in range(KT):
                    if kt + 1 < KT:
                        turn_k(kt + 1)
                    pe.wait_ge(k_t_ready, kt + 1)
                    for c in range(CT):
                        mm = pe.matmul(core.bank[4 + kt // 4][:, (kt % 4) * P:(kt % 4 + 1) * P],
                                       q_t[:, c, :], k_t[:, kt % 2, c, :], start=(c == 0), stop=(c == CT - 1))
                    mm.then_inc(s_ready, 1)
                pe.wait_ge(exp_ready, 1)
                for j in range(NC):
                    for i in range(4):
                        kt = 4 * j + i
                        mm = pe.transpose(core.bank[j][:, i * P:(i + 1) * P], s_sb[:, kt * P:(kt + 1) * P],
                                          core.ident[:])
                    mm.then_inc(p_turned, 1)
                for kt in range(KT):
                    pe.wait_ge(p_t_ready, kt + 1)
                    mm = pe.matmul(core.bank[4][:], p_t[:, kt, :], ctx_sb[:, kt, :], start=(kt == 0),
                                   stop=(kt == KT - 1))
                mm.then_inc(o_ready, 1)

            @block.scalar
            def _(act):
                act.wait_ge(ctx_in, 16)
                for kt in range(KT):
                    if kt > 0:
                        act.wait_ge(squared_f, kt)
                    act.activation(junk[:], ctx_sb[:, kt, :], ACT.Square,
                                   accum_out=sumsq_f[:, kt:kt + 1]).then_inc(squared_f, 1)
                act.wait_ge(squared_f, KT)
                act.activation(rstd_f[:], sumsq_f[:], ACT.Sqrt, bias=core.eps6[:], scale=1.0 / D).then_inc(rms_f, 1)
                act.wait_ge(q_biased, 1)
                act.activation(junk[:], q_sb[:], ACT.Square, accum_out=sumsq_q[:]).then_inc(q_squared, 1)
                act.wait_ge(q_squared, 1)
                act.activation(rstd_q[:], sumsq_q[:], ACT.Sqrt, bias=core.eps6[:], scale=1.0 / D).then_inc(rms_q, 1)
                for kt in range(KT):
                    act.wait_ge(k_biased, kt + 1)
                    if kt > 0:
                        act.wait_ge(k_squared, kt)
                    act.activation(junk[:], k_sb[:, kt, :], ACT.Square,
                                   accum_out=sumsq_k[:, kt:kt + 1]).then_inc(k_squared, 1)
                act.wait_ge(k_squared, KT)
                act.activation(rstd_k[:], sumsq_k[:], ACT.Sqrt, bias=core.eps6[:], scale=1.0 / D).then_inc(rms_k, 1)
                for kt in range(KT):
                    act.wait_ge(k_turned, kt + 1)
                    if kt >= 2:
                        act.wait_ge(s_ready, kt - 1)
                    act.activation(k_t[:, kt % 2, :, :], core.bank[kt % 2][:].rearrange("p (c k) -> p c k", c=CT),
                                   ACT.Copy).then_inc(k_t_ready, 1)
                act.wait_ge(max_ready, 1)
                act.activation(s_sb[:], s_sb[:], ACT.Exp, bias=neg_max[:], scale=1.0,
                               accum_out=row_sum[:]).then_inc(exp_ready, 1)
                for kt in range(KT):
                    act.wait_ge(p_turned, kt // 4 + 1)
                    act.activation(p_t[:, kt, :], core.bank[kt // 4][:, (kt % 4) * P:(kt % 4 + 1) * P],
                                   ACT.Copy, scale=rstd_f[:, kt:kt + 1]).then_inc(p_t_ready, 1)

            @block.vector
            def _(dve):
                steps = Steps(dve, own)
                dve.wait_ge(w_in, 16)
                dve.wait_ge(rows_in, 32)
                for c in range(CT):
                    dve.tensor_scalar(w[:, c, D:], w[:, c, D:], col_sb[:, c:c + 1], None, ALU.mult).then_inc(wk_folded, 1)
                dve.wait_ge(q_proj, 1)
                dve.tensor_tensor(q_sb[:], core.bank[2][:], row_sb[:, 0, :], ALU.add).then_inc(q_biased, 1)
                steps.then(dve.scalar_tensor_tensor(row_sb[:, 2, :], row_sb[:, 2, :], float(D ** -0.5),
                                                    row_sb[:, 3, :], ALU.mult, ALU.mult))
                dve.wait_ge(rms_f, 1)
                steps.then(dve.reciprocal(rstd_f[:], rstd_f[:]))
                dve.wait_ge(rms_q, 1)
                steps.then(dve.reciprocal(rstd_q[:], rstd_q[:]))
                dve.scalar_tensor_tensor(q_sb[:], q_sb[:], rstd_q[:], row_sb[:, 2, :], ALU.mult,
                                         ALU.mult).then_inc(q_ready, 1)
                for kt in range(KT):
                    dve.wait_ge(k_proj, kt + 1)
                    dve.scalar_tensor_tensor(k_sb[:, kt, :], core.bank[kt % 2][:], rstd_f[:, kt:kt + 1],
                                             row_sb[:, 1, :], ALU.mult, ALU.add).then_inc(k_biased, 1)
                dve.wait_ge(q_turned, 1)
                dve.tensor_copy(q_t[:], core.bank[3][:].rearrange("p (c q) -> p c q", c=CT)).then_inc(q_t_ready, 1)
                dve.wait_ge(rms_k, 1)
                steps.then(dve.reciprocal(rstd_k[:], rstd_k[:]))
                for kt in range(KT):
                    dve.tensor_scalar(k_sb[:, kt, :], k_sb[:, kt, :], rstd_k[:, kt:kt + 1], None,
                                      ALU.mult).then_inc(k_scaled, 1)
                for j in range(NC):
                    dve.wait_ge(s_ready, 4 * j + 4)
                    steps.then(dve.tensor_copy(s_sb[:, j * 512:(j + 1) * 512], core.bank[4 + j][:]))
                    steps.then(dve.tensor_reduce(part_max[:, j:j + 1], s_sb[:, j * 512:(j + 1) * 512], AX.X, ALU.max))
                dve.tensor_reduce(neg_max[:], part_max[:], AX.X, ALU.max, negate=True).then_inc(max_ready, 1)
                dve.wait_ge(exp_ready, 1)
                steps.then(dve.reciprocal(r_sum[:], row_sum[:]))
                dve.wait_ge(o_ready, 1)
                steps.then(dve.scalar_tensor_tensor(o_sb[:], core.bank[4][:], r_sum[:], row_sb[:, 4, :],
                                                    ALU.mult, ALU.mult))
                dve.tensor_tensor(core.x[:], core.x[:], o_sb[:], ALU.add)


def narrow_cross_attention(core, name, w_dram, w_out, mask_u8, group_cols):
    nc = core.nc
    E = 16
    with Stage(core, name) as st:
        w = st.sb("w", [P, CT, 2 * P + D])
        w_o = st.sb("w_o", [P, CT, D])
        mask_b = st.sb("mask_b", [P, SK], U8)
        mask_sb = st.sb("mask", [P, SK])
        groups = st.sb("groups", [P, NG])
        k_t = st.sb("k_t", [P, SK])
        v_sb = st.sb("v", [P, KT, P])
        q_t = st.sb("q_t", [P, HG, P])
        q_own = st.sb("q_own", [P, HG, P])
        s_sb = st.sb("s", [P, HG, SK])
        p_t = st.sb("p_t", [P, 4, HG * P])
        part_max = st.sb("part_max", [P, HG, NC])
        neg_max = st.sb("neg_max", [P, HG])
        row_sum = st.sb("row_sum", [P, HG])
        r_sum = st.sb("r_sum", [P, HG])
        o_sb = st.sb("o", [P, D])
        o_t = st.sb("o_t", [P, CT, P])
        w_in = st.sem("w_in")
        mask_in = st.sem("mask_in")
        mask_ready = st.sem("mask_ready")
        proj_ready = st.sem("proj_ready")
        kq_copied = st.sem("kq_copied")
        v_copied = st.sem("v_copied")
        q_own_ready = st.sem("q_own_ready")
        s_ready = st.sem("s_ready")
        s_seen = st.sem("s_seen")
        s_read = st.sem("s_read")
        max_ready = st.sem("max_ready")
        exp_ready = st.sem("exp_ready")
        turned = st.sem("turned")
        pt_dve = st.sem("pt_dve")
        pt_act = st.sem("pt_act")
        pv_done = st.sem("pv_done")
        recip_ready = st.sem("recip_ready")
        o_read = st.sem("o_read")
        o_turned = st.sem("o_turned")
        o_t_ready = st.sem("o_t_ready")
        out_ready = st.sem("out_ready")
        out_bank = core.bank[7]
        ring_bank = lambda n: core.bank[3 + n % 4]
        with nc.Block() as block:
            @block.sync
            def _(sp):
                sp.dma_start(w[:], w_dram).then_inc(w_in, 16)
                sp.dma_start(mask_b[:], mask_u8).then_inc(mask_in, 16)
                sp.dma_start(groups[:], group_cols).then_inc(mask_in, 16)
                sp.dma_start(w_o[:], w_out).then_inc(w_in, 16)

            @block.tensor
            def _(pe):
                pe.wait_ge(w_in, 32)
                for n in range(9):
                    if n >= 3:
                        if n - 3 <= NC:
                            pe.wait_ge(kq_copied, n - 2)
                        else:
                            pe.wait_ge(v_copied, n - 3 - NC)
                    out = core.bank[n % 3]
                    if n < NC:
                        for c in range(CT):
                            mm = pe.matmul(out[:], w[:, c, 0:P], core.ctx_t[:, c, n * 512:(n + 1) * 512],
                                           start=(c == 0), stop=(c == CT - 1))
                    elif n == NC:
                        for h in range(HG):
                            for c in range(CT):
                                mm = pe.matmul(out[:, h * P:(h + 1) * P],
                                               w[:, c, 2 * P + h * P:2 * P + (h + 1) * P], core.xn_t[:, c, :],
                                               start=(c == 0), stop=(c == CT - 1))
                    else:
                        for j in range(4):
                            kt = 4 * (n - NC - 1) + j
                            for c in range(CT):
                                mm = pe.matmul(out[:, j * P:(j + 1) * P], core.ctx_t[:, c, kt * P:(kt + 1) * P],
                                               w[:, c, P:2 * P], start=(c == 0), stop=(c == CT - 1))
                    mm.then_inc(proj_ready, 1)
                pe.wait_ge(kq_copied, NC + 1)
                pe.wait_ge(v_copied, 4)
                with pe.Fori(0, NG) as g:
                    pe.wait_ge(q_own_ready, g + 1)
                    for h in range(HG):
                        for c in range(NC):
                            n = h * NC + c
                            if n < 4:
                                pe.wait_ge(pt_dve, g * 8 + 1)
                                pe.wait_ge(pt_act, g * 8 + 1)
                            else:
                                pe.wait_ge(s_read, g * 16 + n - 3)
                            pe.matmul(ring_bank(n)[:], q_own[:, h, :], k_t[:, c * 512:(c + 1) * 512],
                                      start=True, stop=True).then_inc(s_ready, 1)

                    def turn(kt):
                        if kt < 4:
                            pe.wait_ge(s_read, g * 16 + 16)
                            pe.wait_ge(exp_ready, g * 4 + 4)
                        else:
                            pe.wait_ge((pt_act if kt % 2 else pt_dve), g * 8 + (kt - 4) // 2 + 2)
                        for h in range(HG):
                            mm = pe.transpose(ring_bank(kt)[:, h * P:(h + 1) * P],
                                              s_sb[:, h, kt * P:(kt + 1) * P], core.ident[:])
                        mm.then_inc(turned, 1)

                    def weigh(kt):
                        pe.wait_ge((pt_act if kt % 2 else pt_dve), g * 8 + kt // 2 + 2)
                        if kt == 0:
                            pe.wait_ge(o_read, g + 1)
                        for h in range(HG):
                            mm = pe.matmul(out_bank[:, h * E:(h + 1) * E], p_t[:, kt % 4, h * P:(h + 1) * P],
                                           v_sb[:, kt, bass.ds(g * E, E)], start=(kt == 0 and h == 0),
                                           stop=(kt == KT - 1), skip_group_check=True)
                        mm.then_inc(pv_done, 1)

                    for kt in range(KT + 2):
                        if kt < KT:
                            turn(kt)
                        if kt >= 2:
                            weigh(kt - 2)
                pe.wait_ge(o_read, NG + 1)
                for c in range(CT):
                    mm = pe.transpose(core.bank[0][:, c * P:(c + 1) * P], o_sb[:, c * P:(c + 1) * P], core.ident[:])
                mm.then_inc(o_turned, 1)
                pe.wait_ge(o_t_ready, 1)
                for c in range(CT):
                    mm = pe.matmul(core.bank[1][:], o_t[:, c, :], w_o[:, c, :], start=(c == 0), stop=(c == CT - 1))
                mm.then_inc(out_ready, 1)

            @block.scalar
            def _(act):
                act.sem_inc(pt_act, 1)
                for n in range(9):
                    act.wait_ge(proj_ready, n + 1)
                    if n < NC:
                        act.activation(k_t[:, n * 512:(n + 1) * 512], core.bank[n % 3][:], ACT.Copy).then_inc(kq_copied, 1)
                    elif n == NC:
                        act.activation(q_t[:], core.bank[n % 3][:].rearrange("p (h q) -> p h q", h=HG), ACT.Copy,
                                       scale=float(E ** -0.5)).then_inc(kq_copied, 1)
                    else:
                        j = n - NC - 1
                        act.activation(v_sb[:, 4 * j:4 * j + 4, :],
                                       core.bank[n % 3][:].rearrange("p (k d) -> p k d", k=4),
                                       ACT.Copy).then_inc(v_copied, 1)
                with act.Fori(0, NG) as g:
                    for h in range(HG):
                        act.wait_ge(max_ready, g * 4 + h + 1)
                        act.activation(s_sb[:, h, :], s_sb[:, h, :], ACT.Exp, bias=neg_max[:, h:h + 1],
                                       scale=1.0, accum_out=row_sum[:, h:h + 1]).then_inc(exp_ready, 1)
                    for kt in range(1, KT, 2):
                        act.wait_ge(turned, g * 16 + kt + 1)
                        if kt >= 4:
                            act.wait_ge(pv_done, g * 16 + kt - 3)
                        act.activation(p_t[:, kt % 4, :], ring_bank(kt)[:], ACT.Copy).then_inc(pt_act, 1)

            @block.vector
            def _(dve):
                for one_ahead in (o_read, pt_dve):
                    dve.sem_inc(one_ahead, 1)
                dve.wait_ge(mask_in, 32)
                dve.tensor_scalar(mask_sb[:], mask_b[:], 1.0, -LOWEST, ALU.subtract, ALU.mult).then_inc(mask_ready, 1)
                dve.wait_ge(mask_ready, 1)
                dve.wait_ge(kq_copied, NC + 1)
                with dve.Fori(0, NG) as g:
                    dve.tensor_scalar(q_own[:].rearrange("p h q -> p (h q)"), q_t[:].rearrange("p h q -> p (h q)"),
                                      groups[:, bass.ds(g, 1)], None, ALU.mult).then_inc(q_own_ready, 1)
                    for h in range(HG):
                        for c in range(NC):
                            n = h * NC + c
                            dve.wait_ge(s_ready, g * 16 + n + 1)
                            dve.sem_inc(s_seen, 1)
                            dve.tensor_tensor_reduce(
                                s_sb[:, h, c * 512:(c + 1) * 512], ring_bank(n)[:],
                                mask_sb[:, c * 512:(c + 1) * 512], 1.0, LOWEST, ALU.add, ALU.max,
                                part_max[:, h, c:c + 1]).then_inc(s_read, 1)
                        dve.wait_ge(s_read, g * 16 + h * NC + NC)
                        dve.tensor_reduce(neg_max[:, h:h + 1], part_max[:, h, :], AX.X, ALU.max,
                                          negate=True).then_inc(max_ready, 1)
                    for kt in range(0, KT, 2):
                        dve.wait_ge(turned, g * 16 + kt + 1)
                        if kt >= 4:
                            dve.wait_ge(pv_done, g * 16 + kt - 3)
                        dve.tensor_copy(p_t[:, kt % 4, :], ring_bank(kt)[:]).then_inc(pt_dve, 1)
                        if kt == 4:
                            dve.wait_ge(exp_ready, g * 4 + 4)
                            dve.reciprocal(r_sum[:], row_sum[:]).then_inc(recip_ready, 1)
                    dve.wait_ge(pv_done, g * 16 + 16)
                    dve.wait_ge(recip_ready, g + 1)
                    dve.tensor_tensor(o_sb[:, bass.ds(g * HG * E, HG * E)].rearrange("p (h e) -> p h e", h=HG),
                                      out_bank[:, 0:HG * E].rearrange("p (h e) -> p h e", h=HG),
                                      r_sum[:].unsqueeze(2).to_broadcast([P, HG, E]), ALU.mult).then_inc(o_read, 1)
                dve.wait_ge(o_turned, 1)
                dve.tensor_copy(o_t[:], core.bank[0][:].rearrange("p (c q) -> p c q", c=CT)).then_inc(o_t_ready, 1)
                dve.wait_ge(out_ready, 1)
                dve.tensor_tensor(core.x[:], core.x[:], core.bank[1][:], ALU.add)


def latent_attention(core, name, a, causal, eps_inside):
    nc = core.nc
    QR, KR, RD = 192, 64, 64
    LO = QR - P
    PE_W = HG * RD
    SCALE = float((HD + RD) ** -0.5)
    with Stage(core, name) as st:
        w_a = st.sb("w_a", [P, CT, QR + KR + RD])
        row_sb = st.sb("rows", [P, QR + KR])
        rot = st.sb("rot", [P, 2, RD])
        masked = st.sb("mask", [P, P])
        w_hi = [st.sb(f"w_hi{b}", [P, HG * HD + PE_W]) for b in range(2)]
        w_lo = [st.sb(f"w_lo{b}", [LO, HG * HD + PE_W + 2 * HG * HD]) for b in range(2)]
        w_o = [st.sb(f"w_o{b}", [P, HG, D]) for b in range(2)]
        junk = st.sb("junk", [P, QR])
        sumsq = st.sb("sumsq", [P, 2])
        rstd = st.sb("rstd", [P, 2])
        lat = st.sb("lat", [P, QR + KR])
        k_pe = st.sb("k_pe", [P, RD])
        k_sw = st.sb("k_sw", [P, RD])
        lat_hi = st.sb("lat_hi", [P, P])
        lat_lo = st.sb("lat_lo", [LO, 3, P])
        q_t = st.sb("q_t", [P, HG, P])
        k_t = st.sb("k_t", [P, HG, P])
        v_sb = [st.sb(f"v{b}", [P, HG, HD]) for b in range(2)]
        q_pe = st.sb("q_pe", [P, HG, RD])
        q_sw = st.sb("q_sw", [P, HG, RD])
        q_pe_t = st.sb("q_pe_t", [RD, HG, P])
        s_sb = st.sb("s", [P, HG, P])
        neg_max = st.sb("neg_max", [P, HG])
        row_sum = st.sb("row_sum", [P, HG])
        r_sum = st.sb("r_sum", [P, HG])
        p_t = st.sb("p_t", [P, HG, P])
        o_t = st.sb("o_t", [P, HG, P])
        w_a_in = st.sem("w_a_in")
        rows_in = st.sem("rows_in")
        w_in = [st.sem(f"w_in{b}") for b in range(2)]
        o_in = [st.sem(f"o_in{b}") for b in range(2)]
        own = st.sem("own")
        rows_scaled = st.sem("rows_scaled")
        lat_proj = st.sem("lat_proj")
        squared = st.sem("squared")
        rms_ready = st.sem("rms_ready")
        lat_ready = st.sem("lat_ready")
        lat_turned = st.sem("lat_turned")
        lat_t_ready = st.sem("lat_t_ready")
        q_proj = st.sem("q_proj")
        k_proj = st.sem("k_proj")
        v_proj = st.sem("v_proj")
        pe_proj = st.sem("pe_proj")
        q_copied = st.sem("q_copied")
        v_copied = st.sem("v_copied")
        k_copied = st.sem("k_copied")
        pe_read = st.sem("pe_read")
        pe_ready = st.sem("pe_ready")
        pe_turned = st.sem("pe_turned")
        pe_copied = st.sem("pe_copied")
        s_ready = st.sem("s_ready")
        s_masked = st.sem("s_masked")
        max_ready = st.sem("max_ready")
        exp_ready = st.sem("exp_ready")
        recip_ready = st.sem("recip_ready")
        p_ready = st.sem("p_ready")
        p_turned = st.sem("p_turned")
        p_t_ready = st.sem("p_t_ready")
        o_ready = st.sem("o_ready")
        o_t_ready = st.sem("o_t_ready")
        wo_done = st.sem("wo_done")
        x_added = st.sem("x_added")
        banks = core.bank
        per_head = lambda bank: bank[:].rearrange("p (h q) -> p h q", h=HG)

        with nc.Block() as block:
            @block.sync
            def _(sp):
                sp.dma_start(w_a[:], a["w_a"]).then_inc(w_a_in, 16)
                sp.dma_start(row_sb[:], a["rows"].to_broadcast([P, QR + KR])).then_inc(rows_in, 16)
                sp.dma_start(rot[:], a["rot"]).then_inc(rows_in, 16)
                sp.dma_start(masked[:], a["causal"]).then_inc(rows_in, 16)
                for b in range(2):
                    sp.dma_start(w_hi[b][:], a["hi"][b]).then_inc(w_in[b], 16)
                    sp.dma_start(w_lo[b][:], a["lo"][b]).then_inc(w_in[b], 16)
                    sp.dma_start(w_o[b][:], a["o"][b]).then_inc(o_in[b], 16)
                with sp.Fori(0, NG // 2 - 1) as i:
                    for b in range(2):
                        sp.wait_ge(pe_proj, i * 2 + b + 1)
                        sp.dma_start(w_hi[b][:], a["hi"][i * 2 + (2 + b)]).then_inc(w_in[b], 16)
                        sp.dma_start(w_lo[b][:], a["lo"][i * 2 + (2 + b)]).then_inc(w_in[b], 16)
                        sp.wait_ge(wo_done, i * 2 + b + 1)
                        sp.dma_start(w_o[b][:], a["o"][i * 2 + (2 + b)]).then_inc(o_in[b], 16)

            @block.tensor
            def _(pe):
                pe.wait_ge(w_a_in, 16)
                for c in range(CT):
                    mm = pe.matmul(banks[0][:, 0:QR + KR + RD], core.xn_t[:, c, :], w_a[:, c, :], start=(c == 0),
                                   stop=(c == CT - 1))
                mm.then_inc(lat_proj, 1)
                pe.wait_ge(lat_ready, 1)
                pe.transpose(banks[1][:, 0:P], lat[:, 0:P], core.ident[:])
                pe.transpose(banks[1][0:LO, P:2 * P], lat[:, P:QR], core.ident[:])
                pe.transpose(banks[1][0:KR, 2 * P:3 * P], lat[:, QR:], core.ident[:])
                pe.transpose(banks[1][0:RD, 3 * P:4 * P], k_pe[:], core.ident[:]).then_inc(lat_turned, 1)
                pe.wait_ge(lat_t_ready, 2)

                def project(g, b, i):
                    pe.wait_ge(w_in[b], i * 32 + 32)
                    pe.wait_ge(q_copied, g + 1)
                    for h in range(HG):
                        pe.matmul(banks[0][:, h * P:(h + 1) * P], w_hi[b][:, h * HD:(h + 1) * HD], lat_hi[:],
                                  start=True, stop=False)
                        mm = pe.matmul(banks[0][:, h * P:(h + 1) * P], w_lo[b][:, h * HD:(h + 1) * HD],
                                       lat_lo[:, 0, :], start=False, stop=True)
                    mm.then_inc(q_proj, 1)
                    KO = HG * HD + PE_W
                    pe.wait_ge(k_copied, g + 1)
                    for h in range(HG):
                        mm = pe.matmul(banks[1][:, h * P:(h + 1) * P], w_lo[b][:, KO + h * HD:KO + (h + 1) * HD],
                                       lat_lo[:, 1, :], start=True, stop=True)
                    mm.then_inc(k_proj, 1)
                    pe.wait_ge(v_copied, g + 1)
                    pe.matmul(banks[2][:], lat_lo[:, 1, :], w_lo[b][:, KO + HG * HD:], start=True,
                              stop=True).then_inc(v_proj, 1)
                    pe.wait_ge(pe_read, g + 1)
                    pe.matmul(banks[3][:, 0:PE_W], lat_hi[:], w_hi[b][:, HG * HD:], start=True, stop=False)
                    pe.matmul(banks[3][:, 0:PE_W], lat_lo[:, 0, :], w_lo[b][:, HG * HD:KO], start=False,
                              stop=True).then_inc(pe_proj, 1)

                def attend(g, b, i, following):
                    pe.wait_ge(pe_ready, g + 1)
                    pe.wait_ge(pe_copied, g + 1)
                    for j in range(HG // 2):
                        mm = pe.transpose(banks[4][:, j * P:(j + 1) * P],
                                          q_pe[:, 2 * j:2 * j + 2, :].rearrange("p h e -> p (h e)"),
                                          core.ident[:])
                    mm.then_inc(pe_turned, 1)
                    pe.wait_ge(q_copied, g + 2)
                    pe.wait_ge(k_copied, g + 2)
                    pe.wait_ge(pe_copied, g + 2)
                    pe.wait_ge(s_masked, g + 1)
                    for h in range(HG):
                        pe.matmul(banks[5][:, h * P:(h + 1) * P], q_t[:, h, :], k_t[:, h, :], start=True, stop=False)
                        mm = pe.matmul(banks[5][:, h * P:(h + 1) * P], q_pe_t[:, h, :], lat_lo[:, 2, :],
                                       start=False, stop=True)
                    mm.then_inc(s_ready, 1)
                    if following is not None:
                        project(*following)
                    pe.wait_ge(p_ready, g + 1)
                    pe.wait_ge(x_added, g + 1)
                    for h in range(HG):
                        mm = pe.transpose(banks[6][:, h * P:(h + 1) * P], s_sb[:, h, :], core.ident[:])
                    mm.then_inc(p_turned, 1)
                    pe.wait_ge(p_t_ready, g + 1)
                    pe.wait_ge(v_copied, g + 2)
                    for h in range(HG):
                        mm = pe.matmul(banks[7][:, h * P:(h + 1) * P], v_sb[b][:, h, :], p_t[:, h, :], start=True,
                                       stop=True)
                    mm.then_inc(o_ready, 1)
                    pe.wait_ge(o_t_ready, g + 1)
                    pe.wait_ge(o_in[b], i * 16 + 16)
                    for h in range(HG):
                        mm = pe.matmul(banks[6][:], o_t[:, h, :], w_o[b][:, h, :], start=(h == 0),
                                       stop=(h == HG - 1))
                    mm.then_inc(wo_done, 1)

                project(0, 0, 0)
                with pe.Fori(0, NG // 2 - 1) as i:
                    attend(i * 2, 0, i, (i * 2 + 1, 1, i))
                    attend(i * 2 + 1, 1, i, (i * 2 + 2, 0, i + 1))
                attend(NG - 2, 0, NG // 2 - 1, (NG - 1, 1, NG // 2 - 1))
                attend(NG - 1, 1, NG // 2 - 1, None)

            @block.scalar
            def _(act):
                for one_ahead in (q_copied, v_copied):
                    act.sem_inc(one_ahead, 1)
                act.wait_ge(lat_proj, 1)
                act.activation(junk[:], banks[0][:, 0:QR], ACT.Square, accum_out=sumsq[:, 0:1]).then_inc(squared, 1)
                act.wait_ge(squared, 1)
                act.activation(junk[:, 0:KR], banks[0][:, QR:QR + KR], ACT.Square,
                               accum_out=sumsq[:, 1:2]).then_inc(squared, 1)
                act.wait_ge(squared, 2)
                bias = core.eps5[:] if eps_inside else core.zero[:]
                act.activation(rstd[:, 0:1], sumsq[:, 0:1], ACT.Sqrt, bias=bias, scale=1.0 / QR).then_inc(rms_ready, 1)
                act.activation(rstd[:, 1:2], sumsq[:, 1:2], ACT.Sqrt, bias=bias, scale=1.0 / KR).then_inc(rms_ready, 1)

                def keep(g, b):
                    act.wait_ge(q_proj, g + 1)
                    if not (isinstance(g, int) and g == 0):
                        act.wait_ge(s_ready, g)
                    act.activation(q_t[:], per_head(banks[0]), ACT.Copy).then_inc(q_copied, 1)
                    act.wait_ge(v_proj, g + 1)
                    act.activation(v_sb[b][:], per_head(banks[2]), ACT.Copy).then_inc(v_copied, 1)

                def softmax(g, b, following):
                    act.wait_ge(max_ready, g + 1)
                    for h in range(HG):
                        act.activation(s_sb[:, h, :], s_sb[:, h, :], ACT.Exp, bias=neg_max[:, h:h + 1],
                                       scale=1.0, accum_out=row_sum[:, h:h + 1]).then_inc(exp_ready, 1)
                    if following is not None:
                        keep(*following)
                    act.wait_ge(p_turned, g + 1)
                    act.activation(p_t[:], per_head(banks[6]), ACT.Copy).then_inc(p_t_ready, 1)
                    act.wait_ge(o_ready, g + 1)
                    act.activation(o_t[:], per_head(banks[7]), ACT.Copy).then_inc(o_t_ready, 1)

                keep(0, 0)
                with act.Fori(0, NG // 2 - 1) as i:
                    softmax(i * 2, 0, (i * 2 + 1, 1))
                    softmax(i * 2 + 1, 1, (i * 2 + 2, 0))
                softmax(NG - 2, 0, (NG - 1, 1))
                softmax(NG - 1, 1, None)

            @block.vector
            def _(dve):
                for one_ahead in (k_copied, pe_read, pe_copied, s_masked, x_added):
                    dve.sem_inc(one_ahead, 1)
                steps = Steps(dve, own)
                dve.wait_ge(rows_in, 48)
                dve.tensor_scalar(row_sb[:, 0:QR], row_sb[:, 0:QR], SCALE, None, ALU.mult).then_inc(rows_scaled, 1)
                dve.wait_ge(rms_ready, 2)
                if not eps_inside:
                    steps.then(dve.tensor_scalar(rstd[:], rstd[:], 1e-6, None, ALU.add))
                steps.then(dve.reciprocal(rstd[:], rstd[:]))
                dve.wait_ge(rows_scaled, 1)
                steps.then(dve.scalar_tensor_tensor(lat[:, 0:QR], banks[0][:, 0:QR], rstd[:, 0:1], row_sb[:, 0:QR],
                                                    ALU.mult, ALU.mult))
                steps.then(dve.scalar_tensor_tensor(lat[:, QR:], banks[0][:, QR:QR + KR], rstd[:, 1:2],
                                                    row_sb[:, QR:], ALU.mult, ALU.mult))
                half = RD // 2
                src = banks[0][:, QR + KR:QR + KR + RD]
                steps.then(dve.tensor_tensor(k_pe[:], src, rot[:, 0, :], ALU.mult))
                steps.then(dve.tensor_tensor(k_sw[:, 0:half], src[:, half:], rot[:, 1, 0:half], ALU.mult))
                steps.then(dve.tensor_tensor(k_sw[:, half:], src[:, 0:half], rot[:, 1, half:], ALU.mult))
                dve.tensor_tensor(k_pe[:], k_pe[:], k_sw[:], ALU.add).then_inc(lat_ready, 1)
                dve.wait_ge(lat_turned, 1)
                dve.tensor_copy(lat_hi[:], banks[1][:, 0:P]).then_inc(lat_t_ready, 1)
                dve.tensor_copy(lat_lo[:], banks[1][0:LO, P:].rearrange("p (t q) -> p t q", t=3)).then_inc(lat_t_ready, 1)

                def keep(g):
                    dve.wait_ge(k_proj, g + 1)
                    if not (isinstance(g, int) and g == 0):
                        dve.wait_ge(s_ready, g)
                    dve.tensor_copy(k_t[:], per_head(banks[1])).then_inc(k_copied, 1)
                    dve.wait_ge(pe_proj, g + 1)
                    if not (isinstance(g, int) and g == 0):
                        dve.wait_ge(pe_turned, g)
                    src = banks[3][:, 0:PE_W].rearrange("p (h e) -> p h e", h=HG)
                    wide, thin = [P, HG, RD], [P, HG, half]
                    cos = rot[:, 0, :].unsqueeze(1).to_broadcast(wide)
                    lo = rot[:, 1, 0:half].unsqueeze(1).to_broadcast(thin)
                    hi = rot[:, 1, half:].unsqueeze(1).to_broadcast(thin)
                    dve.tensor_tensor(q_pe[:], src, cos, ALU.mult)
                    dve.tensor_tensor(q_sw[:, :, 0:half], src[:, :, half:], lo, ALU.mult)
                    dve.tensor_tensor(q_sw[:, :, half:], src[:, :, 0:half], hi, ALU.mult).then_inc(pe_read, 1)
                    dve.wait_ge(pe_read, g + 2)
                    dve.tensor_tensor(q_pe[:], q_pe[:], q_sw[:], ALU.add).then_inc(pe_ready, 1)

                def turn_rotary(g):
                    dve.wait_ge(pe_turned, g + 1)
                    if not (isinstance(g, int) and g == 0):
                        dve.wait_ge(s_ready, g)
                    for odd in range(2):
                        copy = dve.tensor_copy(
                            q_pe_t[:, odd:HG:2, :],
                            banks[4][odd * RD:(odd + 1) * RD, 0:2 * P].rearrange("p (h q) -> p h q", h=HG // 2))
                    copy.then_inc(pe_copied, 1)

                def softmax(g, following):
                    turn_rotary(g)
                    dve.wait_ge(s_ready, g + 1)
                    if not (isinstance(g, int) and g == 0):
                        dve.wait_ge(p_turned, g)
                    if causal:
                        dve.tensor_tensor(s_sb[:], per_head(banks[5]),
                                          masked[:].unsqueeze(1).to_broadcast([P, HG, P]), ALU.add).then_inc(s_masked, 1)
                    else:
                        dve.tensor_copy(s_sb[:], per_head(banks[5])).then_inc(s_masked, 1)
                    dve.wait_ge(s_masked, g + 2)
                    dve.tensor_reduce(neg_max[:], s_sb[:], AX.X, ALU.max, negate=True).then_inc(max_ready, 1)
                    dve.wait_ge(exp_ready, g * 4 + 4)
                    dve.reciprocal(r_sum[:], row_sum[:]).then_inc(recip_ready, 1)
                    dve.wait_ge(recip_ready, g + 1)
                    dve.tensor_tensor(s_sb[:], s_sb[:], r_sum[:].unsqueeze(2).to_broadcast([P, HG, P]),
                                      ALU.mult).then_inc(p_ready, 1)
                    if following is not None:
                        keep(following)
                    dve.wait_ge(wo_done, g + 1)
                    dve.tensor_tensor(core.x[:], core.x[:], banks[6][:], ALU.add).then_inc(x_added, 1)

                keep(0)
                with dve.Fori(0, NG // 2 - 1) as i:
                    softmax(i * 2, i * 2 + 1)
                    softmax(i * 2 + 1, i * 2 + 2)
                softmax(NG - 2, NG - 1)
                softmax(NG - 1, None)


def latent_inputs(a, name):
    return {"w_a": a[f"{name}_w"], "rows": a[f"{name}_rows"], "rot": a["latent_rot"], "causal": a["causal"],
            "hi": a[f"{name}_hi"], "lo": a[f"{name}_lo"], "o": a[f"{name}_o"]}


STAGE_OF = {
    "L0x": lambda core, name, a: wide_cross_attention(
        core, name, a["L0x_kqv"], a["L0x_o"], a["L0x_mask"],
        rotary=(a["L0x_cos"], a["L0x_sin"], a["L0x_cos_q"], a["L0x_sin_q"])),
    "L0a": lambda core, name, a: per_token_head_attention(core, name, a["L0a_w"], a["L0a_rows"]),
    "L0f": lambda core, name, a: adapter_ffn(core, name, a["L0f_w"], a["L0f_rows"], a["L0f_up"], 3, 16,
                                             starts=a["L0f_starts"], clamp_iota=a["iota8"][:, 0:3]),
    "L1f": lambda core, name, a: adapter_ffn(core, name, a["L1f_w"], a["L1f_rows"], a["L1f_up"], 8, 16,
                                             gate=True, clamp_iota=a["iota8"]),
    "L1x": lambda core, name, a: feature_cross_attention(core, name, a["L1x_w"], a["L1x_ctx"], a["L1x_cols"],
                                                         a["L1x_rows"]),
    "L1a": lambda core, name, a: latent_attention(core, name, latent_inputs(a, "L1a"), True, True),
    "L2x": lambda core, name, a: narrow_cross_attention(core, name, a["L2x_w"], a["L2x_o"], a["L2x_mask"],
                                                        a["L2x_groups"]),
    "L2a": lambda core, name, a: latent_attention(core, name, latent_inputs(a, "L2a"), False, False),
    "L2f": lambda core, name, a: mixed_adapter_ffn(core, name, a["L2f_w"], a["L2f_keys"], a["L2f_up"]),
    "L3a": lambda core, name, a: single_head_attention(core, name, a["L3a_w"], a["L3a_o"], a["L3a_cols"],
                                                       a["L3a_rows"]),
    "L3f": lambda core, name, a: codebook_ffn(core, name, a["L3f_books"], a["L3f_codes"], a["L3f_entry"],
                                              a["L3f_rows"]),
    "L3x": lambda core, name, a: wide_cross_attention(
        core, name, a["L3x_kqv"], a["L3x_o"], a["L3x_mask"], norm_cols=a["L3x_cols"]),
}
STAGES = ("L0x", "L0a", "L0f", "L1x", "L1a", "L1f", "L2x", "L2a", "L2f", "L3x", "L3a", "L3f")


def load_start(core, a):
    nc = core.nc
    with Stage(core, "start") as st:
        loaded = st.sem("loaded")
        with nc.Block() as block:
            @block.sync
            def _(sp):
                sp.dma_start(core.x[:], a["x"]).then_inc(loaded, 16)
                sp.dma_start(core.ident[:], a["ident"]).then_inc(loaded, 16)
                sp.dma_start(core.ctx_t[:], a["ctx_t"]).then_inc(loaded, 16)
                sp.wait_ge(loaded, 48)

            @block.gpsimd
            def _(pool):
                pool.memset(core.ones[:], 1.0)
                pool.memset(core.zero[:], 0.0)
                pool.memset(core.eps5[:], 1e-5)
                pool.memset(core.eps6[:], 1e-6)


def store_result(core, out):
    nc = core.nc
    with Stage(core, "end") as st:
        stored = st.sem("stored")
        with nc.Block() as block:
            @block.sync
            def _(sp):
                sp.dma_start(out, core.x[:]).then_inc(stored, 16)
                sp.wait_ge(stored, 16)


def perceiver(nc, a, out, stages=STAGES):
    with ExitStack() as ctx:
        core = Core(nc, ctx)
        load_start(core, a)
        for name in stages:
            layer_norm(core, name + "_ln")
            STAGE_OF[name](core, name, a)
        store_result(core, out)


def by_feature(w):
    return w.reshape(CT, P, -1).transpose(1, 0, 2)


def grouped(w_q, w_k, w_v, w_o):
    per_group = []
    for g in range(NG):
        cols = [w_k[:, g * HD:(g + 1) * HD], w_q[:, g * HG * HD:(g + 1) * HG * HD], w_v[:, g * HD:(g + 1) * HD]]
        per_group.append(by_feature(np.concatenate(cols, axis=1)))
    return np.stack(per_group), w_o.reshape(NG, HG, HD, D).transpose(0, 2, 1, 3)


def rotary_angles(width, positions):
    inv = (1.0 / 10000.0 ** (np.arange(0, width, 2, dtype=np.float32) / np.float32(width))).astype(np.float32)
    return np.arange(positions, dtype=np.float32)[:, None] * inv[None, :]


def layouts(i):
    f = np.float32
    a = {"x": i["x"][0], "ident": np.eye(P, dtype=f), "ctx_t": by_feature(i["ctx_4096"][0].T)}
    a["L0x_kqv"], a["L0x_o"] = grouped(i["L0_xattn_wq"], i["L0_xattn_wk"], i["L0_xattn_wv"], i["L0_xattn_wo"])
    a["L0x_mask"] = i["mask_BxSxS2_ff0"][0]
    ang = rotary_angles(HD, SK).T
    cos, sin = np.cos(ang).astype(f), np.sin(ang).astype(f)
    scale = f(1.0) / np.sqrt(f(HD))
    a["L0x_cos"] = np.concatenate([cos, cos])
    a["L0x_sin"] = np.concatenate([-sin, sin])
    a["L0x_cos_q"] = a["L0x_cos"][:, :P] * scale
    a["L0x_sin_q"] = a["L0x_sin"][:, :P] * scale
    a["L3x_kqv"], a["L3x_o"] = grouped(i["L3_xattn_q_proj_w"].T, i["L3_xattn_k_proj_w"].T,
                                       i["L3_xattn_v_proj_w"].T, i["L3_xattn_o_proj_w"].T)
    a["L3x_mask"] = i["mask_1x1xSxS2_ff0"][0, 0]
    a["L3x_cols"] = np.stack([i["L3_xattn_q_norm_w"], i["L3_xattn_k_norm_w"]], axis=1)
    row = lambda *parts: np.concatenate(parts)[None, :]
    beside = lambda *parts: by_feature(np.concatenate(parts, axis=1))
    a["iota8"] = np.arange(8, dtype=f)[None, :]
    a["L0a_w"] = beside(*(i[f"L0_attn_W{n}"].T for n in "qkvo"))
    a["L0a_rows"] = row(*(i[f"L0_attn_b{n}"] for n in "qkvo"))
    a["L0f_w"] = beside(i["L0_ffn_weight"].T, i["L0_ffn_lora_A"].reshape(48, D).T)
    a["L0f_rows"] = row(i["L0_ffn_bias"])
    a["L0f_up"] = i["L0_ffn_lora_B"].transpose(0, 2, 1).reshape(48, D)
    a["L0f_starts"] = i["L0_ffn_lora_start_indices"][None, :]
    a["L1f_w"] = beside(i["L1_ffn_base_w"].T, i["L1_ffn_lora_A"].reshape(P, D).T, i["L1_ffn_gate_w"].T)
    a["L1f_rows"] = row(i["L1_ffn_base_b"])
    a["L1f_up"] = i["L1_ffn_lora_B"].transpose(0, 2, 1).reshape(P, D)
    a["L2f_w"] = beside(i["L2_ffn_W_org"].T, i["L2_ffn_lora_down"].transpose(1, 0, 2).reshape(D, D),
                        i["L2_ffn_Wq"].T)
    a["L2f_keys"] = i["L2_ffn_lora_keys"].T
    a["L2f_up"] = by_feature(i["L2_ffn_lora_up"].reshape(D, D))
    a["L3a_w"] = by_feature(i["L3_attn_Wqkv"])
    a["L3a_o"] = i["L3_attn_Wo"]
    a["L3a_cols"] = i["L3_attn_bqkv"][:2 * HD].reshape(2, HD).T
    a["L3a_rows"] = row(i["L3_attn_bqkv"][2 * HD:], i["L3_attn_bo"])
    books = np.zeros((4, 32, 8, 2, 4, 16), f)
    for group in range(8):
        for book in range(4):
            books[book, :, group, group % 2, book] = i["L3_ffn_codebooks"][4 * group + book]
    a["L3f_books"] = books.reshape(P, 8, P)
    codes = np.concatenate([i["L3_ffn_codes"], i["L3_ffn_centroids"]], axis=1)
    codes = np.broadcast_to(codes.reshape(8, 4, 1, D + 32), (8, 4, 32, D + 32))
    a["L3f_codes"] = codes.transpose(1, 2, 0, 3).reshape(P, 8, D + 32)
    a["L3f_entry"] = np.tile(np.arange(32, dtype=f), 4)[:, None]
    a["L3f_rows"] = row(i["L3_ffn_bias"], i["L3_ffn_ln_weight"])
    a["L1x_w"] = beside(i["L1_xattn_Wq_w"].T, i["L1_xattn_Wk_w"].T)
    a["L1x_ctx"] = i["ctx_4096"][0].reshape(KT, P, D).transpose(1, 0, 2)
    a["L1x_cols"] = i["L1_xattn_fn_w"].reshape(CT, P).T
    a["L1x_rows"] = row(*(i[f"L1_xattn_{n}"] for n in ("Wq_b", "Wk_b", "qn_w", "kn_w", "fn_w")))
    ang = rotary_angles(64, P)
    cos, sin = np.cos(ang).astype(f), np.sin(ang).astype(f)
    a["latent_rot"] = np.stack([np.concatenate([cos, cos], 1), np.concatenate([-sin, sin], 1)], axis=1)
    a["causal"] = np.triu(np.full((P, P), LOWEST, f), 1)
    halves = np.r_[0:64:2, 1:64:2]
    a.update(latent_layouts("L1a", i["L1_attn_q_a_w"], i["L1_attn_kv_a_w"], i["L1_attn_q_a_norm_w"],
                            i["L1_attn_kv_a_norm_w"], i["L1_attn_q_b_w"], i["L1_attn_kv_b_w"],
                            i["L1_attn_o_w"], halves))
    a.update(latent_layouts("L2a", i["L2_attn_w_qa"], i["L2_attn_w_kva"], i["L2_attn_g_qa"],
                            i["L2_attn_g_kva"], i["L2_attn_w_qb"], i["L2_attn_w_kvb"], i["L2_attn_w_o"],
                            np.arange(64)))
    q_by_place = i["L2_xattn_w_q"].reshape(NG, HG, 16, D).transpose(1, 0, 2, 3).reshape(D, D)
    a["L2x_w"] = beside(i["L2_xattn_w_k"].T, i["L2_xattn_w_v"].T, q_by_place.T)
    a["L2x_o"] = by_feature(i["L2_xattn_w_out"].T)
    a["L2x_mask"] = i["mask_SxS2_bk0"]
    a["L2x_groups"] = np.repeat(np.eye(NG, dtype=f), 16, axis=0)
    return a


def latent_layouts(name, q_a, kv_a, g_q, g_kv, q_b, kv_b, o, order):
    kv_a = np.concatenate([kv_a[:, :64], kv_a[:, 64:][:, order]], axis=1)
    q_b = q_b.reshape(192, NG, HG, 192).transpose(1, 0, 2, 3)
    q_b = np.concatenate([q_b[..., :128].reshape(NG, 192, 512), q_b[..., 128:][..., order].reshape(NG, 192, 256)], 2)
    kv_b = kv_b.reshape(64, NG, HG, 2, 128).transpose(1, 0, 3, 2, 4).reshape(NG, 64, 1024)
    return {f"{name}_w": by_feature(np.concatenate([q_a, kv_a], axis=1)),
            f"{name}_rows": np.concatenate([g_q, g_kv])[None, :],
            f"{name}_hi": q_b[:, :128], f"{name}_lo": np.concatenate([q_b[:, 128:], kv_b], axis=2),
            f"{name}_o": o.reshape(NG, HG, HD, D).transpose(0, 2, 1, 3)}


def kernel(**inputs):
    import concourse.bacc as bacc
    from concourse.bass_utils import run_bass_kernel_spmd

    laid = {k: np.ascontiguousarray(v) for k, v in layouts({k: np.asarray(v) for k, v in inputs.items()}).items()}
    nc = bacc.Bacc("TRN2", target_bir_lowering=False, num_devices=1)
    aps = {k: nc.dram_tensor(f"in_{k}", v.shape, mybir.dt.from_np(v.dtype), kind="ExternalInput").ap()
           for k, v in laid.items()}
    out = nc.dram_tensor("out", (P, D), F32, kind="ExternalOutput").ap()
    perceiver(nc, aps, out)
    result = run_bass_kernel_spmd(nc, [{f"in_{k}": v for k, v in laid.items()}], core_ids=[0])
    return result.results[0]["out"].reshape(1, P, D)
```

```python
from contextlib import ExitStack

import numpy as np

import concourse.bass as bass
from concourse import mybir
from concourse.alu_op_type import AluOpType as ALU

ACT = mybir.ActivationFunctionType
AX = mybir.AxisListType
F32 = mybir.dt.float32
I32 = mybir.dt.int32
U8 = mybir.dt.uint8

P = 128
D = 512
CT = D // P
SK = 2048
KT = SK // P
NC = SK // 512
HD = 128
NH = 32
NG = 8
HG = NH // NG
LOWEST = float(np.finfo(np.float32).min)


class Steps:

    def __init__(self, eng, sem, base=0):
        self.eng, self.sem, self.base, self.n = eng, sem, base, 0

    def then(self, ins):
        self.n += 1
        ins.then_inc(self.sem, 1)
        self.eng.wait_ge(self.sem, self.base + self.n)


class Memory:

    ALIGN = 64

    def __init__(self, nc):
        self.nc, self.first, self.end = nc, -(-nc.sbuf_base // 64) * 64, nc.sbuf_usable_end
        self.taken = {}

    def take(self, name, shape, dt=F32):
        size = int(np.prod(shape[1:])) * mybir.dt.size(dt)
        size = -(-size // self.ALIGN) * self.ALIGN
        at = self.first
        for lo, hi in sorted(self.taken.values()):
            if at + size <= lo:
                break
            at = max(at, hi)
        assert at + size <= self.end, f"{name} does not fit"
        self.taken[name] = (at, at + size)
        return self.nc.alloc_sbuf_tensor_at(name, shape, dt, offset=at)

    def give_back(self, names):
        for name in names:
            del self.taken[name]


class Core:

    def __init__(self, nc, ctx):
        self.nc = nc
        self.memory = Memory(nc)
        self.ctx = ctx
        self.freed = ExitStack()
        self.keys = None
        self.stale = []
        sb = self.memory.take
        self.x = sb("x", [P, D])
        self.xn_t = sb("xn_t", [P, CT, P])
        self.ctx_t = sb("ctx_t", [P, CT, SK])
        self.ident = sb("ident", [P, P])
        self.ones = sb("ones", [P, P])
        self.eps5 = sb("eps5", [P, 1])
        self.eps6 = sb("eps6", [P, 1])
        self.zero = sb("zero", [P, 1])
        self.bank = [ctx.enter_context(nc.psum_tensor(f"bank{i}", [P, 512], F32)) for i in range(8)]

    def end_with_last(self, stage):
        self.memory.give_back(stage.names)
        self.stale = self.stale + stage.sems
        self.freed.callback(stage.ctx.close)

    def clear_stale(self, pool):
        for s in self.stale:
            pool.sem_clear(s)


class Stage:

    def __init__(self, core, name):
        self.core, self.name = core, name
        self.ctx = ExitStack()
        self.sems, self.names = [], []

    def __enter__(self):
        return self

    def sb(self, name, shape, dt=F32):
        self.names.append(f"{self.name}_{name}")
        return self.core.memory.take(self.names[-1], shape, dt)

    def sem(self, name):
        s = self.ctx.enter_context(self.core.nc.semaphore(f"{self.name}_{name}"))
        self.sems.append(s)
        return s

    def __exit__(self, *exc):
        if exc[0] is None:
            self.core.memory.give_back(self.names)
            self.core.freed.close()
            self.core.freed, self.core.stale = self.ctx, self.sems


class LayerNorm:

    def __init__(self, core, st, bank):
        self.core, self.bank = core, bank
        self.xn = st.sb("ln_xn", [P, D])
        self.stats = st.sb("ln_stats", [P, 6])
        self.mean_var = st.sb("ln_mean_var", [P, 2])
        self.small = st.sb("ln_small", [P, 3])
        self.own = st.sem("ln_own")
        self.var_ready = st.sem("ln_var_ready")
        self.std_ready = st.sem("ln_std_ready")
        self.xn_ready = st.sem("ln_xn_ready")
        self.turned = st.sem("ln_turned")
        self.ready = st.sem("ln_ready")

    def vector(self, dve):
        core, steps = self.core, Steps(dve, self.own)
        veps, std, rstd = (self.small[:, i:i + 1] for i in range(3))
        steps.then(dve.bn_stats(self.stats[:], core.x[:]))
        steps.then(dve.bn_aggr(self.mean_var[:], self.stats[:]))
        dve.tensor_scalar(veps, self.mean_var[:, 1:2], 1e-5, None, ALU.add).then_inc(self.var_ready, 1)
        dve.wait_ge(self.std_ready, 1)
        steps.then(dve.reciprocal(rstd, std))
        dve.tensor_scalar(self.xn[:], core.x[:], self.mean_var[:, 0:1], rstd, ALU.subtract,
                          ALU.mult).then_inc(self.xn_ready, 1)
        dve.wait_ge(self.turned, 1)
        dve.tensor_copy(core.xn_t[:], self.bank[:].rearrange("p (c q) -> p c q", c=CT)).then_inc(self.ready, 1)

    def scalar(self, act):
        act.wait_ge(self.var_ready, 1)
        act.activation(self.small[:, 1:2], self.small[:, 0:1], ACT.Sqrt).then_inc(self.std_ready, 1)

    def tensor(self, pe):
        pe.wait_ge(self.xn_ready, 1)
        for c in range(CT):
            mm = pe.transpose(self.bank[:, c * P:(c + 1) * P], self.xn[:, c * P:(c + 1) * P], self.core.ident[:])
        mm.then_inc(self.turned, 1)
        pe.wait_ge(self.ready, 1)


def wide_cross_attention(core, name, wkqv, wo, mask, rotary=None, norm_cols=None):
    nc = core.nc
    SCALE = float(1.0 / np.sqrt(np.float32(HD)))
    PROJ = NC + 1
    with Stage(core, name) as st:
        if rotary is not None:
            cos_t = st.sb("cos_t", [P, SK])
            sin_t = st.sb("sin_t", [P, SK])
            cos_q = st.sb("cos_q", [P, P])
            sin_q = st.sb("sin_q", [P, P])
        else:
            cols = st.sb("cols", [P, 3])
        w_kqv = st.sb("w_kqv", [P, CT, 768])
        w_o = st.sb("w_o", [P, HG, D])
        mask_sb = st.sb("mask", [P, SK])
        consts_in = st.sem("consts_in")
        w_in = st.sem("w_in")
        wo_in = st.sem("wo_in")

        def issue(sp):
            sp.dma_start(w_kqv[:], wkqv[0]).then_inc(w_in, 16)
            sp.dma_start(mask_sb[:], mask).then_inc(consts_in, 16)
            if rotary is not None:
                for t, src in zip((cos_t, sin_t, cos_q, sin_q), rotary):
                    sp.dma_start(t[:], src).then_inc(consts_in, 16)
            else:
                sp.dma_start(cols[:, 0:2], norm_cols).then_inc(consts_in, 16)
            sp.dma_start(w_o[:], wo[0]).then_inc(wo_in, 16)

        following = yield issue
        norm = LayerNorm(core, st, core.bank[0])
        k_t = st.sb("k_t", [P, SK])
        q_t = st.sb("q_t", [P, HG * P])
        v_sb = st.sb("v", [P, KT, HD])
        aux = st.sb("aux", [P, 2, 512])
        s_sb = st.sb("s", [P, HG, SK])
        p_t = st.sb("p_t", [P, 4, HG * P])
        part_max = st.sb("part_max", [P, HG, NC])
        neg_max = st.sb("neg_max", [P, HG])
        row_sum = st.sb("row_sum", [P, HG])
        r_sum = st.sb("r_sum", [P, HG])
        diag = st.sb("diag", [P, HG, P])
        o_raw = st.sb("o_raw", [P, HG * P])
        o_t = st.sb("o_t", [P, HG * P])
        if rotary is None:
            rms = st.sb("rms", [P, 512])

        proj_ready = st.sem("proj_ready")
        proj_read_act = st.sem("proj_read_act")
        proj_read_dve = st.sem("proj_read_dve")
        aux_used = st.sem("aux_used")
        sumsq_ready = st.sem("sumsq_ready")
        rms_ready = st.sem("rms_ready")
        kq_ready = st.sem("kq_ready")
        v_proj = st.sem("v_proj")
        v_ready = st.sem("v_ready")
        s_ready = st.sem("s_ready")
        s_seen = st.sem("s_seen")
        s_read = st.sem("s_read")
        max_ready = st.sem("max_ready")
        exp_ready = st.sem("exp_ready")
        turned = st.sem("turned")
        pt_dve = st.sem("pt_dve")
        pt_act = st.sem("pt_act")
        pv_done = st.sem("pv_done")
        diag_ready = st.sem("diag_ready")
        rinv_ready = st.sem("rinv_ready")
        o_raw_ready = st.sem("o_raw_ready")
        o_ready = st.sem("o_ready")
        wo_done = st.sem("wo_done")
        x_added = st.sem("x_added")
        dve_own = st.sem("dve_own")
        diag_recip = st.sem("diag_recip")
        out_bank, rinv_bank, wo_bank = core.bank[7], core.bank[0], core.bank[1]
        proj_bank = lambda n: core.bank[n % 3]
        ring_bank = lambda n: core.bank[3 + n % 4]

        consts_all = 16 * (5 if rotary is not None else 2)

        with nc.Block() as block:
            @block.gpsimd
            def _(pool):
                core.clear_stale(pool)

            @block.sync
            def _(sp):
                following(sp)
                with sp.Fori(1, NG) as g:
                    sp.wait_ge(v_proj, g * 4)
                    sp.dma_start(w_kqv[:], wkqv[g]).then_inc(w_in, 16)
                    sp.wait_ge(wo_done, g)
                    sp.dma_start(w_o[:], wo[g]).then_inc(wo_in, 16)

            @block.tensor
            def _(pe):
                norm.tensor(pe)
                with pe.Fori(0, NG) as g:
                    pe.wait_ge(w_in, g * 16 + 16)

                    def sum_squares(n):
                        pe.wait_ge(proj_read_act, g * PROJ + n + 1)
                        if n > 0:
                            pe.wait_ge(rms_ready, g * PROJ + n)
                        pe.matmul(out_bank[:], core.ones[:], aux[:, n % 2, :], start=True,
                                  stop=True).then_inc(sumsq_ready, 1)

                    for n in range(PROJ):
                        if n < 3:
                            pe.wait_ge(x_added, g + 1)
                            pe.wait_ge(v_ready, g * 4 + 1)
                        else:
                            pe.wait_ge(proj_read_dve, g * PROJ + n - 2)
                        if n < NC:
                            for c in range(CT):
                                mm = pe.matmul(proj_bank(n)[:], w_kqv[:, c, 0:128],
                                               core.ctx_t[:, c, n * 512:(n + 1) * 512],
                                               start=(c == 0), stop=(c == CT - 1))
                        else:
                            for h in range(HG):
                                for c in range(CT):
                                    mm = pe.matmul(proj_bank(n)[:, h * P:(h + 1) * P],
                                                   w_kqv[:, c, 128 + h * HD:128 + (h + 1) * HD],
                                                   core.xn_t[:, c, :], start=(c == 0), stop=(c == CT - 1))
                        mm.then_inc(proj_ready, 1)
                        if rotary is None and n > 0:
                            sum_squares(n - 1)

                    def project_v(n):
                        if n < 3:
                            pe.wait_ge(proj_read_dve, g * PROJ + n + 3)
                        else:
                            pe.wait_ge(v_ready, g * 4 + 2)
                        for j in range(4):
                            kt = 4 * n + j
                            for c in range(CT):
                                mm = pe.matmul(proj_bank(PROJ + n)[:, j * P:(j + 1) * P],
                                               core.ctx_t[:, c, kt * P:(kt + 1) * P],
                                               w_kqv[:, c, 640:768], start=(c == 0), stop=(c == CT - 1))
                        mm.then_inc(v_proj, 1)

                    project_v(0)
                    if rotary is None:
                        sum_squares(PROJ - 1)
                    project_v(1)
                    pe.wait_ge(kq_ready, g * PROJ + PROJ)
                    for h in range(HG):
                        for c in range(NC):
                            n = h * NC + c
                            if n < 4:
                                pe.wait_ge(pt_dve, g * 8 + 1)
                                pe.wait_ge(pt_act, g * 8 + 1)
                            else:
                                pe.wait_ge(s_read, g * 16 + n - 3)
                            pe.matmul(ring_bank(n)[:], q_t[:, h * P:(h + 1) * P],
                                      k_t[:, c * 512:(c + 1) * 512], start=True,
                                      stop=True).then_inc(s_ready, 1)
                    project_v(2)
                    project_v(3)

                    def turn(kt):
                        if kt < 4:
                            pe.wait_ge(s_read, g * 16 + 16)
                            pe.wait_ge(exp_ready, g * 4 + 4)
                        else:
                            pe.wait_ge((pt_act if kt % 2 else pt_dve), g * 8 + (kt - 4) // 2 + 2)
                        for h in range(HG):
                            mm = pe.transpose(ring_bank(kt)[:, h * P:(h + 1) * P],
                                              s_sb[:, h, kt * P:(kt + 1) * P], core.ident[:])
                        mm.then_inc(turned, 1)

                    def weigh(kt):
                        pe.wait_ge((pt_act if kt % 2 else pt_dve), g * 8 + kt // 2 + 2)
                        if kt == 0:
                            pe.wait_ge(v_ready, g * 4 + 5)
                        pe.matmul(out_bank[:], v_sb[:, kt, :], p_t[:, kt % 4, :], start=(kt == 0),
                                  stop=(kt == KT - 1)).then_inc(pv_done, 1)

                    for kt in range(KT + 2):
                        if kt < KT:
                            turn(kt)
                        if kt >= 2:
                            weigh(kt - 2)
                    pe.wait_ge(diag_ready, g * 4 + 4)
                    pe.matmul(rinv_bank[:], core.ones[:], diag[:].rearrange("p h q -> p (h q)"),
                              start=True, stop=True).then_inc(rinv_ready, 1)
                    pe.wait_ge(wo_in, g * 16 + 16)
                    pe.wait_ge(o_ready, g + 1)
                    for h in range(HG):
                        mm = pe.matmul(wo_bank[:], o_t[:, h * P:(h + 1) * P], w_o[:, h, :],
                                       start=(h == 0), stop=(h == HG - 1))
                    mm.then_inc(wo_done, 1)

            @block.scalar
            def _(act):
                norm.scalar(act)
                act.sem_inc(v_ready, 1)
                act.sem_inc(pt_act, 1)
                with act.Fori(0, NG) as g:
                    for n in range(PROJ):
                        act.wait_ge(proj_ready, g * PROJ + n + 1)
                        src = proj_bank(n)
                        if rotary is not None:
                            if n >= 2:
                                act.wait_ge(aux_used, g * PROJ + n)
                            else:
                                act.wait_ge(aux_used, g * PROJ + 1)
                            act.activation(aux[64:128, n % 2, :], src[0:64, :], ACT.Copy)
                            act.activation(aux[0:64, n % 2, :], src[64:128, :],
                                           ACT.Copy).then_inc(proj_read_act, 1)
                        else:
                            if n >= 2:
                                act.wait_ge(sumsq_ready, g * PROJ + n - 1)
                            act.activation(aux[:, n % 2, :], src[:], ACT.Square,
                                           scale=float(HD ** -0.5)).then_inc(proj_read_act, 1)
                            if n > 0:
                                act.wait_ge(sumsq_ready, g * PROJ + n)
                                act.wait_ge(kq_ready, g * PROJ + n - 1)
                                act.activation(rms[:], out_bank[:], ACT.Sqrt,
                                               bias=core.eps5[:]).then_inc(rms_ready, 1)
                    if rotary is None:
                        act.wait_ge(sumsq_ready, g * PROJ + PROJ)
                        act.wait_ge(kq_ready, g * PROJ + PROJ - 1)
                        act.activation(rms[:], out_bank[:], ACT.Sqrt, bias=core.eps5[:]).then_inc(rms_ready, 1)

                    def keep_v(n):
                        act.wait_ge(v_proj, g * 4 + n + 1)
                        act.activation(v_sb[:, 4 * n:4 * n + 4, :],
                                       proj_bank(PROJ + n)[:].rearrange("p (k d) -> p k d", k=4),
                                       ACT.Copy).then_inc(v_ready, 1)

                    keep_v(0)
                    keep_v(1)
                    for h in range(HG):
                        act.wait_ge(max_ready, g * 4 + h + 1)
                        act.activation(s_sb[:, h, :], s_sb[:, h, :], ACT.Exp, bias=neg_max[:, h:h + 1],
                                       scale=1.0, accum_out=row_sum[:, h:h + 1]).then_inc(exp_ready, 1)
                    keep_v(2)
                    keep_v(3)
                    for kt in range(1, KT, 2):
                        act.wait_ge(turned, g * 16 + kt + 1)
                        if kt >= 4:
                            act.wait_ge(pv_done, g * 16 + kt - 3)
                        act.activation(p_t[:, kt % 4, :], ring_bank(kt)[:], ACT.Copy).then_inc(pt_act, 1)
                    act.wait_ge(pv_done, g * 16 + 16)
                    act.activation(o_raw[:], out_bank[:], ACT.Copy).then_inc(o_raw_ready, 1)

            @block.vector
            def _(dve):
                norm.vector(dve)
                for one_ahead in (x_added, pt_dve, aux_used):
                    dve.sem_inc(one_ahead, 1)
                dve.wait_ge(consts_in, consts_all)
                own_a_round = 2 * PROJ if rotary is not None else PROJ
                if rotary is None:
                    dve.tensor_scalar(cols[:, 2:3], cols[:, 0:1], SCALE, None, ALU.mult)
                with dve.Fori(0, NG) as g:
                    steps = Steps(dve, dve_own, base=g * own_a_round)
                    for n in range(PROJ):
                        dst = k_t[:, n * 512:(n + 1) * 512] if n < NC else q_t[:]
                        dve.wait_ge(proj_read_act, g * PROJ + n + 1)
                        if rotary is not None:
                            if n < NC:
                                view = lambda t: t
                                cos, sin = (t[:, n * 512:(n + 1) * 512] for t in (cos_t, sin_t))
                            else:
                                view = lambda t: t.rearrange("p (h q) -> p h q", h=HG)
                                cos, sin = (t[:].unsqueeze(1).to_broadcast([P, HG, P]) for t in (cos_q, sin_q))
                            dve.tensor_tensor(view(dst), view(proj_bank(n)[:]), cos,
                                              ALU.mult).then_inc(proj_read_dve, 1)
                            steps.then(dve.tensor_tensor(view(aux[:, n % 2, :]), view(aux[:, n % 2, :]),
                                                         sin, ALU.mult))
                            dve.wait_ge(proj_read_dve, g * PROJ + n + 1)
                            steps.then(dve.tensor_tensor(dst, dst, aux[:, n % 2, :], ALU.add))
                            dve.sem_inc(aux_used, 1)
                            dve.sem_inc(kq_ready, 1)
                        else:
                            weight = cols[:, 1:2] if n < NC else cols[:, 2:3]
                            dve.tensor_scalar(dst, proj_bank(n)[:], weight, None,
                                              ALU.mult).then_inc(proj_read_dve, 1)
                            dve.wait_ge(rms_ready, g * PROJ + n + 1)
                            steps.then(dve.reciprocal(rms[:], rms[:]))
                            dve.wait_ge(proj_read_dve, g * PROJ + n + 1)
                            dve.tensor_tensor(dst, dst, rms[:], ALU.mult).then_inc(kq_ready, 1)
                    assert steps.n == own_a_round
                    for h in range(HG):
                        for c in range(NC):
                            n = h * NC + c
                            dve.wait_ge(s_ready, g * 16 + n + 1)
                            dve.sem_inc(s_seen, 1)
                            dve.tensor_tensor_reduce(
                                s_sb[:, h, c * 512:(c + 1) * 512], ring_bank(n)[:],
                                mask_sb[:, c * 512:(c + 1) * 512], 1.0, LOWEST, ALU.add, ALU.max,
                                part_max[:, h, c:c + 1]).then_inc(s_read, 1)
                        dve.wait_ge(s_read, g * 16 + h * NC + NC)
                        dve.tensor_reduce(neg_max[:, h:h + 1], part_max[:, h, :], AX.X, ALU.max,
                                          negate=True).then_inc(max_ready, 1)
                    for kt in range(0, KT, 2):
                        dve.wait_ge(turned, g * 16 + kt + 1)
                        if kt >= 4:
                            dve.wait_ge(pv_done, g * 16 + kt - 3)
                        dve.tensor_copy(p_t[:, kt % 4, :], ring_bank(kt)[:]).then_inc(pt_dve, 1)
                        if kt == 4:
                            dve.wait_ge(exp_ready, g * 4 + 4)
                            dve.reciprocal(r_sum[:], row_sum[:]).then_inc(diag_recip, 1)
                            dve.wait_ge(diag_recip, g + 1)
                            for h in range(HG):
                                dve.tensor_scalar(diag[:, h, :], core.ident[:], r_sum[:, h:h + 1], None,
                                                  ALU.mult).then_inc(diag_ready, 1)
                    dve.wait_ge(rinv_ready, g + 1)
                    dve.wait_ge(o_raw_ready, g + 1)
                    dve.tensor_tensor(o_t[:], o_raw[:], rinv_bank[:], ALU.mult).then_inc(o_ready, 1)
                    dve.wait_ge(wo_done, g + 1)
                    dve.tensor_tensor(core.x[:], core.x[:], wo_bank[:], ALU.add).then_inc(x_added, 1)


class ContextKeys:

    def __init__(self, core, a):
        self.core, self.a = core, a
        self.st = st = Stage(core, "L1k")
        self.k_t = st.sb("k_t", [P, KT, CT, P])
        self.rstd_f = st.sb("rstd_f", [P, KT])
        self.work = work = Stage(core, "L1kw")
        self.w = work.sb("w", [P, CT, D])
        self.cols = work.sb("cols", [P, CT])
        self.row = work.sb("row", [P, D])
        self.ctx = work.sb("ctx", [P, 2, 4, D])
        self.junk = work.sb("junk", [P, D])
        self.raw = work.sb("raw", [P, 4, D])
        self.sumsq_f = work.sb("sumsq_f", [P, KT])
        self.rms_f = work.sb("rms_f", [P, KT])
        self.sumsq_k = work.sb("sumsq_k", [P, KT])
        self.rms_k = work.sb("rms_k", [P, KT])
        self.rstd_k = work.sb("rstd_k", [P, KT])
        sem = work.sem
        self.loaded = sem("loaded")
        self.ctx_in = [sem(f"ctx_in{i}") for i in range(2)]
        self.folded = sem("folded")
        self.squared_f = sem("squared_f")
        self.rms_f_ready = sem("rms_f_ready")
        self.rstd_f_ready = sem("rstd_f_ready")
        self.proj = sem("proj")
        self.biased = sem("biased")
        self.squared_k = sem("squared_k")
        self.rms_k_ready = sem("rms_k_ready")
        self.rstd_k_ready = sem("rstd_k_ready")
        self.scaled = sem("scaled")
        self.turned = sem("turned")
        self.kept = sem("kept")

    def made(self):
        self.core.memory.give_back(self.work.names)
        self.st.sems += self.work.sems
        self.st.ctx = self.work.ctx

    def issue(self, sp):
        sp.dma_start(self.w[:], self.a["L1x_w"][:, :, D:]).then_inc(self.loaded, 16)
        sp.dma_start(self.cols[:], self.a["L1x_cols"]).then_inc(self.loaded, 16)
        sp.dma_start(self.row[:], self.a["L1x_rows"][:, D:2 * D].to_broadcast([P, D])).then_inc(self.loaded, 16)
        for j in range(NC):
            if j >= 2:
                sp.wait_ge(self.squared_f, 4 * j - 4)
            sp.dma_start(self.ctx[:, j % 2], self.a["L1x_ctx"][:, 4 * j:4 * j + 4, :]).then_inc(self.ctx_in[j % 2], 16)

    def tensor(self, pe, kt):
        if kt < KT:
            if kt == 0:
                pe.wait_ge(self.folded, CT)
            if kt >= 2:
                pe.wait_ge(self.biased, kt - 1)
            for c in range(CT):
                mm = pe.matmul(self.core.bank[5 + kt % 2][:], self.core.ctx_t[:, c, kt * P:(kt + 1) * P],
                               self.w[:, c, :], start=(c == 0), stop=(c == CT - 1))
            mm.then_inc(self.proj, 1)
        if kt >= 3:
            pe.wait_ge(self.scaled, kt - 2)
            if kt > 3:
                pe.wait_ge(self.kept, kt - 3)
            for c in range(CT):
                mm = pe.transpose(self.core.bank[7][:, c * P:(c + 1) * P], self.raw[:, (kt - 3) % 4, c * P:(c + 1) * P],
                                  self.core.ident[:])
            mm.then_inc(self.turned, 1)

    def scalar_context(self, act, j):
        act.wait_ge(self.ctx_in[j % 2], 16 * (j // 2) + 16)
        for kt in range(4 * j, 4 * j + 4):
            if kt > 0:
                act.wait_ge(self.squared_f, kt)
            act.activation(self.junk[:], self.ctx[:, j % 2, kt % 4, :], ACT.Square,
                           accum_out=self.sumsq_f[:, kt:kt + 1]).then_inc(self.squared_f, 1)
        act.wait_ge(self.squared_f, 4 * j + 4)
        act.activation(self.rms_f[:, 4 * j:4 * j + 4], self.sumsq_f[:, 4 * j:4 * j + 4], ACT.Sqrt,
                       bias=self.core.eps6[:], scale=1.0 / D).then_inc(self.rms_f_ready, 1)

    def scalar(self, act, kt):
        if kt < KT:
            act.wait_ge(self.biased, kt + 1)
            if kt > 0:
                act.wait_ge(self.squared_k, kt)
            else:
                act.wait_ge(self.squared_f, KT)
            act.activation(self.junk[:], self.raw[:, kt % 4, :], ACT.Square,
                           accum_out=self.sumsq_k[:, kt:kt + 1]).then_inc(self.squared_k, 1)
            act.wait_ge(self.squared_k, kt + 1)
            act.activation(self.rms_k[:, kt:kt + 1], self.sumsq_k[:, kt:kt + 1], ACT.Sqrt,
                           bias=self.core.eps6[:], scale=1.0 / D).then_inc(self.rms_k_ready, 1)
        if 1 <= kt <= KT:
            act.wait_ge(self.rstd_k_ready, kt)
            act.activation(self.raw[:, (kt - 1) % 4, :], self.raw[:, (kt - 1) % 4, :], ACT.Copy,
                           scale=self.rstd_k[:, kt - 1:kt]).then_inc(self.scaled, 1)
        if kt >= 3:
            act.wait_ge(self.turned, kt - 2)
            act.activation(self.k_t[:, kt - 3, :, :], self.core.bank[7][:].rearrange("p (c k) -> p c k", c=CT),
                           ACT.Copy).then_inc(self.kept, 1)

    def vector_start(self, dve):
        dve.wait_ge(self.loaded, 48)
        for c in range(CT):
            dve.tensor_scalar(self.w[:, c, :], self.w[:, c, :], self.cols[:, c:c + 1], None,
                              ALU.mult).then_inc(self.folded, 1)

    def vector(self, dve, kt):
        if kt % 4 == 0 and kt < KT:
            j = kt // 4
            dve.wait_ge(self.rms_f_ready, j + 1)
            dve.reciprocal(self.rstd_f[:, 4 * j:4 * j + 4], self.rms_f[:, 4 * j:4 * j + 4]).then_inc(self.rstd_f_ready, 1)
            dve.wait_ge(self.rstd_f_ready, j + 1)
        if kt < KT:
            dve.wait_ge(self.proj, kt + 1)
            if kt >= 4:
                dve.wait_ge(self.turned, kt - 3)
            dve.scalar_tensor_tensor(self.raw[:, kt % 4, :], self.core.bank[5 + kt % 2][:],
                                     self.rstd_f[:, kt:kt + 1], self.row[:], ALU.mult,
                                     ALU.add).then_inc(self.biased, 1)
        if 1 <= kt <= KT:
            dve.wait_ge(self.rms_k_ready, kt)
            dve.reciprocal(self.rstd_k[:, kt - 1:kt], self.rms_k[:, kt - 1:kt]).then_inc(self.rstd_k_ready, 1)


def context_keys_alone(core, keys):
    with core.nc.Block() as block:
        @block.sync
        def _(sp):
            keys.issue(sp)

        @block.tensor
        def _(pe):
            for kt in range(KT + 3):
                keys.tensor(pe, kt)

        @block.scalar
        def _(act):
            for j in range(NC):
                keys.scalar_context(act, j)
            for kt in range(KT + 3):
                keys.scalar(act, kt)

        @block.vector
        def _(dve):
            keys.vector_start(dve)
            for kt in range(KT + 1):
                keys.vector(dve, kt)


def per_token_head_attention(core, name, w_qkvo, rows, a):
    nc = core.nc
    H, E = 32, 16
    THRESH = 0.001
    PARTS = 16
    HP = H // PARTS
    with Stage(core, name) as st:
        w = st.sb("w", [P, CT, 4 * D])
        bias = st.sb("bias", [P, 4 * D])
        w_in = st.sem("w_in")
        bias_in = st.sem("bias_in")

        def issue(sp):
            for j in range(4):
                sp.dma_start(w[:, :, j * D:(j + 1) * D], w_qkvo[:, :, j * D:(j + 1) * D]).then_inc(w_in, 16)
            sp.dma_start(bias[:], rows.to_broadcast([P, 4 * D])).then_inc(bias_in, 16)

        following = yield issue
        norm = LayerNorm(core, st, core.bank[0])
        core.keys = keys = ContextKeys(core, a)
        qkv = st.sb("qkv", [P, 3, D])
        prod = st.sb("prod", [P, HP * H * E])
        prod_pool = st.sb("prod_pool", [P, 2, HP * H * E])
        s_sb = st.sb("s", [P, H, H])
        keep = st.sb("keep", [P, H, H])
        top = st.sb("top", [P, H])
        total = st.sb("total", [P, H])
        r_total = st.sb("r_total", [P, H])
        o_sb = st.sb("o", [P, H, E])
        o_t = st.sb("o_t", [P, CT, P])
        qkv_ready = st.sem("qkv_ready")
        own = st.sem("own")
        qkv_biased = st.sem("qkv_biased")
        prod_ready = st.sem("prod_ready")
        pool_ready = st.sem("pool_ready")
        summed = st.sem("summed")
        shifted = st.sem("shifted")
        exp_ready = st.sem("exp_ready")
        kept = st.sem("kept")
        o_ready = st.sem("o_ready")
        o_turned = st.sem("o_turned")
        o_t_ready = st.sem("o_t_ready")
        out_ready = st.sem("out_ready")
        q = qkv[:, 0, :].rearrange("p (h e) -> p h e", h=H)
        k = qkv[:, 1, :].rearrange("p (g e) -> p g e", g=H)
        v = qkv[:, 2, :].rearrange("p (g e) -> p e g", g=H)

        def factors(phase, i):
            heads = slice(i * HP, (i + 1) * HP)
            left, right = (k, q[:, heads, :]) if phase == 0 else (v, s_sb[:, heads, :])
            shape = [P, HP, H, E] if phase == 0 else [P, HP, E, H]
            return shape, left.unsqueeze(1).to_broadcast(shape), right.unsqueeze(2).to_broadcast(shape)

        with nc.Block() as block:
            @block.gpsimd
            def _(pool):
                core.clear_stale(pool)
                for phase in range(2):
                    if phase == 0:
                        pool.wait_ge(qkv_biased, 3)
                    else:
                        pool.wait_ge(kept, 1)
                    for i in range(1, PARTS, 2):
                        n = phase * PARTS + i
                        if n >= 5:
                            pool.wait_ge(summed, n - 3)
                        shape, left, right = factors(phase, i)
                        view = prod_pool[:, (n // 2) % 2, :].rearrange("p (a b c) -> p a b c", a=shape[1], b=shape[2])
                        pool.tensor_tensor(view, left, right, ALU.mult).then_inc(pool_ready, 1)

            @block.sync
            def _(sp):
                keys.issue(sp)
                following(sp)

            @block.tensor
            def _(pe):
                norm.tensor(pe)
                pe.wait_ge(w_in, 64)
                for j in range(3):
                    for c in range(CT):
                        mm = pe.matmul(core.bank[j][:], core.xn_t[:, c, :], w[:, c, j * D:(j + 1) * D],
                                       start=(c == 0), stop=(c == CT - 1))
                    mm.then_inc(qkv_ready, 1)
                for kt in range(KT + 3):
                    keys.tensor(pe, kt)
                pe.wait_ge(o_ready, 1)
                o_flat = o_sb[:].rearrange("p h e -> p (h e)")
                for c in range(CT):
                    mm = pe.transpose(core.bank[3][:, c * P:(c + 1) * P], o_flat[:, c * P:(c + 1) * P],
                                      core.ident[:])
                mm.then_inc(o_turned, 1)
                pe.wait_ge(o_t_ready, 1)
                for c in range(CT):
                    mm = pe.matmul(core.bank[4][:], o_t[:, c, :], w[:, c, 3 * D:], start=(c == 0),
                                   stop=(c == CT - 1))
                mm.then_inc(out_ready, 1)

            @block.scalar
            def _(act):
                norm.scalar(act)
                for j in range(NC):
                    keys.scalar_context(act, j)
                for kt in range(KT + 3):
                    if kt == 8:
                        act.wait_ge(shifted, 1)
                        act.activation(s_sb[:], s_sb[:], ACT.Exp, scale=float(E ** -0.5)).then_inc(exp_ready, 1)
                    keys.scalar(act, kt)

            @block.vector
            def _(dve):
                norm.vector(dve)
                steps = Steps(dve, own)
                keys.vector_start(dve)
                dve.wait_ge(bias_in, 16)
                for j in range(3):
                    dve.wait_ge(qkv_ready, j + 1)
                    dve.tensor_tensor(qkv[:, j, :], core.bank[j][:], bias[:, j * D:(j + 1) * D],
                                      ALU.add).then_inc(qkv_biased, 1)
                dve.wait_ge(qkv_biased, 3)
                prods, tile = 0, 0

                def sum_parts(phase, dst):
                    nonlocal prods, tile
                    for i in range(PARTS):
                        n = phase * PARTS + i
                        shape, left, right = factors(phase, i)
                        split = dict(a=shape[1], b=shape[2])
                        if i % 2 == 0:
                            if n >= 2:
                                dve.wait_ge(summed, n - 1)
                            view = prod[:].rearrange("p (a b c) -> p a b c", **split)
                            dve.tensor_tensor(view, left, right, ALU.mult).then_inc(prod_ready, 1)
                            prods += 1
                            dve.wait_ge(prod_ready, prods)
                        else:
                            view = prod_pool[:, (n // 2) % 2, :].rearrange("p (a b c) -> p a b c", **split)
                            dve.wait_ge(pool_ready, n // 2 + 1)
                        dve.tensor_reduce(dst[:, i * HP:(i + 1) * HP, :], view, AX.X, ALU.add).then_inc(summed, 1)
                        if i % 2 and tile <= KT:
                            keys.vector(dve, tile)
                            tile += 1
                    dve.wait_ge(summed, (phase + 1) * PARTS)

                sum_parts(0, s_sb)
                dve.tensor_scalar(keep[:], s_sb[:], float(E ** -0.5), THRESH, ALU.mult, ALU.is_gt)
                steps.then(dve.tensor_reduce(top[:], s_sb[:], AX.X, ALU.max))
                dve.tensor_tensor(s_sb[:], s_sb[:], top[:].unsqueeze(2).to_broadcast([P, H, H]),
                                  ALU.subtract).then_inc(shifted, 1)
                dve.wait_ge(exp_ready, 1)
                dve.tensor_tensor(s_sb[:], s_sb[:], keep[:], ALU.mult).then_inc(kept, 1)
                dve.wait_ge(kept, 1)
                steps.then(dve.tensor_reduce(total[:], s_sb[:], AX.X, ALU.add))
                steps.then(dve.reciprocal(r_total[:], total[:]))
                sum_parts(1, o_sb)
                dve.tensor_tensor(o_sb[:], o_sb[:], r_total[:].unsqueeze(2).to_broadcast([P, H, E]),
                                  ALU.mult).then_inc(o_ready, 1)
                while tile <= KT:
                    keys.vector(dve, tile)
                    tile += 1
                steps.then(dve.tensor_tensor(core.x[:], core.x[:], bias[:, 3 * D:], ALU.add))
                dve.wait_ge(o_turned, 1)
                dve.tensor_copy(o_t[:], core.bank[3][:].rearrange("p (c q) -> p c q", c=CT)).then_inc(o_t_ready, 1)
                dve.wait_ge(out_ready, 1)
                dve.tensor_tensor(core.x[:], core.x[:], core.bank[4][:], ALU.add)
        keys.made()


def adapter_ffn(core, name, w_in_dram, rows, up_dram, adapters, rank, gate=False, starts=None,
                clamp_iota=None):
    nc = core.nc
    R = adapters * rank
    WIDE = R + (adapters if gate else 0)
    with Stage(core, name) as st:
        w = st.sb("w", [P, CT, D + WIDE])
        bias = st.sb("bias", [P, D])
        up = st.sb("up", [R, D])
        iota = st.sb("iota", [P, adapters])
        start_rows = st.sb("starts", [P, 4], I32)
        w_in = st.sem("w_in")
        rows_in = st.sem("rows_in")

        def issue(sp):
            sp.dma_start(w[:], w_in_dram).then_inc(w_in, 16)
            sp.dma_start(up[:], up_dram).then_inc(w_in, 16)
            sp.dma_start(bias[:], rows.to_broadcast([P, D])).then_inc(rows_in, 16)
            sp.dma_start(iota[:], clamp_iota.to_broadcast([P, adapters])).then_inc(rows_in, 16)
            if starts is not None:
                sp.dma_start(start_rows[:], starts.to_broadcast([P, 4])).then_inc(rows_in, 16)

        following = yield issue
        norm = LayerNorm(core, st, core.bank[0])
        low = st.sb("low", [P, WIDE])
        coef = st.sb("coef", [P, adapters])
        first = st.sb("first", [P, adapters])
        second = st.sb("second", [P, adapters])
        rest = st.sb("rest", [P, adapters])
        scal = st.sb("scal", [P, 8])
        low_c = st.sb("low_c", [P, R])
        low_t = st.sb("low_t", [R, P])
        reached = st.sb("reached", [P, 4])
        own = st.sem("own")
        low_ready = st.sem("low_ready")
        scaled = st.sem("scaled")
        turned = st.sem("turned")
        low_t_ready = st.sem("low_t_ready")
        out_ready = st.sem("out_ready")
        gap_ready = st.sem("gap_ready")
        gap_exp = st.sem("gap_exp")
        with nc.Block() as block:
            @block.gpsimd
            def _(pool):
                core.clear_stale(pool)

            @block.sync
            def _(sp):
                following(sp)

            @block.tensor
            def _(pe):
                norm.tensor(pe)
                pe.wait_ge(w_in, 32)
                for c in range(CT):
                    mm = pe.matmul(core.bank[1][:, 0:WIDE], core.xn_t[:, c, :], w[:, c, D:],
                                   start=(c == 0), stop=(c == CT - 1))
                mm.then_inc(low_ready, 1)
                for c in range(CT):
                    pe.matmul(core.bank[0][:], core.xn_t[:, c, :], w[:, c, 0:D], start=(c == 0), stop=False)
                pe.wait_ge(scaled, 1)
                pe.transpose(core.bank[2][0:R, 0:P], low_c[:], core.ident[:]).then_inc(turned, 1)
                pe.wait_ge(low_t_ready, 1)
                pe.matmul(core.bank[0][:], low_t[:], up[:], start=False, stop=True).then_inc(out_ready, 1)

            @block.scalar
            def _(act):
                norm.scalar(act)
                if gate:
                    act.wait_ge(gap_ready, 1)
                    act.activation(scal[:, 3:4], scal[:, 2:3], ACT.Exp).then_inc(gap_exp, 1)

            @block.vector
            def _(dve):
                norm.vector(dve)
                steps = Steps(dve, own)
                dve.wait_ge(rows_in, 16 * (3 if starts is not None else 2))
                steps.then(dve.tensor_tensor(core.x[:], core.x[:], bias[:], ALU.add))
                if not gate:
                    steps.then(dve.tensor_scalar(reached[:], start_rows[:], 0.0, None, ALU.is_le))
                    steps.then(dve.tensor_reduce(scal[:, 0:1], reached[:], AX.X, ALU.add))
                    steps.then(dve.tensor_scalar(scal[:, 1:2], scal[:, 0:1], 2.0, 0.0, ALU.subtract, ALU.max))
                    steps.then(dve.tensor_scalar(scal[:, 2:3], scal[:, 1:2], float(adapters - 1), None, ALU.min))
                    steps.then(dve.tensor_scalar(scal[:, 3:4], scal[:, 0:1], 1.5, None, ALU.is_gt))
                    steps.then(dve.tensor_scalar(coef[:], iota[:], scal[:, 2:3], scal[:, 3:4],
                                                 ALU.is_equal, ALU.mult))
                    dve.wait_ge(low_ready, 1)
                    source = core.bank[1][:, 0:R]
                else:
                    dve.wait_ge(low_ready, 1)
                    steps.then(dve.tensor_copy(low[:], core.bank[1][:, 0:WIDE]))
                    logits = low[:, R:]

                    def pick(dst, values, peak):
                        steps.then(dve.tensor_reduce(peak, values, AX.X, ALU.max))
                        steps.then(dve.tensor_scalar(dst, values, peak, float(adapters), ALU.not_equal, ALU.mult))
                        steps.then(dve.tensor_tensor(dst, dst, iota[:], ALU.add))
                        steps.then(dve.tensor_reduce(scal[:, 6:7], dst, AX.X, ALU.min))
                        steps.then(dve.tensor_scalar(dst, iota[:], scal[:, 6:7], None, ALU.is_equal))

                    pick(first[:], logits, scal[:, 0:1])
                    steps.then(dve.scalar_tensor_tensor(rest[:], first[:], LOWEST, logits, ALU.mult, ALU.add))
                    pick(second[:], rest[:], scal[:, 1:2])
                    dve.tensor_tensor(scal[:, 2:3], scal[:, 1:2], scal[:, 0:1], ALU.subtract).then_inc(gap_ready, 1)
                    dve.wait_ge(gap_exp, 1)
                    steps.then(dve.tensor_scalar(scal[:, 4:5], scal[:, 3:4], 1.0, 0.5, ALU.add, ALU.mult))
                    steps.then(dve.reciprocal(scal[:, 5:6], scal[:, 4:5]))
                    steps.then(dve.tensor_scalar(coef[:], second[:], scal[:, 3:4], None, ALU.mult))
                    steps.then(dve.tensor_tensor(coef[:], coef[:], first[:], ALU.add))
                    steps.then(dve.tensor_scalar(coef[:], coef[:], scal[:, 5:6], None, ALU.mult))
                    source = low[:, 0:R]
                dve.tensor_tensor(low_c[:].rearrange("p (a r) -> p a r", a=adapters),
                                  source.rearrange("p (a r) -> p a r", a=adapters),
                                  coef[:].unsqueeze(2).to_broadcast([P, adapters, rank]),
                                  ALU.mult).then_inc(scaled, 1)
                dve.wait_ge(turned, 1)
                dve.tensor_copy(low_t[:], core.bank[2][0:R, 0:P]).then_inc(low_t_ready, 1)
                dve.wait_ge(out_ready, 1)
                dve.tensor_tensor(core.x[:], core.x[:], core.bank[0][:], ALU.add)


def mixed_adapter_ffn(core, name, w_dram, keys_dram, up_dram):
    nc = core.nc
    A = 8
    with Stage(core, name) as st:
        w = st.sb("w", [P, CT, 2 * D + P])
        keys = st.sb("keys", [P, A])
        up = st.sb("up", [P, CT, D])
        w_in = st.sem("w_in")

        def issue(sp):
            sp.dma_start(w[:], w_dram).then_inc(w_in, 16)
            sp.dma_start(keys[:], keys_dram).then_inc(w_in, 16)
            sp.dma_start(up[:], up_dram).then_inc(w_in, 16)

        following = yield issue
        norm = LayerNorm(core, st, core.bank[0])
        mean = st.sb("mean", [P, CT])
        q_wide = st.sb("q_wide", [P, P])
        coef = st.sb("coef", [P, A])
        coef_col = st.sb("coef_col", [P, CT])
        scal = st.sb("scal", [P, 4])
        h_t = st.sb("h_t", [P, CT, P])
        own = st.sem("own")
        mean_ready = st.sem("mean_ready")
        q_ready = st.sem("q_ready")
        q_wide_ready = st.sem("q_wide_ready")
        scores_ready = st.sem("scores_ready")
        top_ready = st.sem("top_ready")
        exp_ready = st.sem("exp_ready")
        h_ready = st.sem("h_ready")
        h_scaled = st.sem("h_scaled")
        out_ready = st.sem("out_ready")
        with nc.Block() as block:
            @block.gpsimd
            def _(pool):
                core.clear_stale(pool)

            @block.sync
            def _(sp):
                following(sp)

            @block.tensor
            def _(pe):
                norm.tensor(pe)
                pe.wait_ge(w_in, 48)
                pe.wait_ge(mean_ready, 1)
                for c in range(CT):
                    mm = pe.matmul(core.bank[1][:, 0:1], w[:, c, 2 * D:], mean[:, c:c + 1], start=(c == 0),
                                   stop=(c == CT - 1))
                mm.then_inc(q_ready, 1)
                for t in range(CT):
                    for c in range(CT):
                        mm = pe.matmul(core.bank[3][:, t * P:(t + 1) * P], w[:, c, D + t * P:D + (t + 1) * P],
                                       core.xn_t[:, c, :], start=(c == 0), stop=(c == CT - 1))
                mm.then_inc(h_ready, 1)
                pe.wait_ge(q_wide_ready, 1)
                pe.matmul(core.bank[2][:, 0:A], q_wide[:], keys[:], start=True, stop=True).then_inc(scores_ready, 1)
                for c in range(CT):
                    pe.matmul(core.bank[0][:], core.xn_t[:, c, :], w[:, c, 0:D], start=(c == 0), stop=False)
                pe.wait_ge(h_scaled, CT)
                for t in range(CT):
                    mm = pe.matmul(core.bank[0][:], h_t[:, t, :], up[:, t, :], start=False, stop=(t == CT - 1))
                mm.then_inc(out_ready, 1)

            @block.scalar
            def _(act):
                norm.scalar(act)
                act.wait_ge(top_ready, 1)
                act.activation(coef[:], core.bank[2][:, 0:A], ACT.Exp, bias=scal[:, 1:2],
                               scale=float(P ** -0.5), accum_out=scal[:, 2:3]).then_inc(exp_ready, 1)

            @block.vector
            def _(dve):
                norm.vector(dve)
                steps = Steps(dve, own)
                dve.wait_ge(norm.ready, 1)
                steps.then(dve.tensor_reduce(mean[:], core.xn_t[:], AX.X, ALU.add))
                dve.tensor_scalar(mean[:], mean[:], 1.0 / P, None, ALU.mult).then_inc(mean_ready, 1)
                dve.wait_ge(q_ready, 1)
                steps.then(dve.tensor_copy(scal[:, 3:4], core.bank[1][:, 0:1]))
                dve.tensor_scalar(q_wide[:], core.ones[:], scal[:, 3:4], None, ALU.mult).then_inc(q_wide_ready, 1)
                dve.wait_ge(scores_ready, 1)
                steps.then(dve.tensor_reduce(scal[:, 0:1], core.bank[2][:, 0:A], AX.X, ALU.max, negate=True))
                dve.tensor_scalar(scal[:, 1:2], scal[:, 0:1], float(P ** -0.5), None, ALU.mult).then_inc(top_ready, 1)
                dve.wait_ge(exp_ready, 1)
                steps.then(dve.reciprocal(scal[:, 0:1], scal[:, 2:3]))
                steps.then(dve.tensor_scalar(coef[:], coef[:], scal[:, 0:1], None, ALU.mult))
                steps.then(dve.tensor_copy(coef_col[0:64, :], coef[0:64, 0:A:2]))
                steps.then(dve.tensor_copy(coef_col[64:128, :], coef[64:128, 1:A:2]))
                dve.wait_ge(h_ready, 1)
                for t in range(CT):
                    dve.tensor_scalar(h_t[:, t, :], core.bank[3][:, t * P:(t + 1) * P], coef_col[:, t:t + 1],
                                      None, ALU.mult).then_inc(h_scaled, 1)
                dve.wait_ge(out_ready, 1)
                dve.tensor_tensor(core.x[:], core.x[:], core.bank[0][:], ALU.add)


def single_head_attention(core, name, wqkv, wo, qk_cols, rows):
    nc = core.nc
    SCALE = float(HD ** -0.5)
    with Stage(core, name) as st:
        w = st.sb("w", [P, CT, 3 * HD])
        w_o = st.sb("w_o", [P, D])
        cols = st.sb("cols", [P, 2])
        bias = st.sb("bias", [P, HD + D])
        w_in = st.sem("w_in")
        rows_in = st.sem("rows_in")

        def issue(sp):
            sp.dma_start(w[:], wqkv).then_inc(w_in, 16)
            sp.dma_start(w_o[:], wo).then_inc(w_in, 16)
            sp.dma_start(cols[:], qk_cols).then_inc(rows_in, 16)
            sp.dma_start(bias[:], rows.to_broadcast([P, HD + D])).then_inc(rows_in, 16)

        following = yield issue
        norm = LayerNorm(core, st, core.bank[0])
        qk_t = st.sb("qk_t", [P, 2, P])
        v_sb = st.sb("v", [P, HD])
        p_sb = st.sb("p", [P, P])
        p_t = st.sb("p_t", [P, P])
        o_t = st.sb("o_t", [P, P])
        scal = st.sb("scal", [P, 4])
        own = st.sem("own")
        qk_ready = st.sem("qk_ready")
        v_ready = st.sem("v_ready")
        qk_biased = st.sem("qk_biased")
        v_biased = st.sem("v_biased")
        s_ready = st.sem("s_ready")
        top_ready = st.sem("top_ready")
        exp_ready = st.sem("exp_ready")
        p_ready = st.sem("p_ready")
        p_turned = st.sem("p_turned")
        p_t_ready = st.sem("p_t_ready")
        o_ready = st.sem("o_ready")
        o_t_ready = st.sem("o_t_ready")
        out_ready = st.sem("out_ready")
        with nc.Block() as block:
            @block.gpsimd
            def _(pool):
                core.clear_stale(pool)

            @block.sync
            def _(sp):
                following(sp)

            @block.tensor
            def _(pe):
                norm.tensor(pe)
                pe.wait_ge(w_in, 32)
                for j in range(2):
                    for c in range(CT):
                        mm = pe.matmul(core.bank[0][:, j * P:(j + 1) * P], w[:, c, j * HD:(j + 1) * HD],
                                       core.xn_t[:, c, :], start=(c == 0), stop=(c == CT - 1))
                mm.then_inc(qk_ready, 1)
                for c in range(CT):
                    mm = pe.matmul(core.bank[1][:, 0:HD], core.xn_t[:, c, :], w[:, c, 2 * HD:], start=(c == 0),
                                   stop=(c == CT - 1))
                mm.then_inc(v_ready, 1)
                pe.wait_ge(qk_biased, 2)
                pe.matmul(core.bank[2][:, 0:P], qk_t[:, 0, :], qk_t[:, 1, :], start=True,
                          stop=True).then_inc(s_ready, 1)
                pe.wait_ge(p_ready, 1)
                pe.transpose(core.bank[3][:, 0:P], p_sb[:], core.ident[:]).then_inc(p_turned, 1)
                pe.wait_ge(p_t_ready, 1)
                pe.wait_ge(v_biased, 1)
                pe.matmul(core.bank[4][:, 0:P], v_sb[:], p_t[:], start=True, stop=True).then_inc(o_ready, 1)
                pe.wait_ge(o_t_ready, 1)
                pe.matmul(core.bank[5][:], o_t[:], w_o[:], start=True, stop=True).then_inc(out_ready, 1)

            @block.scalar
            def _(act):
                norm.scalar(act)
                act.wait_ge(top_ready, 1)
                act.activation(p_sb[:], core.bank[2][:, 0:P], ACT.Exp, bias=scal[:, 1:2], scale=SCALE,
                               accum_out=scal[:, 2:3]).then_inc(exp_ready, 1)

            @block.vector
            def _(dve):
                norm.vector(dve)
                steps = Steps(dve, own)
                dve.wait_ge(rows_in, 32)
                steps.then(dve.tensor_tensor(core.x[:], core.x[:], bias[:, HD:], ALU.add))
                dve.wait_ge(qk_ready, 1)
                for j in range(2):
                    dve.tensor_scalar(qk_t[:, j, :], core.bank[0][:, j * P:(j + 1) * P], cols[:, j:j + 1], None,
                                      ALU.add).then_inc(qk_biased, 1)
                dve.wait_ge(v_ready, 1)
                dve.tensor_tensor(v_sb[:], core.bank[1][:, 0:HD], bias[:, 0:HD], ALU.add).then_inc(v_biased, 1)
                dve.wait_ge(s_ready, 1)
                steps.then(dve.tensor_reduce(scal[:, 0:1], core.bank[2][:, 0:P], AX.X, ALU.max, negate=True))
                dve.tensor_scalar(scal[:, 1:2], scal[:, 0:1], SCALE, None, ALU.mult).then_inc(top_ready, 1)
                dve.wait_ge(exp_ready, 1)
                steps.then(dve.reciprocal(scal[:, 3:4], scal[:, 2:3]))
                dve.tensor_scalar(p_sb[:], p_sb[:], scal[:, 3:4], None, ALU.mult).then_inc(p_ready, 1)
                dve.wait_ge(p_turned, 1)
                dve.tensor_copy(p_t[:], core.bank[3][:, 0:P]).then_inc(p_t_ready, 1)
                dve.wait_ge(o_ready, 1)
                dve.tensor_copy(o_t[:], core.bank[4][:, 0:P]).then_inc(o_t_ready, 1)
                dve.wait_ge(out_ready, 1)
                dve.tensor_tensor(core.x[:], core.x[:], core.bank[5][:], ALU.add)


def codebook_ffn(core, name, books, codes, entry, rows):
    nc = core.nc
    N = 32
    BG = 8
    with Stage(core, name) as st:
        books_sb = st.sb("books", [P, BG, P])
        codes_sb = st.sb("codes", [P, BG, D + N], I32)
        entry_sb = st.sb("entry", [P, 1])
        bias = st.sb("bias", [P, D + N])
        loaded = st.sem("loaded")

        def issue(sp):
            sp.dma_start(books_sb[:], books).then_inc(loaded, 16)
            sp.dma_start(codes_sb[:], codes).then_inc(loaded, 16)
            sp.dma_start(entry_sb[:], entry).then_inc(loaded, 16)
            sp.dma_start(bias[:], rows.to_broadcast([P, D + N])).then_inc(loaded, 16)

        following = yield issue
        norm = LayerNorm(core, st, core.bank[7])
        hot = st.sb("hot", [P, BG, D + N])
        w_t = st.sb("w_t", [P, CT, D + N])
        dots = st.sb("dots", [P, N])
        stats = st.sb("stats", [P, 6])
        mean_var = st.sb("mean_var", [P, 2])
        scal = st.sb("scal", [P, 8])
        taken = st.sb("taken", [P, N])
        k_mask = st.sb("k_mask", [P, N])
        y_sb = st.sb("y", [P, D])
        own = st.sem("own")
        hot_ready = st.sem("hot_ready")
        w_ready = st.sem("w_ready")
        w_copied = st.sem("w_copied")
        c_copied = st.sem("c_copied")
        dots_ready = st.sem("dots_ready")
        y_ready = st.sem("y_ready")
        var_ready = st.sem("var_ready")
        std_ready = st.sem("std_ready")
        top_ready = st.sem("top_ready")
        exp_ready = st.sem("exp_ready")
        taken_ready = st.sem("taken_ready")
        count_ready = st.sem("count_ready")
        with nc.Block() as block:
            @block.gpsimd
            def _(pool):
                core.clear_stale(pool)

            @block.sync
            def _(sp):
                following(sp)

            @block.tensor
            def _(pe):
                norm.tensor(pe)
                for t in range(CT):
                    pe.wait_ge(hot_ready, 2 * t + 2)
                    big, small = core.bank[t % 2], core.bank[2 + t % 2]
                    if t >= 2:
                        pe.wait_ge(w_copied, t - 1)
                        pe.wait_ge(c_copied, t - 1)
                    for j in range(2):
                        pe.matmul(big[:], books_sb[:, 2 * t + j, :], hot[:, 2 * t + j, 0:D], start=(j == 0),
                                  stop=(j == 1))
                    for j in range(2):
                        mm = pe.matmul(small[:, 0:N], books_sb[:, 2 * t + j, :], hot[:, 2 * t + j, D:],
                                       start=(j == 0), stop=(j == 1))
                    mm.then_inc(w_ready, 1)
                pe.wait_ge(w_copied, CT)
                pe.wait_ge(c_copied, CT)
                for c in range(CT):
                    mm = pe.matmul(core.bank[4][:, 0:N], core.xn_t[:, c, :], w_t[:, c, D:], start=(c == 0),
                                   stop=(c == CT - 1))
                mm.then_inc(dots_ready, 1)
                for c in range(CT):
                    mm = pe.matmul(core.bank[5][:], core.xn_t[:, c, :], w_t[:, c, 0:D], start=(c == 0),
                                   stop=(c == CT - 1))
                mm.then_inc(y_ready, 1)
                pe.wait_ge(taken_ready, 1)
                pe.matmul(core.bank[6][:, 0:N], core.ones[:], taken[:], start=True, stop=True).then_inc(count_ready, 1)

            @block.scalar
            def _(act):
                norm.scalar(act)
                for t in range(CT):
                    act.wait_ge(w_ready, t + 1)
                    act.activation(w_t[:, t, 0:D], core.bank[t % 2][:], ACT.Copy).then_inc(w_copied, 1)
                    act.activation(w_t[:, t, D:], core.bank[2 + t % 2][:, 0:N], ACT.Copy).then_inc(c_copied, 1)
                act.wait_ge(var_ready, 1)
                act.activation(scal[:, 1:2], scal[:, 0:1], ACT.Sqrt).then_inc(std_ready, 1)
                act.wait_ge(top_ready, 1)
                act.activation(dots[:], dots[:], ACT.Exp, bias=scal[:, 3:4], scale=1.0,
                               accum_out=scal[:, 4:5]).then_inc(exp_ready, 1)

            @block.vector
            def _(dve):
                norm.vector(dve)
                steps = Steps(dve, own)
                dve.wait_ge(loaded, 64)
                for j in range(BG):
                    dve.tensor_scalar(hot[:, j, :], codes_sb[:, j, :], entry_sb[:], None,
                                      ALU.is_equal).then_inc(hot_ready, 1)
                dve.wait_ge(dots_ready, 1)
                steps.then(dve.bn_stats(stats[:], core.bank[4][:, 0:N]))
                steps.then(dve.bn_aggr(mean_var[:], stats[:]))
                dve.tensor_scalar(scal[:, 0:1], mean_var[:, 1:2], 1e-5, None, ALU.add).then_inc(var_ready, 1)
                dve.wait_ge(std_ready, 1)
                steps.then(dve.reciprocal(scal[:, 2:3], scal[:, 1:2]))
                steps.then(dve.tensor_scalar(dots[:], core.bank[4][:, 0:N], mean_var[:, 0:1], scal[:, 2:3],
                                             ALU.subtract, ALU.mult))
                steps.then(dve.tensor_tensor(dots[:], dots[:], bias[:, D:], ALU.mult))
                dve.tensor_reduce(scal[:, 3:4], dots[:], AX.X, ALU.max, negate=True).then_inc(top_ready, 1)
                dve.wait_ge(y_ready, 1)
                steps.then(dve.tensor_tensor(y_sb[:], core.bank[5][:], bias[:, 0:D], ALU.add))
                dve.wait_ge(exp_ready, 1)
                steps.then(dve.reciprocal(scal[:, 5:6], scal[:, 4:5]))
                dve.tensor_scalar(taken[:], dots[:], scal[:, 5:6], 0.5, ALU.mult, ALU.is_gt).then_inc(taken_ready, 1)
                dve.wait_ge(taken_ready, 1)
                steps.then(dve.tensor_reduce(scal[:, 6:7], taken[:], AX.X, ALU.max))
                dve.wait_ge(count_ready, 1)
                steps.then(dve.tensor_scalar(k_mask[:], core.bank[6][:, 0:N], 0.5, scal[:, 6:7], ALU.is_gt,
                                             ALU.mult))
                steps.then(dve.tensor_tensor(y_sb[:].rearrange("p (n o) -> p n o", n=N),
                                             y_sb[:].rearrange("p (n o) -> p n o", n=N),
                                             k_mask[:].unsqueeze(2).to_broadcast([P, N, D // N]), ALU.mult))
                dve.tensor_tensor(core.x[:], core.x[:], y_sb[:], ALU.add)


def feature_cross_attention(core, name, a):
    nc = core.nc
    with Stage(core, name) as st:
        w = st.sb("w", [P, CT, D])
        ctx_sb = st.sb("ctx", [P, KT, D])
        row_sb = st.sb("rows", [P, 5, D])
        w_in = st.sem("w_in")
        ctx_in = st.sem("ctx_in")
        rows_in = st.sem("rows_in")

        def issue(sp):
            sp.dma_start(w[:], a["L1x_w"][:, :, 0:D]).then_inc(w_in, 16)
            sp.dma_start(row_sb[:].rearrange("p r f -> p (r f)"), a["L1x_rows"].to_broadcast([P, 5 * D])).then_inc(rows_in, 16)
            sp.dma_start(ctx_sb[:], a["L1x_ctx"]).then_inc(ctx_in, 16)

        following = yield issue
        if core.keys is None:
            core.keys = ContextKeys(core, a)
            context_keys_alone(core, core.keys)
            core.keys.made()
        keys, k_t, rstd_f = core.keys, core.keys.k_t, core.keys.rstd_f
        norm = LayerNorm(core, st, core.bank[0])
        junk = st.sb("junk", [P, D])
        sumsq_q = st.sb("sumsq_q", [P, 1])
        rstd_q = st.sb("rstd_q", [P, 1])
        q_sb = st.sb("q", [P, D])
        q_t = st.sb("q_t", [P, CT, P])
        s_sb = st.sb("s", [P, SK])
        part_max = st.sb("part_max", [P, NC])
        neg_max = st.sb("neg_max", [P, 1])
        row_sum = st.sb("row_sum", [P, NC])
        r_sum = st.sb("r_sum", [P, 2])
        p_t = st.sb("p_t", [P, KT, P])
        o_sb = st.sb("o", [P, D])
        own = st.sem("own")
        q_proj = st.sem("q_proj")
        q_biased = st.sem("q_biased")
        q_squared = st.sem("q_squared")
        rms_q = st.sem("rms_q")
        q_ready = st.sem("q_ready")
        q_turned = st.sem("q_turned")
        q_t_ready = st.sem("q_t_ready")
        s_ready = st.sem("s_ready")
        max_ready = st.sem("max_ready")
        exp_ready = st.sem("exp_ready")
        p_turned = st.sem("p_turned")
        p_t_dve = st.sem("p_t_dve")
        p_t_act = st.sem("p_t_act")
        o_ready = st.sem("o_ready")
        with nc.Block() as block:
            @block.gpsimd
            def _(pool):
                core.clear_stale(pool)

            @block.sync
            def _(sp):
                following(sp)

            @block.tensor
            def _(pe):
                norm.tensor(pe)
                pe.wait_ge(w_in, 16)
                for c in range(CT):
                    mm = pe.matmul(core.bank[2][:], core.xn_t[:, c, :], w[:, c, :], start=(c == 0),
                                   stop=(c == CT - 1))
                mm.then_inc(q_proj, 1)
                pe.wait_ge(q_ready, 1)
                for c in range(CT):
                    mm = pe.transpose(core.bank[3][:, c * P:(c + 1) * P], q_sb[:, c * P:(c + 1) * P], core.ident[:])
                mm.then_inc(q_turned, 1)
                pe.wait_ge(q_t_ready, 1)
                for j in range(NC):
                    for c in range(CT):
                        mm = pe.matmul(core.bank[4 + j][:].rearrange("p (t k) -> p t k", t=4), q_t[:, c, :],
                                       k_t[:, 4 * j:4 * j + 4, c, :], start=(c == 0), stop=(c == CT - 1))
                    mm.then_inc(s_ready, 1)
                for j in range(NC):
                    pe.wait_ge(exp_ready, j + 1)
                    for i in range(4):
                        kt = 4 * j + i
                        mm = pe.transpose(core.bank[j][:, i * P:(i + 1) * P], s_sb[:, kt * P:(kt + 1) * P],
                                          core.ident[:])
                    mm.then_inc(p_turned, 1)
                pe.wait_ge(ctx_in, 16)
                for kt in range(KT):
                    pe.wait_ge(p_t_dve if kt // 4 % 2 else p_t_act, kt // 8 * 4 + kt % 4 + 1)
                    mm = pe.matmul(core.bank[4][:], p_t[:, kt, :], ctx_sb[:, kt, :], start=(kt == 0),
                                   stop=(kt == KT - 1))
                mm.then_inc(o_ready, 1)

            @block.scalar
            def _(act):
                norm.scalar(act)
                act.wait_ge(q_biased, 1)
                act.activation(junk[:], q_sb[:], ACT.Square, accum_out=sumsq_q[:]).then_inc(q_squared, 1)
                act.wait_ge(q_squared, 1)
                act.activation(rstd_q[:], sumsq_q[:], ACT.Sqrt, bias=core.eps6[:], scale=1.0 / D).then_inc(rms_q, 1)
                act.wait_ge(max_ready, 1)
                for j in range(NC):
                    act.activation(s_sb[:, j * 512:(j + 1) * 512], core.bank[4 + j][:], ACT.Exp, bias=neg_max[:],
                                   scale=1.0, accum_out=row_sum[:, j:j + 1]).then_inc(exp_ready, 1)
                for j in range(0, NC, 2):
                    act.wait_ge(p_turned, j + 1)
                    for kt in range(4 * j, 4 * j + 4):
                        act.activation(p_t[:, kt, :], core.bank[j][:, (kt % 4) * P:(kt % 4 + 1) * P],
                                       ACT.Copy, scale=rstd_f[:, kt:kt + 1]).then_inc(p_t_act, 1)

            @block.vector
            def _(dve):
                norm.vector(dve)
                steps = Steps(dve, own)
                dve.wait_ge(rows_in, 16)
                steps.then(dve.scalar_tensor_tensor(row_sb[:, 2, :], row_sb[:, 2, :], float(D ** -0.5),
                                                    row_sb[:, 3, :], ALU.mult, ALU.mult))
                dve.wait_ge(q_proj, 1)
                dve.tensor_tensor(q_sb[:], core.bank[2][:], row_sb[:, 0, :], ALU.add).then_inc(q_biased, 1)
                dve.wait_ge(rms_q, 1)
                steps.then(dve.reciprocal(rstd_q[:], rstd_q[:]))
                dve.scalar_tensor_tensor(q_sb[:], q_sb[:], rstd_q[:], row_sb[:, 2, :], ALU.mult,
                                         ALU.mult).then_inc(q_ready, 1)
                dve.wait_ge(q_turned, 1)
                dve.tensor_copy(q_t[:], core.bank[3][:].rearrange("p (c q) -> p c q", c=CT)).then_inc(q_t_ready, 1)
                for j in range(NC):
                    dve.wait_ge(s_ready, j + 1)
                    steps.then(dve.tensor_reduce(part_max[:, j:j + 1], core.bank[4 + j][:], AX.X, ALU.max))
                dve.tensor_reduce(neg_max[:], part_max[:], AX.X, ALU.max, negate=True).then_inc(max_ready, 1)
                for j in range(1, NC, 2):
                    dve.wait_ge(p_turned, j + 1)
                    for kt in range(4 * j, 4 * j + 4):
                        dve.tensor_scalar(p_t[:, kt, :], core.bank[j][:, (kt % 4) * P:(kt % 4 + 1) * P],
                                          rstd_f[:, kt:kt + 1], None, ALU.mult).then_inc(p_t_dve, 1)
                dve.wait_ge(exp_ready, NC)
                steps.then(dve.tensor_reduce(r_sum[:, 0:1], row_sum[:], AX.X, ALU.add))
                steps.then(dve.reciprocal(r_sum[:, 1:2], r_sum[:, 0:1]))
                dve.wait_ge(o_ready, 1)
                steps.then(dve.scalar_tensor_tensor(o_sb[:], core.bank[4][:], r_sum[:, 1:2], row_sb[:, 4, :],
                                                    ALU.mult, ALU.mult))
                dve.tensor_tensor(core.x[:], core.x[:], o_sb[:], ALU.add)
    core.end_with_last(keys.st)
    core.keys = None


def narrow_cross_attention(core, name, w_dram, w_out, mask_u8, group_cols):
    nc = core.nc
    E = 16
    with Stage(core, name) as st:
        w = st.sb("w", [P, CT, 2 * P + D])
        w_o = st.sb("w_o", [P, CT, D])
        mask_b = st.sb("mask_b", [P, SK], U8)
        groups = st.sb("groups", [P, NG])
        w_in = st.sem("w_in")
        mask_in = st.sem("mask_in")

        def issue(sp):
            sp.dma_start(w[:], w_dram).then_inc(w_in, 16)
            sp.dma_start(mask_b[:], mask_u8).then_inc(mask_in, 16)
            sp.dma_start(groups[:], group_cols).then_inc(mask_in, 16)
            sp.dma_start(w_o[:], w_out).then_inc(w_in, 16)

        following = yield issue
        norm = LayerNorm(core, st, core.bank[0])
        mask_sb = st.sb("mask", [P, SK])
        k_t = st.sb("k_t", [P, SK])
        v_sb = st.sb("v", [P, KT, P])
        q_t = st.sb("q_t", [P, HG, P])
        q_own = st.sb("q_own", [P, HG, P])
        s_sb = st.sb("s", [P, HG, SK])
        p_t = st.sb("p_t", [P, 4, HG * P])
        part_max = st.sb("part_max", [P, HG, NC])
        neg_max = st.sb("neg_max", [P, HG])
        row_sum = st.sb("row_sum", [P, HG])
        r_sum = st.sb("r_sum", [P, HG])
        diag = st.sb("diag", [P, HG, P])
        o_raw = st.sb("o_raw", [P, HG * P])
        o_t = st.sb("o_t", [P, HG, P])
        mask_ready = st.sem("mask_ready")
        proj_ready = st.sem("proj_ready")
        kq_copied = st.sem("kq_copied")
        v_copied = st.sem("v_copied")
        q_own_ready = st.sem("q_own_ready")
        s_ready = st.sem("s_ready")
        s_seen = st.sem("s_seen")
        s_read = st.sem("s_read")
        max_ready = st.sem("max_ready")
        exp_ready = st.sem("exp_ready")
        turned = st.sem("turned")
        pt_dve = st.sem("pt_dve")
        pt_act = st.sem("pt_act")
        pv_done = st.sem("pv_done")
        recip_ready = st.sem("recip_ready")
        diag_ready = st.sem("diag_ready")
        rinv_ready = st.sem("rinv_ready")
        o_raw_ready = st.sem("o_raw_ready")
        o_scaled = st.sem("o_scaled")
        o_added = st.sem("o_added")
        out_ready = st.sem("out_ready")
        out_bank = core.bank[7]
        ring_bank = lambda n: core.bank[3 + n % 4]
        with nc.Block() as block:
            @block.gpsimd
            def _(pool):
                core.clear_stale(pool)

            @block.sync
            def _(sp):
                following(sp)

            @block.tensor
            def _(pe):
                norm.tensor(pe)
                pe.wait_ge(w_in, 32)
                for n in range(9):
                    if n >= 3:
                        if n - 3 <= NC:
                            pe.wait_ge(kq_copied, n - 2)
                        else:
                            pe.wait_ge(v_copied, n - 3 - NC)
                    out = core.bank[n % 3]
                    if n < NC:
                        for c in range(CT):
                            mm = pe.matmul(out[:], w[:, c, 0:P], core.ctx_t[:, c, n * 512:(n + 1) * 512],
                                           start=(c == 0), stop=(c == CT - 1))
                    elif n == NC:
                        for h in range(HG):
                            for c in range(CT):
                                mm = pe.matmul(out[:, h * P:(h + 1) * P],
                                               w[:, c, 2 * P + h * P:2 * P + (h + 1) * P], core.xn_t[:, c, :],
                                               start=(c == 0), stop=(c == CT - 1))
                    else:
                        for j in range(4):
                            kt = 4 * (n - NC - 1) + j
                            for c in range(CT):
                                mm = pe.matmul(out[:, j * P:(j + 1) * P], core.ctx_t[:, c, kt * P:(kt + 1) * P],
                                               w[:, c, P:2 * P], start=(c == 0), stop=(c == CT - 1))
                    mm.then_inc(proj_ready, 1)
                pe.wait_ge(kq_copied, NC + 1)
                pe.wait_ge(v_copied, 4)
                with pe.Fori(0, NG) as g:
                    pe.wait_ge(q_own_ready, g + 1)
                    for h in range(HG):
                        for c in range(NC):
                            n = h * NC + c
                            if n < 4:
                                pe.wait_ge(pt_dve, g * 8 + 1)
                                pe.wait_ge(pt_act, g * 8 + 1)
                            else:
                                pe.wait_ge(s_read, g * 16 + n - 3)
                            pe.matmul(ring_bank(n)[:], q_own[:, h, :], k_t[:, c * 512:(c + 1) * 512],
                                      start=True, stop=True).then_inc(s_ready, 1)

                    def turn(kt):
                        if kt < 4:
                            pe.wait_ge(s_read, g * 16 + 16)
                            pe.wait_ge(exp_ready, g * 4 + 4)
                        else:
                            pe.wait_ge((pt_act if kt % 2 else pt_dve), g * 8 + (kt - 4) // 2 + 2)
                        for h in range(HG):
                            mm = pe.transpose(ring_bank(kt)[:, h * P:(h + 1) * P],
                                              s_sb[:, h, kt * P:(kt + 1) * P], core.ident[:])
                        mm.then_inc(turned, 1)

                    def weigh(kt):
                        pe.wait_ge((pt_act if kt % 2 else pt_dve), g * 8 + kt // 2 + 2)
                        if kt == 0:
                            pe.wait_ge(o_raw_ready, g + 1)
                        pe.matmul(out_bank[:], v_sb[:, kt, :], p_t[:, kt % 4, :], start=(kt == 0),
                                  stop=(kt == KT - 1)).then_inc(pv_done, 1)

                    for kt in range(KT + 2):
                        if kt < KT:
                            turn(kt)
                        if kt >= 2:
                            weigh(kt - 2)
                    pe.wait_ge(diag_ready, g * 4 + 4)
                    pe.wait_ge(o_added, g + 1)
                    pe.matmul(core.bank[0][:], core.ones[:], diag[:].rearrange("p h q -> p (h q)"),
                              start=True, stop=True).then_inc(rinv_ready, 1)
                pe.wait_ge(o_added, NG + 1)
                for h in range(HG):
                    mm = pe.matmul(core.bank[1][:], o_t[:, h, :], w_o[:, h, :], start=(h == 0), stop=(h == HG - 1))
                mm.then_inc(out_ready, 1)

            @block.scalar
            def _(act):
                norm.scalar(act)
                for one_ahead in (pt_act, o_raw_ready):
                    act.sem_inc(one_ahead, 1)
                for n in range(9):
                    act.wait_ge(proj_ready, n + 1)
                    if n < NC:
                        act.activation(k_t[:, n * 512:(n + 1) * 512], core.bank[n % 3][:], ACT.Copy).then_inc(kq_copied, 1)
                    elif n == NC:
                        act.activation(q_t[:], core.bank[n % 3][:].rearrange("p (h q) -> p h q", h=HG), ACT.Copy,
                                       scale=float(E ** -0.5)).then_inc(kq_copied, 1)
                    else:
                        j = n - NC - 1
                        act.activation(v_sb[:, 4 * j:4 * j + 4, :],
                                       core.bank[n % 3][:].rearrange("p (k d) -> p k d", k=4),
                                       ACT.Copy).then_inc(v_copied, 1)
                with act.Fori(0, NG) as g:
                    for h in range(HG):
                        act.wait_ge(max_ready, g * 4 + h + 1)
                        act.activation(s_sb[:, h, :], s_sb[:, h, :], ACT.Exp, bias=neg_max[:, h:h + 1],
                                       scale=1.0, accum_out=row_sum[:, h:h + 1]).then_inc(exp_ready, 1)
                    for kt in range(1, KT, 2):
                        act.wait_ge(turned, g * 16 + kt + 1)
                        if kt >= 4:
                            act.wait_ge(pv_done, g * 16 + kt - 3)
                        act.activation(p_t[:, kt % 4, :], ring_bank(kt)[:], ACT.Copy).then_inc(pt_act, 1)
                    act.wait_ge(pv_done, g * 16 + 16)
                    act.wait_ge(o_added, g + 1)
                    act.activation(o_raw[:], out_bank[:], ACT.Copy,
                                   scale=groups[:, bass.ds(g, 1)]).then_inc(o_raw_ready, 1)

            @block.vector
            def _(dve):
                norm.vector(dve)
                for one_ahead in (o_added, pt_dve):
                    dve.sem_inc(one_ahead, 1)
                dve.memset(o_t[:], 0.0)
                dve.wait_ge(mask_in, 32)
                dve.tensor_scalar(mask_sb[:], mask_b[:], 1.0, -LOWEST, ALU.subtract, ALU.mult).then_inc(mask_ready, 1)
                dve.wait_ge(mask_ready, 1)
                dve.wait_ge(kq_copied, NC + 1)
                with dve.Fori(0, NG) as g:
                    dve.tensor_scalar(q_own[:].rearrange("p h q -> p (h q)"), q_t[:].rearrange("p h q -> p (h q)"),
                                      groups[:, bass.ds(g, 1)], None, ALU.mult).then_inc(q_own_ready, 1)
                    for h in range(HG):
                        for c in range(NC):
                            n = h * NC + c
                            dve.wait_ge(s_ready, g * 16 + n + 1)
                            dve.sem_inc(s_seen, 1)
                            dve.tensor_tensor_reduce(
                                s_sb[:, h, c * 512:(c + 1) * 512], ring_bank(n)[:],
                                mask_sb[:, c * 512:(c + 1) * 512], 1.0, LOWEST, ALU.add, ALU.max,
                                part_max[:, h, c:c + 1]).then_inc(s_read, 1)
                        dve.wait_ge(s_read, g * 16 + h * NC + NC)
                        dve.tensor_reduce(neg_max[:, h:h + 1], part_max[:, h, :], AX.X, ALU.max,
                                          negate=True).then_inc(max_ready, 1)
                    for kt in range(0, KT, 2):
                        dve.wait_ge(turned, g * 16 + kt + 1)
                        if kt >= 4:
                            dve.wait_ge(pv_done, g * 16 + kt - 3)
                        dve.tensor_copy(p_t[:, kt % 4, :], ring_bank(kt)[:]).then_inc(pt_dve, 1)
                        if kt == 4:
                            dve.wait_ge(exp_ready, g * 4 + 4)
                            dve.reciprocal(r_sum[:], row_sum[:]).then_inc(recip_ready, 1)
                            dve.wait_ge(recip_ready, g + 1)
                            for h in range(HG):
                                dve.tensor_scalar(diag[:, h, :], core.ident[:], r_sum[:, h:h + 1], None,
                                                  ALU.mult).then_inc(diag_ready, 1)
                    dve.wait_ge(o_raw_ready, g + 2)
                    dve.wait_ge(rinv_ready, g + 1)
                    dve.tensor_tensor(o_raw[:], o_raw[:], core.bank[0][:], ALU.mult).then_inc(o_scaled, 1)
                    dve.wait_ge(o_scaled, g + 1)
                    flat = o_t[:].rearrange("p h q -> p (h q)")
                    dve.tensor_tensor(flat, flat, o_raw[:], ALU.add).then_inc(o_added, 1)
                dve.wait_ge(out_ready, 1)
                dve.tensor_tensor(core.x[:], core.x[:], core.bank[1][:], ALU.add)


def latent_attention(core, name, a, causal, eps_inside):
    nc = core.nc
    QR, KR, RD = 192, 64, 64
    LO = QR - P
    PE_W = HG * RD
    SCALE = float((HD + RD) ** -0.5)
    with Stage(core, name) as st:
        w_a = st.sb("w_a", [P, CT, QR + KR + RD])
        row_sb = st.sb("rows", [P, QR + KR])
        rot = st.sb("rot", [P, 2, RD])
        masked = st.sb("mask", [P, P])
        w_hi = [st.sb(f"w_hi{b}", [P, HG * HD + PE_W]) for b in range(2)]
        w_lo = [st.sb(f"w_lo{b}", [LO, HG * HD + PE_W + 2 * HG * HD]) for b in range(2)]
        w_o = [st.sb(f"w_o{b}", [P, HG, D]) for b in range(2)]
        w_a_in = st.sem("w_a_in")
        rows_in = st.sem("rows_in")
        w_in = [st.sem(f"w_in{b}") for b in range(2)]
        o_in = [st.sem(f"o_in{b}") for b in range(2)]

        def issue(sp):
            sp.dma_start(w_a[:], a["w_a"]).then_inc(w_a_in, 16)
            sp.dma_start(row_sb[:], a["rows"].to_broadcast([P, QR + KR])).then_inc(rows_in, 16)
            sp.dma_start(rot[:], a["rot"]).then_inc(rows_in, 16)
            sp.dma_start(masked[:], a["causal"]).then_inc(rows_in, 16)
            for b in range(2):
                sp.dma_start(w_hi[b][:], a["hi"][b]).then_inc(w_in[b], 16)
                sp.dma_start(w_lo[b][:], a["lo"][b]).then_inc(w_in[b], 16)
                sp.dma_start(w_o[b][:], a["o"][b]).then_inc(o_in[b], 16)

        following = yield issue
        norm = LayerNorm(core, st, core.bank[0])
        junk = st.sb("junk", [P, QR])
        sumsq = st.sb("sumsq", [P, 2])
        rstd = st.sb("rstd", [P, 2])
        lat = st.sb("lat", [P, QR + KR])
        k_pe = st.sb("k_pe", [P, RD])
        k_sw = st.sb("k_sw", [P, RD])
        lat_hi = st.sb("lat_hi", [P, P])
        lat_lo = st.sb("lat_lo", [LO, 3, P])
        q_t = st.sb("q_t", [P, HG, P])
        k_t = st.sb("k_t", [P, HG, P])
        v_sb = [st.sb(f"v{b}", [P, HG, HD]) for b in range(2)]
        q_pe = st.sb("q_pe", [P, HG, RD])
        q_sw = st.sb("q_sw", [P, HG, RD])
        q_pe_t = st.sb("q_pe_t", [RD, HG, P])
        s_sb = [st.sb(f"s{b}", [P, HG, P]) for b in range(2)]
        neg_max = st.sb("neg_max", [P, HG])
        row_sum = st.sb("row_sum", [P, HG])
        r_sum = st.sb("r_sum", [P, HG])
        p_t = st.sb("p_t", [P, HG, P])
        o_t = st.sb("o_t", [P, HG, P])
        own = st.sem("own")
        rows_scaled = st.sem("rows_scaled")
        lat_proj = st.sem("lat_proj")
        squared = st.sem("squared")
        rms_ready = st.sem("rms_ready")
        lat_ready = st.sem("lat_ready")
        lat_turned = st.sem("lat_turned")
        lat_t_ready = st.sem("lat_t_ready")
        q_proj = st.sem("q_proj")
        k_proj = st.sem("k_proj")
        v_proj = st.sem("v_proj")
        pe_proj = st.sem("pe_proj")
        q_copied = st.sem("q_copied")
        v_copied = st.sem("v_copied")
        k_copied = st.sem("k_copied")
        pe_read = st.sem("pe_read")
        pe_ready = st.sem("pe_ready")
        pe_turned = st.sem("pe_turned")
        pe_copied = st.sem("pe_copied")
        s_ready = st.sem("s_ready")
        s_masked = st.sem("s_masked")
        max_ready = st.sem("max_ready")
        exp_ready = st.sem("exp_ready")
        recip_ready = st.sem("recip_ready")
        p_ready = st.sem("p_ready")
        p_turned = st.sem("p_turned")
        p_t_ready = st.sem("p_t_ready")
        o_ready = st.sem("o_ready")
        o_t_ready = st.sem("o_t_ready")
        wo_done = st.sem("wo_done")
        x_added = st.sem("x_added")
        banks = core.bank
        per_head = lambda bank: bank[:].rearrange("p (h q) -> p h q", h=HG)

        with nc.Block() as block:
            @block.gpsimd
            def _(pool):
                core.clear_stale(pool)

            @block.sync
            def _(sp):
                following(sp)
                def load_projections(n, b):
                    sp.wait_ge(v_proj, n - 1)
                    sp.dma_start(w_hi[b][:], a["hi"][n]).then_inc(w_in[b], 16)
                    sp.dma_start(w_lo[b][:], a["lo"][n]).then_inc(w_in[b], 16)

                def load_output(n, b):
                    sp.wait_ge(wo_done, n - 1)
                    sp.dma_start(w_o[b][:], a["o"][n]).then_inc(o_in[b], 16)

                load_projections(2, 0)
                load_projections(3, 1)
                with sp.Fori(0, NG // 2 - 2) as i:
                    for b in range(2):
                        load_output(i * 2 + (2 + b), b)
                        load_projections(i * 2 + (4 + b), b)
                load_output(NG - 2, 0)
                load_output(NG - 1, 1)

            @block.tensor
            def _(pe):
                norm.tensor(pe)
                pe.wait_ge(w_a_in, 16)
                for c in range(CT):
                    mm = pe.matmul(banks[0][:, 0:QR + KR + RD], core.xn_t[:, c, :], w_a[:, c, :], start=(c == 0),
                                   stop=(c == CT - 1))
                mm.then_inc(lat_proj, 1)
                pe.wait_ge(lat_ready, 1)
                pe.transpose(banks[1][:, 0:P], lat[:, 0:P], core.ident[:])
                pe.transpose(banks[1][0:LO, P:2 * P], lat[:, P:QR], core.ident[:])
                pe.transpose(banks[1][0:KR, 2 * P:3 * P], lat[:, QR:], core.ident[:])
                pe.transpose(banks[1][0:RD, 3 * P:4 * P], k_pe[:], core.ident[:]).then_inc(lat_turned, 1)
                pe.wait_ge(lat_t_ready, 2)

                KO = HG * HD + PE_W

                def project(g, b, i):
                    pe.wait_ge(w_in[b], i * 32 + 32)
                    pe.wait_ge(pe_read, g + 1)
                    pe.matmul(banks[3][:, 0:PE_W], lat_hi[:], w_hi[b][:, HG * HD:], start=True, stop=False)
                    pe.matmul(banks[3][:, 0:PE_W], lat_lo[:, 0, :], w_lo[b][:, HG * HD:KO], start=False,
                              stop=True).then_inc(pe_proj, 1)
                    pe.wait_ge(q_copied, g + 1)
                    for h in range(HG):
                        pe.matmul(banks[0][:, h * P:(h + 1) * P], w_hi[b][:, h * HD:(h + 1) * HD], lat_hi[:],
                                  start=True, stop=False)
                        mm = pe.matmul(banks[0][:, h * P:(h + 1) * P], w_lo[b][:, h * HD:(h + 1) * HD],
                                       lat_lo[:, 0, :], start=False, stop=True)
                    mm.then_inc(q_proj, 1)
                    pe.wait_ge(k_copied, g + 1)
                    for h in range(HG):
                        mm = pe.matmul(banks[1][:, h * P:(h + 1) * P], w_lo[b][:, KO + h * HD:KO + (h + 1) * HD],
                                       lat_lo[:, 1, :], start=True, stop=True)
                    mm.then_inc(k_proj, 1)
                    pe.wait_ge(v_copied, g + 1)
                    pe.matmul(banks[2][:], lat_lo[:, 1, :], w_lo[b][:, KO + HG * HD:], start=True,
                              stop=True).then_inc(v_proj, 1)

                def turn_rotary(g):
                    pe.wait_ge(pe_ready, g + 1)
                    pe.wait_ge(pe_copied, g + 1)
                    for j in range(HG // 2):
                        mm = pe.transpose(banks[4][:, j * P:(j + 1) * P],
                                          q_pe[:, 2 * j:2 * j + 2, :].rearrange("p h e -> p (h e)"),
                                          core.ident[:])
                    mm.then_inc(pe_turned, 1)

                def score(g):
                    pe.wait_ge(q_copied, g + 2)
                    pe.wait_ge(k_copied, g + 2)
                    pe.wait_ge(pe_copied, g + 2)
                    pe.wait_ge(s_masked, g + 1)
                    for h in range(HG):
                        pe.matmul(banks[5][:, h * P:(h + 1) * P], q_t[:, h, :], k_t[:, h, :], start=True, stop=False)
                        mm = pe.matmul(banks[5][:, h * P:(h + 1) * P], q_pe_t[:, h, :], lat_lo[:, 2, :],
                                       start=False, stop=True)
                    mm.then_inc(s_ready, 1)

                def turn_probabilities(g, b):
                    pe.wait_ge(p_ready, g + 1)
                    pe.wait_ge(x_added, g + 1)
                    for h in range(HG):
                        mm = pe.transpose(banks[6][:, h * P:(h + 1) * P], s_sb[b][:, h, :], core.ident[:])
                    mm.then_inc(p_turned, 1)

                def weigh(g, b):
                    pe.wait_ge(p_t_ready, g + 1)
                    pe.wait_ge(v_copied, g + 2)
                    pe.wait_ge(o_t_ready, g + 1)
                    for h in range(HG):
                        mm = pe.matmul(banks[7][:, h * P:(h + 1) * P], v_sb[b][:, h, :], p_t[:, h, :], start=True,
                                       stop=True)
                    mm.then_inc(o_ready, 1)

                def project_out(g, b, i):
                    pe.wait_ge(o_t_ready, g + 2)
                    pe.wait_ge(o_in[b], i * 16 + 16)
                    for h in range(HG):
                        mm = pe.matmul(banks[6][:], o_t[:, h, :], w_o[b][:, h, :], start=(h == 0),
                                       stop=(h == HG - 1))
                    mm.then_inc(wo_done, 1)

                def step(g, b, i, before=True, this=True, after=True):
                    prev_i, next_i = (i, i + 1) if b else (i - 1, i)
                    if this:
                        score(g)
                    if before:
                        turn_probabilities(g - 1, 1 - b)
                    if after:
                        project(g + 1, 1 - b, next_i)
                    if before:
                        weigh(g - 1, 1 - b)
                    if after:
                        turn_rotary(g + 1)
                    if before:
                        project_out(g - 1, 1 - b, prev_i)

                project(0, 0, 0)
                turn_rotary(0)
                step(0, 0, 0, before=False)
                with pe.Fori(0, NG // 2 - 1) as i:
                    step(i * 2 + 1, 1, i)
                    step(i * 2 + 2, 0, i + 1)
                step(NG - 1, 1, NG // 2 - 1, after=False)
                step(NG, 0, NG // 2, this=False, after=False)

            @block.scalar
            def _(act):
                norm.scalar(act)
                for one_ahead in (q_copied, v_copied, o_t_ready):
                    act.sem_inc(one_ahead, 1)
                act.wait_ge(lat_proj, 1)
                act.activation(junk[:], banks[0][:, 0:QR], ACT.Square, accum_out=sumsq[:, 0:1]).then_inc(squared, 1)
                act.wait_ge(squared, 1)
                act.activation(junk[:, 0:KR], banks[0][:, QR:QR + KR], ACT.Square,
                               accum_out=sumsq[:, 1:2]).then_inc(squared, 1)
                act.wait_ge(squared, 2)
                bias = core.eps5[:] if eps_inside else core.zero[:]
                act.activation(rstd[:, 0:1], sumsq[:, 0:1], ACT.Sqrt, bias=bias, scale=1.0 / QR).then_inc(rms_ready, 1)
                act.activation(rstd[:, 1:2], sumsq[:, 1:2], ACT.Sqrt, bias=bias, scale=1.0 / KR).then_inc(rms_ready, 1)

                def keep_q(g):
                    act.wait_ge(q_proj, g + 1)
                    if not (isinstance(g, int) and g == 0):
                        act.wait_ge(s_ready, g)
                    act.activation(q_t[:], per_head(banks[0]), ACT.Copy).then_inc(q_copied, 1)

                def keep_v(g, b, used=True):
                    act.wait_ge(v_proj, g + 1)
                    if used:
                        act.wait_ge(o_ready, g - 1)
                    act.activation(v_sb[b][:], per_head(banks[2]), ACT.Copy).then_inc(v_copied, 1)

                def step(g, b, before=True, this=True, after=True):
                    if before:
                        act.wait_ge(p_turned, g)
                        act.activation(p_t[:], per_head(banks[6]), ACT.Copy).then_inc(p_t_ready, 1)
                    if this:
                        act.wait_ge(max_ready, g + 1)
                        for h in range(HG):
                            act.activation(s_sb[b][:, h, :], s_sb[b][:, h, :], ACT.Exp, bias=neg_max[:, h:h + 1],
                                           scale=1.0, accum_out=row_sum[:, h:h + 1]).then_inc(exp_ready, 1)
                    if after:
                        keep_q(g + 1)
                    if before:
                        act.wait_ge(o_ready, g)
                        act.activation(o_t[:], per_head(banks[7]), ACT.Copy).then_inc(o_t_ready, 1)
                    if after:
                        keep_v(g + 1, 1 - b, used=before)

                keep_q(0)
                keep_v(0, 0, used=False)
                step(0, 0, before=False)
                with act.Fori(0, NG // 2 - 1) as i:
                    step(i * 2 + 1, 1)
                    step(i * 2 + 2, 0)
                step(NG - 1, 1, after=False)
                step(NG, 0, this=False, after=False)

            @block.vector
            def _(dve):
                norm.vector(dve)
                for one_ahead in (k_copied, pe_read, pe_copied, s_masked, x_added):
                    dve.sem_inc(one_ahead, 1)
                steps = Steps(dve, own)
                dve.wait_ge(rows_in, 48)
                dve.tensor_scalar(row_sb[:, 0:QR], row_sb[:, 0:QR], SCALE, None, ALU.mult).then_inc(rows_scaled, 1)
                dve.wait_ge(rms_ready, 2)
                if not eps_inside:
                    steps.then(dve.tensor_scalar(rstd[:], rstd[:], 1e-6, None, ALU.add))
                steps.then(dve.reciprocal(rstd[:], rstd[:]))
                dve.wait_ge(rows_scaled, 1)
                steps.then(dve.scalar_tensor_tensor(lat[:, 0:QR], banks[0][:, 0:QR], rstd[:, 0:1], row_sb[:, 0:QR],
                                                    ALU.mult, ALU.mult))
                steps.then(dve.scalar_tensor_tensor(lat[:, QR:], banks[0][:, QR:QR + KR], rstd[:, 1:2],
                                                    row_sb[:, QR:], ALU.mult, ALU.mult))
                half = RD // 2
                src = banks[0][:, QR + KR:QR + KR + RD]
                steps.then(dve.tensor_tensor(k_pe[:], src, rot[:, 0, :], ALU.mult))
                steps.then(dve.tensor_tensor(k_sw[:, 0:half], src[:, half:], rot[:, 1, 0:half], ALU.mult))
                steps.then(dve.tensor_tensor(k_sw[:, half:], src[:, 0:half], rot[:, 1, half:], ALU.mult))
                dve.tensor_tensor(k_pe[:], k_pe[:], k_sw[:], ALU.add).then_inc(lat_ready, 1)
                dve.wait_ge(lat_turned, 1)
                dve.tensor_copy(lat_hi[:], banks[1][:, 0:P]).then_inc(lat_t_ready, 1)
                dve.tensor_copy(lat_lo[:], banks[1][0:LO, P:].rearrange("p (t q) -> p t q", t=3)).then_inc(lat_t_ready, 1)

                def keep(g):
                    dve.wait_ge(pe_proj, g + 1)
                    if not (isinstance(g, int) and g == 0):
                        dve.wait_ge(pe_turned, g)
                    src = banks[3][:, 0:PE_W].rearrange("p (h e) -> p h e", h=HG)
                    wide, thin = [P, HG, RD], [P, HG, half]
                    cos = rot[:, 0, :].unsqueeze(1).to_broadcast(wide)
                    lo = rot[:, 1, 0:half].unsqueeze(1).to_broadcast(thin)
                    hi = rot[:, 1, half:].unsqueeze(1).to_broadcast(thin)
                    dve.tensor_tensor(q_pe[:], src, cos, ALU.mult)
                    dve.tensor_tensor(q_sw[:, :, 0:half], src[:, :, half:], lo, ALU.mult)
                    dve.tensor_tensor(q_sw[:, :, half:], src[:, :, 0:half], hi, ALU.mult).then_inc(pe_read, 1)
                    dve.wait_ge(pe_read, g + 2)
                    dve.tensor_tensor(q_pe[:], q_pe[:], q_sw[:], ALU.add).then_inc(pe_ready, 1)
                    dve.wait_ge(k_proj, g + 1)
                    if not (isinstance(g, int) and g == 0):
                        dve.wait_ge(s_ready, g)
                    dve.tensor_copy(k_t[:], per_head(banks[1])).then_inc(k_copied, 1)

                def turn_rotary(g):
                    dve.wait_ge(pe_turned, g + 1)
                    if not (isinstance(g, int) and g == 0):
                        dve.wait_ge(s_ready, g)
                    for odd in range(2):
                        copy = dve.tensor_copy(
                            q_pe_t[:, odd:HG:2, :],
                            banks[4][odd * RD:(odd + 1) * RD, 0:2 * P].rearrange("p (h q) -> p h q", h=HG // 2))
                    copy.then_inc(pe_copied, 1)

                def step(g, b, before=True, this=True, after=True):
                    if this:
                        dve.wait_ge(s_ready, g + 1)
                        if causal:
                            dve.tensor_tensor(s_sb[b][:], per_head(banks[5]),
                                              masked[:].unsqueeze(1).to_broadcast([P, HG, P]),
                                              ALU.add).then_inc(s_masked, 1)
                        else:
                            dve.tensor_copy(s_sb[b][:], per_head(banks[5])).then_inc(s_masked, 1)
                        dve.wait_ge(s_masked, g + 2)
                        dve.tensor_reduce(neg_max[:], s_sb[b][:], AX.X, ALU.max, negate=True).then_inc(max_ready, 1)
                    if after:
                        keep(g + 1)
                    if this:
                        dve.wait_ge(exp_ready, g * 4 + 4)
                        dve.reciprocal(r_sum[:], row_sum[:]).then_inc(recip_ready, 1)
                        dve.wait_ge(recip_ready, g + 1)
                        dve.tensor_tensor(s_sb[b][:], s_sb[b][:], r_sum[:].unsqueeze(2).to_broadcast([P, HG, P]),
                                          ALU.mult).then_inc(p_ready, 1)
                    if after:
                        turn_rotary(g + 1)
                    if before:
                        dve.wait_ge(wo_done, g)
                        dve.tensor_tensor(core.x[:], core.x[:], banks[6][:], ALU.add).then_inc(x_added, 1)

                keep(0)
                turn_rotary(0)
                step(0, 0, before=False)
                with dve.Fori(0, NG // 2 - 1) as i:
                    step(i * 2 + 1, 1)
                    step(i * 2 + 2, 0)
                step(NG - 1, 1, after=False)
                step(NG, 0, this=False, after=False)


def latent_inputs(a, name):
    return {"w_a": a[f"{name}_w"], "rows": a[f"{name}_rows"], "rot": a["latent_rot"], "causal": a["causal"],
            "hi": a[f"{name}_hi"], "lo": a[f"{name}_lo"], "o": a[f"{name}_o"]}


STAGE_OF = {
    "L0x": lambda core, name, a: wide_cross_attention(
        core, name, a["L0x_kqv"], a["L0x_o"], a["L0x_mask"],
        rotary=(a["L0x_cos"], a["L0x_sin"], a["L0x_cos_q"], a["L0x_sin_q"])),
    "L0a": lambda core, name, a: per_token_head_attention(core, name, a["L0a_w"], a["L0a_rows"], a),
    "L0f": lambda core, name, a: adapter_ffn(core, name, a["L0f_w"], a["L0f_rows"], a["L0f_up"], 3, 16,
                                             starts=a["L0f_starts"], clamp_iota=a["iota8"][:, 0:3]),
    "L1f": lambda core, name, a: adapter_ffn(core, name, a["L1f_w"], a["L1f_rows"], a["L1f_up"], 8, 16,
                                             gate=True, clamp_iota=a["iota8"]),
    "L1x": lambda core, name, a: feature_cross_attention(core, name, a),
    "L1a": lambda core, name, a: latent_attention(core, name, latent_inputs(a, "L1a"), True, True),
    "L2x": lambda core, name, a: narrow_cross_attention(core, name, a["L2x_w"], a["L2x_o"], a["L2x_mask"],
                                                        a["L2x_groups"]),
    "L2a": lambda core, name, a: latent_attention(core, name, latent_inputs(a, "L2a"), False, False),
    "L2f": lambda core, name, a: mixed_adapter_ffn(core, name, a["L2f_w"], a["L2f_keys"], a["L2f_up"]),
    "L3a": lambda core, name, a: single_head_attention(core, name, a["L3a_w"], a["L3a_o"], a["L3a_cols"],
                                                       a["L3a_rows"]),
    "L3f": lambda core, name, a: codebook_ffn(core, name, a["L3f_books"], a["L3f_codes"], a["L3f_entry"],
                                              a["L3f_rows"]),
    "L3x": lambda core, name, a: wide_cross_attention(
        core, name, a["L3x_kqv"], a["L3x_o"], a["L3x_mask"], norm_cols=a["L3x_cols"]),
}
STAGES = ("L0x", "L0a", "L0f", "L1x", "L1a", "L1f", "L2x", "L2a", "L2f", "L3x", "L3a", "L3f")


def load_start(core, a, following):
    nc = core.nc
    with Stage(core, "start") as st:
        loaded = st.sem("loaded")
        with nc.Block() as block:
            @block.sync
            def _(sp):
                sp.dma_start(core.x[:], a["x"]).then_inc(loaded, 16)
                sp.dma_start(core.ident[:], a["ident"]).then_inc(loaded, 16)
                sp.dma_start(core.ctx_t[:], a["ctx_t"]).then_inc(loaded, 16)
                following(sp)
                sp.wait_ge(loaded, 48)

            @block.gpsimd
            def _(pool):
                pool.memset(core.ones[:], 1.0)
                pool.memset(core.zero[:], 0.0)
                pool.memset(core.eps5[:], 1e-5)
                pool.memset(core.eps6[:], 1e-6)


def store_result(core, out):
    nc = core.nc
    with Stage(core, "end") as st:
        stored = st.sem("stored")
        with nc.Block() as block:
            @block.gpsimd
            def _(pool):
                core.clear_stale(pool)

            @block.sync
            def _(sp):
                sp.dma_start(out, core.x[:]).then_inc(stored, 16)
                sp.wait_ge(stored, 16)

        with nc.Block() as block:
            @block.gpsimd
            def _(pool):
                pool.sem_clear(stored)


def perceiver(nc, a, out, stages=STAGES):
    with ExitStack() as ctx:
        core = Core(nc, ctx)
        stage = STAGE_OF[stages[0]](core, stages[0], a)
        load_start(core, a, next(stage))
        for name in (*stages[1:], None):
            coming = STAGE_OF[name](core, name, a) if name else None
            following = next(coming) if coming else (lambda sp: None)
            try:
                stage.send(following)
            except StopIteration:
                pass
            stage = coming
        store_result(core, out)
        core.freed.close()


def by_feature(w):
    return w.reshape(CT, P, -1).transpose(1, 0, 2)


def grouped(w_q, w_k, w_v, w_o):
    per_group = []
    for g in range(NG):
        cols = [w_k[:, g * HD:(g + 1) * HD], w_q[:, g * HG * HD:(g + 1) * HG * HD], w_v[:, g * HD:(g + 1) * HD]]
        per_group.append(by_feature(np.concatenate(cols, axis=1)))
    return np.stack(per_group), w_o.reshape(NG, HG, HD, D).transpose(0, 2, 1, 3)


def rotary_angles(width, positions):
    inv = (1.0 / 10000.0 ** (np.arange(0, width, 2, dtype=np.float32) / np.float32(width))).astype(np.float32)
    return np.arange(positions, dtype=np.float32)[:, None] * inv[None, :]


def layouts(i):
    f = np.float32
    a = {"x": i["x"][0], "ident": np.eye(P, dtype=f), "ctx_t": by_feature(i["ctx_4096"][0].T)}
    a["L0x_kqv"], a["L0x_o"] = grouped(i["L0_xattn_wq"], i["L0_xattn_wk"], i["L0_xattn_wv"], i["L0_xattn_wo"])
    a["L0x_mask"] = i["mask_BxSxS2_ff0"][0]
    ang = rotary_angles(HD, SK).T
    cos, sin = np.cos(ang).astype(f), np.sin(ang).astype(f)
    scale = f(1.0) / np.sqrt(f(HD))
    a["L0x_cos"] = np.concatenate([cos, cos])
    a["L0x_sin"] = np.concatenate([-sin, sin])
    a["L0x_cos_q"] = a["L0x_cos"][:, :P] * scale
    a["L0x_sin_q"] = a["L0x_sin"][:, :P] * scale
    a["L3x_kqv"], a["L3x_o"] = grouped(i["L3_xattn_q_proj_w"].T, i["L3_xattn_k_proj_w"].T,
                                       i["L3_xattn_v_proj_w"].T, i["L3_xattn_o_proj_w"].T)
    a["L3x_mask"] = i["mask_1x1xSxS2_ff0"][0, 0]
    a["L3x_cols"] = np.stack([i["L3_xattn_q_norm_w"], i["L3_xattn_k_norm_w"]], axis=1)
    row = lambda *parts: np.concatenate(parts)[None, :]
    beside = lambda *parts: by_feature(np.concatenate(parts, axis=1))
    a["iota8"] = np.arange(8, dtype=f)[None, :]
    a["L0a_w"] = beside(*(i[f"L0_attn_W{n}"].T for n in "qkvo"))
    a["L0a_rows"] = row(*(i[f"L0_attn_b{n}"] for n in "qkvo"))
    a["L0f_w"] = beside(i["L0_ffn_weight"].T, i["L0_ffn_lora_A"].reshape(48, D).T)
    a["L0f_rows"] = row(i["L0_ffn_bias"])
    a["L0f_up"] = i["L0_ffn_lora_B"].transpose(0, 2, 1).reshape(48, D)
    a["L0f_starts"] = i["L0_ffn_lora_start_indices"][None, :]
    a["L1f_w"] = beside(i["L1_ffn_base_w"].T, i["L1_ffn_lora_A"].reshape(P, D).T, i["L1_ffn_gate_w"].T)
    a["L1f_rows"] = row(i["L1_ffn_base_b"])
    a["L1f_up"] = i["L1_ffn_lora_B"].transpose(0, 2, 1).reshape(P, D)
    a["L2f_w"] = beside(i["L2_ffn_W_org"].T, i["L2_ffn_lora_down"].transpose(1, 0, 2).reshape(D, D),
                        i["L2_ffn_Wq"].T)
    a["L2f_keys"] = i["L2_ffn_lora_keys"].T
    a["L2f_up"] = by_feature(i["L2_ffn_lora_up"].reshape(D, D))
    a["L3a_w"] = by_feature(i["L3_attn_Wqkv"])
    a["L3a_o"] = i["L3_attn_Wo"]
    a["L3a_cols"] = i["L3_attn_bqkv"][:2 * HD].reshape(2, HD).T
    a["L3a_rows"] = row(i["L3_attn_bqkv"][2 * HD:], i["L3_attn_bo"])
    books = np.zeros((4, 32, 8, 2, 4, 16), f)
    for group in range(8):
        for book in range(4):
            books[book, :, group, group % 2, book] = i["L3_ffn_codebooks"][4 * group + book]
    a["L3f_books"] = books.reshape(P, 8, P)
    codes = np.concatenate([i["L3_ffn_codes"], i["L3_ffn_centroids"]], axis=1)
    codes = np.broadcast_to(codes.reshape(8, 4, 1, D + 32), (8, 4, 32, D + 32))
    a["L3f_codes"] = codes.transpose(1, 2, 0, 3).reshape(P, 8, D + 32)
    a["L3f_entry"] = np.tile(np.arange(32, dtype=f), 4)[:, None]
    a["L3f_rows"] = row(i["L3_ffn_bias"], i["L3_ffn_ln_weight"])
    a["L1x_w"] = beside(i["L1_xattn_Wq_w"].T, i["L1_xattn_Wk_w"].T)
    a["L1x_ctx"] = i["ctx_4096"][0].reshape(KT, P, D).transpose(1, 0, 2)
    a["L1x_cols"] = i["L1_xattn_fn_w"].reshape(CT, P).T
    a["L1x_rows"] = row(*(i[f"L1_xattn_{n}"] for n in ("Wq_b", "Wk_b", "qn_w", "kn_w", "fn_w")))
    ang = rotary_angles(64, P)
    cos, sin = np.cos(ang).astype(f), np.sin(ang).astype(f)
    a["latent_rot"] = np.stack([np.concatenate([cos, cos], 1), np.concatenate([-sin, sin], 1)], axis=1)
    a["causal"] = np.triu(np.full((P, P), LOWEST, f), 1)
    halves = np.r_[0:64:2, 1:64:2]
    a.update(latent_layouts("L1a", i["L1_attn_q_a_w"], i["L1_attn_kv_a_w"], i["L1_attn_q_a_norm_w"],
                            i["L1_attn_kv_a_norm_w"], i["L1_attn_q_b_w"], i["L1_attn_kv_b_w"],
                            i["L1_attn_o_w"], halves))
    a.update(latent_layouts("L2a", i["L2_attn_w_qa"], i["L2_attn_w_kva"], i["L2_attn_g_qa"],
                            i["L2_attn_g_kva"], i["L2_attn_w_qb"], i["L2_attn_w_kvb"], i["L2_attn_w_o"],
                            np.arange(64)))
    q_by_place = i["L2_xattn_w_q"].reshape(NG, HG, 16, D).transpose(1, 0, 2, 3).reshape(D, D)
    a["L2x_w"] = beside(i["L2_xattn_w_k"].T, i["L2_xattn_w_v"].T, q_by_place.T)
    a["L2x_o"] = i["L2_xattn_w_out"].T.reshape(NG, HG, 16, D).transpose(0, 2, 1, 3).reshape(P, HG, D)
    a["L2x_mask"] = i["mask_SxS2_bk0"]
    a["L2x_groups"] = np.repeat(np.eye(NG, dtype=f), 16, axis=0)
    return a


def latent_layouts(name, q_a, kv_a, g_q, g_kv, q_b, kv_b, o, order):
    kv_a = np.concatenate([kv_a[:, :64], kv_a[:, 64:][:, order]], axis=1)
    q_b = q_b.reshape(192, NG, HG, 192).transpose(1, 0, 2, 3)
    q_b = np.concatenate([q_b[..., :128].reshape(NG, 192, 512), q_b[..., 128:][..., order].reshape(NG, 192, 256)], 2)
    kv_b = kv_b.reshape(64, NG, HG, 2, 128).transpose(1, 0, 3, 2, 4).reshape(NG, 64, 1024)
    return {f"{name}_w": by_feature(np.concatenate([q_a, kv_a], axis=1)),
            f"{name}_rows": np.concatenate([g_q, g_kv])[None, :],
            f"{name}_hi": q_b[:, :128], f"{name}_lo": np.concatenate([q_b[:, 128:], kv_b], axis=2),
            f"{name}_o": o.reshape(NG, HG, HD, D).transpose(0, 2, 1, 3)}


def kernel(**inputs):
    import concourse.bacc as bacc
    from concourse.bass_utils import run_bass_kernel_spmd

    laid = {k: np.ascontiguousarray(v) for k, v in layouts({k: np.asarray(v) for k, v in inputs.items()}).items()}
    nc = bacc.Bacc("TRN2", target_bir_lowering=False, num_devices=1)
    aps = {k: nc.dram_tensor(f"in_{k}", v.shape, mybir.dt.from_np(v.dtype), kind="ExternalInput").ap()
           for k, v in laid.items()}
    out = nc.dram_tensor("out", (P, D), F32, kind="ExternalOutput").ap()
    perceiver(nc, aps, out)
    result = run_bass_kernel_spmd(nc, [{f"in_{k}": v for k, v in laid.items()}], core_ids=[0])
    return result.results[0]["out"].reshape(1, P, D)
```

```python
from contextlib import ExitStack

import numpy as np

import concourse.bass as bass
from concourse import mybir
from concourse.alu_op_type import AluOpType as ALU

ACT = mybir.ActivationFunctionType
AX = mybir.AxisListType
F32 = mybir.dt.float32
F32R = mybir.dt.float32r
I32 = mybir.dt.int32
U8 = mybir.dt.uint8

P = 128
D = 512
CT = D // P
SK = 2048
KT = SK // P
NC = SK // 512
HD = 128
NH = 32
NG = 8
HG = NH // NG
LOWEST = float(np.finfo(np.float32).min)


class Steps:

    def __init__(self, eng, sem, base=0):
        self.eng, self.sem, self.base, self.n = eng, sem, base, 0

    def then(self, ins):
        self.n += 1
        ins.then_inc(self.sem, 1)
        self.eng.wait_ge(self.sem, self.base + self.n)


class Memory:

    ALIGN = 64

    def __init__(self, nc):
        self.nc, self.first, self.end = nc, -(-nc.sbuf_base // 64) * 64, nc.sbuf_usable_end
        self.taken = {}

    def take(self, name, shape, dt=F32):
        size = int(np.prod(shape[1:])) * mybir.dt.size(dt)
        size = -(-size // self.ALIGN) * self.ALIGN
        at = self.first
        for lo, hi in sorted(self.taken.values()):
            if at + size <= lo:
                break
            at = max(at, hi)
        assert at + size <= self.end, f"{name} does not fit"
        self.taken[name] = (at, at + size)
        return self.nc.alloc_sbuf_tensor_at(name, shape, dt, offset=at)

    def lend(self, names):
        return {name: self.taken.pop(name) for name in names}

    def take_again(self, lent):
        self.taken.update(lent)

    def give_back(self, names):
        for name in names:
            del self.taken[name]


class Core:

    def __init__(self, nc, ctx):
        self.nc = nc
        self.memory = Memory(nc)
        self.ctx = ctx
        self.freed = ExitStack()
        self.keys = None
        self.stale = []
        sb = self.memory.take
        self.x = sb("x", [P, D])
        self.xn_t = sb("xn_t", [P, CT, P])
        self.ctx_t = None
        self.ident = sb("ident", [P, P])
        self.ones = sb("ones", [P, P])
        self.ones_r = sb("ones_r", [P, P], F32R)
        self.eps5 = sb("eps5", [P, 1])
        self.eps6 = sb("eps6", [P, 1])
        self.zero = sb("zero", [P, 1])
        self.bank = [ctx.enter_context(nc.psum_tensor(f"bank{i}", [P, 512], F32)) for i in range(8)]

    def end_with_last(self, stage):
        self.memory.give_back(stage.names)
        self.stale = self.stale + stage.sems
        self.freed.callback(stage.ctx.close)

    def hold_context(self):
        if self.ctx_t is not None:
            return False
        self.ctx_t = self.memory.take("ctx_t", [P, CT, SK])
        return True

    def drop_context(self):
        self.memory.give_back(["ctx_t"])
        self.ctx_t = None

    def clear_stale(self, pool):
        for s in self.stale:
            pool.sem_clear(s)


class Stage:

    def __init__(self, core, name):
        self.core, self.name = core, name
        self.ctx = ExitStack()
        self.sems, self.names = [], []

    def __enter__(self):
        return self

    def sb(self, name, shape, dt=F32):
        self.names.append(f"{self.name}_{name}")
        return self.core.memory.take(self.names[-1], shape, dt)

    def sem(self, name):
        s = self.ctx.enter_context(self.core.nc.semaphore(f"{self.name}_{name}"))
        self.sems.append(s)
        return s

    def __exit__(self, *exc):
        if exc[0] is None:
            self.core.memory.give_back(self.names)
            self.core.freed.close()
            self.core.freed, self.core.stale = self.ctx, self.sems


class LayerNorm:

    def __init__(self, core, st, bank):
        self.core, self.bank = core, bank
        self.xn = st.sb("ln_xn", [P, D])
        self.stats = st.sb("ln_stats", [P, 6])
        self.mean_var = st.sb("ln_mean_var", [P, 2])
        self.small = st.sb("ln_small", [P, 3])
        self.own = st.sem("ln_own")
        self.var_ready = st.sem("ln_var_ready")
        self.std_ready = st.sem("ln_std_ready")
        self.xn_ready = st.sem("ln_xn_ready")
        self.turned = st.sem("ln_turned")
        self.ready = st.sem("ln_ready")

    def vector(self, dve):
        core, steps = self.core, Steps(dve, self.own)
        veps, std, rstd = (self.small[:, i:i + 1] for i in range(3))
        steps.then(dve.bn_stats(self.stats[:], core.x[:]))
        steps.then(dve.bn_aggr(self.mean_var[:], self.stats[:]))
        dve.tensor_scalar(veps, self.mean_var[:, 1:2], 1e-5, None, ALU.add).then_inc(self.var_ready, 1)
        dve.wait_ge(self.std_ready, 1)
        steps.then(dve.reciprocal(rstd, std))
        dve.tensor_scalar(self.xn[:], core.x[:], self.mean_var[:, 0:1], rstd, ALU.subtract,
                          ALU.mult).then_inc(self.xn_ready, 1)
        dve.wait_ge(self.turned, 1)
        dve.tensor_copy(core.xn_t[:], self.bank[:].rearrange("p (c q) -> p c q", c=CT)).then_inc(self.ready, 1)

    def scalar(self, act):
        act.wait_ge(self.var_ready, 1)
        act.activation(self.small[:, 1:2], self.small[:, 0:1], ACT.Sqrt).then_inc(self.std_ready, 1)

    def tensor(self, pe):
        pe.wait_ge(self.xn_ready, 1)
        for c in range(CT):
            mm = pe.transpose(self.bank[:, c * P:(c + 1) * P], self.xn[:, c * P:(c + 1) * P], self.core.ident[:])
        mm.then_inc(self.turned, 1)
        pe.wait_ge(self.ready, 1)


def wide_cross_attention(core, name, wkqv, wo, mask, ctx_t, rotary=None, norm_cols=None):
    nc = core.nc
    SCALE = float(1.0 / np.sqrt(np.float32(HD)))
    PROJ = NC + 1
    AHEAD = 3
    chunk = lambda n: slice(n * 512, (n + 1) * 512)
    with Stage(core, name) as st:
        if rotary is not None:
            cos_t = st.sb("cos_t", [P, SK])
            sin_t = st.sb("sin_t", [P, SK])
            cos_q = st.sb("cos_q", [P, P])
            sin_q = st.sb("sin_q", [P, P])
        else:
            cols = st.sb("cols", [P, 3])
        w_kqv = st.sb("w_kqv", [P, CT, 768])
        w_o = st.sb("w_o", [P, HG, D])
        mask_sb = st.sb("mask", [P, SK])
        s_sb = st.sb("s", [P, HG, SK])
        ctx_hi = st.sb("ctx_hi", [P, CT, SK], F32R)
        ctx_lo = st.sb("ctx_lo", [P, CT, SK], F32R)
        consts_in = st.sem("consts_in")
        ctx_in = [st.sem(f"ctx_in{n}") for n in range(NC)]
        w_kv_in = st.sem("w_kv_in")
        w_in = st.sem("w_in")
        wo_in = st.sem("wo_in")

        def issue(sp):
            sp.dma_start(w_kqv[:, :, 0:256], wkqv[0][:, :, 0:256]).then_inc(w_kv_in, 16)
            for n in range(NC):
                sp.dma_start(s_sb[:, :, chunk(n)], ctx_t[:, :, chunk(n)]).then_inc(ctx_in[n], 16)
                if n == 0:
                    sp.dma_start(w_kqv[:, :, 256:], wkqv[0][:, :, 256:]).then_inc(w_in, 16)
            if rotary is not None:
                for t, table in zip((cos_t, sin_t, cos_q, sin_q), rotary):
                    sp.dma_start(t[:], table).then_inc(consts_in, 16)
            else:
                sp.dma_start(cols[:, 0:2], norm_cols).then_inc(consts_in, 16)
            sp.dma_start(mask_sb[:], mask).then_inc(consts_in, 16)
            sp.dma_start(w_o[:], wo[0]).then_inc(wo_in, 16)

        lent = [f"{name}_ctx_hi", f"{name}_ctx_lo"]
        if rotary is not None:
            lent += [f"{name}_cos_t", f"{name}_sin_t"]
        lent = core.memory.lend(lent)
        following = yield issue
        core.memory.take_again(lent)
        norm = LayerNorm(core, st, core.bank[0])
        w_hi = st.sb("w_hi", [P, CT, 256], F32R)
        w_lo = st.sb("w_lo", [P, CT, 256], F32R)
        k_hi = st.sb("k_hi", [P, SK], F32R)
        k_lo = st.sb("k_lo", [P, SK], F32R)
        p_hi = k_hi[:].rearrange("p (k n) -> p k n", k=4)
        p_lo = k_lo[:].rearrange("p (k n) -> p k n", k=4)
        q_hi = st.sb("q_hi", [P, HG * P], F32R)
        q_lo = st.sb("q_lo", [P, HG * P], F32R)
        v_hi = st.sb("v_hi", [P, KT, HD], F32R)
        v_lo = st.sb("v_lo", [P, KT, HD], F32R)
        v_t = st.sb("v_t", [P, 2, 512])
        aux = st.sb("aux", [P, 2, 512])
        diag = aux[:, 0, :].rearrange("p (h q) -> p h q", h=HG)
        o_t = st.sb("o_t", [P, HG * P])
        flat = s_sb[:].rearrange("p h k -> p (h k)")
        raw = flat[:, 0:PROJ * 512].rearrange("p (n k) -> p n k", n=PROJ)
        rms = flat[:, PROJ * 512:2 * PROJ * 512].rearrange("p (n k) -> p n k", n=PROJ)
        rinv = st.sb("rinv", [P, HG * P])
        part_max = st.sb("part_max", [P, HG, NC])
        neg_max = st.sb("neg_max", [P, HG])
        row_sum = st.sb("row_sum", [P, HG])
        r_sum = st.sb("r_sum", [P, HG])

        ctx_hi_kept = st.sem("ctx_hi_kept")
        ctx_kept = st.sem("ctx_kept")
        w_hi_kept = st.sem("w_hi_kept")
        w_kept = st.sem("w_kept")
        proj_ready = st.sem("proj_ready")
        proj_read_act = st.sem("proj_read_act")
        proj_read_dve = st.sem("proj_read_dve")
        aux_used = st.sem("aux_used")
        sumsq_ready = st.sem("sumsq_ready")
        rms_read = st.sem("rms_read")
        rms_ready = st.sem("rms_ready")
        raw_ready = st.sem("raw_ready")
        kq_hi_kept = st.sem("kq_hi_kept")
        kq_ready = st.sem("kq_ready")
        vt_proj = st.sem("vt_proj")
        vt_kept = st.sem("vt_kept")
        v_turned = st.sem("v_turned")
        v_hi_kept = st.sem("v_hi_kept")
        v_ready = st.sem("v_ready")
        s_ready = st.sem("s_ready")
        s_seen = st.sem("s_seen")
        s_read = st.sem("s_read")
        max_ready = st.sem("max_ready")
        exp_ready = st.sem("exp_ready")
        turned = st.sem("turned")
        p_hi_kept = st.sem("p_hi_kept")
        p_ready = st.sem("p_ready")
        pv_done = st.sem("pv_done")
        diag_recip = st.sem("diag_recip")
        diag_ready = st.sem("diag_ready")
        rinv_ready = st.sem("rinv_ready")
        rinv_kept = st.sem("rinv_kept")
        o_ready = st.sem("o_ready")
        wo_done = st.sem("wo_done")
        x_added = st.sem("x_added")
        dve_own = st.sem("dve_own")
        cols_ready = st.sem("cols_ready")
        out_bank, rinv_bank, wo_bank = core.bank[7], core.bank[2], core.bank[1]
        proj_bank = lambda n: core.bank[n % 3]
        VT, V = (5, 6, 8, 10), (7, 9, 11, 12)
        ring_bank = lambda n: core.bank[3 + n % 4]
        bits = lambda t: t.bitcast(F32)

        consts_all = 16 * (5 if rotary is not None else 2)

        with nc.Block() as block:
            @block.gpsimd
            def _(pool):
                core.clear_stale(pool)

            @block.sync
            def _(sp):
                def load_w(g):
                    sp.wait_ge(proj_ready, g * PROJ)
                    sp.wait_ge(w_kept, g)
                    sp.dma_start(w_kqv[:], wkqv[g]).then_inc(w_in, 16)

                def load_wo(g):
                    sp.wait_ge(wo_done, g)
                    sp.dma_start(w_o[:], wo[g]).then_inc(wo_in, 16)

                load_w(1)
                with sp.Fori(2, NG) as g:
                    load_w(g)
                    load_wo(g - 1)
                load_wo(NG - 1)
                sp.sem_inc(w_in, 16)
                sp.wait_ge(vt_proj, NG * 4)
                sp.wait_ge(kq_ready, NG * PROJ)
                following(sp)

            @block.tensor
            def _(pe):
                norm.tensor(pe)

                def three_passes(out, left, right, start=True, stop=True):
                    pe.matmul(out, left[0], right[0], start=start, stop=False)
                    pe.matmul(out, left[0], right[1], start=False, stop=False)
                    return pe.matmul(out, left[1], right[0], start=False, stop=stop)

                def project_out(g):
                    pe.wait_ge(wo_in, g * 16 + 16)
                    pe.wait_ge(o_ready, g + 1)
                    for h in range(HG):
                        mm = pe.matmul(wo_bank[:], o_t[:, h * P:(h + 1) * P], w_o[:, h, :],
                                       start=(h == 0), stop=(h == HG - 1))
                    mm.then_inc(wo_done, 1)

                def group(g, first=False):
                    pe.wait_ge(w_kept, g + 1)

                    def sum_squares(n):
                        pe.wait_ge(proj_read_act, g * PROJ + n + 1)
                        if n > 0:
                            pe.wait_ge(rms_read, g * PROJ + n)
                        elif not first:
                            pe.wait_ge(o_ready, g)
                        pe.matmul(out_bank[:], core.ones[:], aux[:, n % 2, :], start=True,
                                  stop=True).then_inc(sumsq_ready, 1)

                    for n in range(PROJ):
                        if n >= 3:
                            pe.wait_ge(proj_read_dve, g * PROJ + n - 2)
                        elif not first:
                            pe.wait_ge(v_ready, g * 4)
                            if n == 1:
                                pe.wait_ge(x_added, g)
                            if n == 2:
                                pe.wait_ge(rinv_kept, g)
                        if n < NC:
                            if first:
                                pe.wait_ge(ctx_kept, n + 1)
                            for c in range(CT):
                                mm = three_passes(proj_bank(n)[:], (w_hi[:, c, 0:128], w_lo[:, c, 0:128]),
                                                  (ctx_hi[:, c, chunk(n)], ctx_lo[:, c, chunk(n)]),
                                                  start=(c == 0), stop=(c == CT - 1))
                        else:
                            pe.wait_ge(w_in, g * 16 + 16)
                            for h in range(HG):
                                for c in range(CT):
                                    mm = pe.matmul(proj_bank(n)[:, h * P:(h + 1) * P],
                                                   w_kqv[:, c, 256 + h * HD:256 + (h + 1) * HD],
                                                   core.xn_t[:, c, :], start=(c == 0), stop=(c == CT - 1))
                        mm.then_inc(proj_ready, 1)
                        if rotary is None and n > 0:
                            sum_squares(n - 1)

                    def project_v(n):
                        if n < 2:
                            pe.wait_ge(proj_read_dve, g * PROJ + n + 3)
                        elif n == 2:
                            pe.wait_ge(vt_kept, g * 4 + 1)
                        else:
                            pe.wait_ge(v_ready, g * 4 + 1)
                        for c in range(CT):
                            mm = three_passes(proj_bank(VT[n])[:], (w_hi[:, c, 128:256], w_lo[:, c, 128:256]),
                                              (ctx_hi[:, c, chunk(n)], ctx_lo[:, c, chunk(n)]),
                                              start=(c == 0), stop=(c == CT - 1))
                        mm.then_inc(vt_proj, 1)

                    def turn_v(n):
                        pe.wait_ge(vt_kept, g * 4 + n + 1)
                        if n == 0:
                            pe.wait_ge(proj_read_dve, g * PROJ + PROJ)
                        elif n < 3:
                            pass
                        else:
                            pe.wait_ge(v_ready, g * 4 + 2)
                        for j in range(4):
                            mm = pe.transpose(proj_bank(V[n])[:, j * P:(j + 1) * P], v_t[:, n % 2, j * P:(j + 1) * P],
                                              core.ident[:])
                        mm.then_inc(v_turned, 1)

                    project_v(0)
                    if rotary is None:
                        sum_squares(PROJ - 1)
                    project_v(1)
                    turn_v(0)
                    project_v(2)
                    turn_v(1)
                    project_v(3)
                    turn_v(2)
                    turn_v(3)
                    pe.wait_ge(kq_ready, g * PROJ + PROJ)
                    for h in range(HG):
                        for c in range(NC):
                            n = h * NC + c
                            if n < 4:
                                if not first:
                                    pe.wait_ge(p_ready, g * 16)
                            else:
                                pe.wait_ge(s_read, g * 16 + n - 3)
                            heads = slice(h * P, (h + 1) * P)
                            three_passes(ring_bank(n)[:], (q_hi[:, heads], q_lo[:, heads]),
                                         (k_hi[:, chunk(c)], k_lo[:, chunk(c)])).then_inc(s_ready, 1)
                    if not first:
                        pe.wait_ge(vt_kept, g * 4 + 4)
                        project_out(g - 1)

                    def turn(kt):
                        if kt < 4:
                            pe.wait_ge(s_read, g * 16 + 16)
                        else:
                            pe.wait_ge(p_ready, g * 16 + kt - 3)
                        for h in range(HG):
                            if kt == 0:
                                pe.wait_ge(exp_ready, g * 4 + h + 1)
                            mm = pe.transpose(ring_bank(kt)[:, h * P:(h + 1) * P],
                                              s_sb[:, h, kt * P:(kt + 1) * P], core.ident[:])
                        mm.then_inc(turned, 1)

                    def weigh(kt):
                        pe.wait_ge(p_ready, g * 16 + kt + 1)
                        if kt == 0:
                            pe.wait_ge(v_ready, g * 4 + 4)
                            if rotary is None:
                                pe.wait_ge(rms_read, g * PROJ + PROJ)
                            elif not first:
                                pe.wait_ge(o_ready, g)
                        three_passes(out_bank[:], (v_hi[:, kt, :], v_lo[:, kt, :]),
                                     (p_hi[:, kt % 4, :], p_lo[:, kt % 4, :]), start=(kt == 0),
                                     stop=(kt == KT - 1)).then_inc(pv_done, 1)

                    for kt in range(KT + AHEAD):
                        if kt < KT:
                            turn(kt)
                        if kt == 12:
                            pe.wait_ge(diag_ready, g * 4 + 4)
                            pe.matmul(rinv_bank[:], core.ones[:], aux[:, 0, :], start=True,
                                      stop=True).then_inc(rinv_ready, 1)
                        if kt >= AHEAD:
                            weigh(kt - AHEAD)

                group(0, first=True)
                with pe.Fori(1, NG) as g:
                    group(g)
                pe.wait_ge(x_added, NG)
                project_out(NG - 1)

            @block.scalar
            def _(act):
                norm.scalar(act)

                def split_w(g):
                    if isinstance(g, int) and g == 0:
                        act.wait_ge(w_kv_in, 16)
                    else:
                        act.wait_ge(w_in, g * 16 + 16)
                    act.activation(w_hi[:], w_kqv[:, :, 0:256], ACT.Copy).then_inc(w_hi_kept, 1)

                split_w(0)
                for n in range(NC):
                    act.wait_ge(ctx_in[n], 16)
                    act.activation(ctx_hi[:, :, chunk(n)], s_sb[:, :, chunk(n)], ACT.Copy).then_inc(ctx_hi_kept, 1)
                act.wait_ge(ctx_kept, NC)

                def group(g, first=False):
                    def keep_hi(n):
                        act.wait_ge(raw_ready, g * PROJ + n + 1)
                        act.activation(k_hi[:, chunk(n)] if n < NC else q_hi[:], raw[:, n, :],
                                       ACT.Copy).then_inc(kq_hi_kept, 1)

                    for n in range(PROJ):
                        act.wait_ge(proj_ready, g * PROJ + n + 1)
                        src = proj_bank(n)
                        if rotary is not None:
                            if n >= 2:
                                act.wait_ge(aux_used, g * PROJ + n - 1)
                            act.activation(aux[64:128, n % 2, :], src[0:64, :], ACT.Copy)
                            act.activation(aux[0:64, n % 2, :], src[64:128, :],
                                           ACT.Copy).then_inc(proj_read_act, 1)
                            if n > 0:
                                keep_hi(n - 1)
                        else:
                            if n >= 2:
                                act.wait_ge(sumsq_ready, g * PROJ + n - 1)
                            act.activation(aux[:, n % 2, :], src[:], ACT.Square,
                                           scale=float(HD ** -0.5)).then_inc(proj_read_act, 1)
                            if n > 0:
                                act.wait_ge(sumsq_ready, g * PROJ + n)
                                act.activation(rms[:, n - 1, :], out_bank[:], ACT.Ln,
                                               bias=core.eps5[:]).then_inc(rms_read, 1)
                    def keep_v_t(n):
                        act.wait_ge(vt_proj, g * 4 + n + 1)
                        if n >= 2:
                            act.wait_ge(v_turned, g * 4 + n - 1)
                        act.activation(v_t[:, n % 2, :], proj_bank(VT[n])[:], ACT.Copy).then_inc(vt_kept, 1)

                    def keep_v(n):
                        act.wait_ge(v_turned, g * 4 + n + 1)
                        act.activation(v_hi[:, 4 * n:4 * n + 4, :],
                                       proj_bank(V[n])[:].rearrange("p (k d) -> p k d", k=4),
                                       ACT.Copy).then_inc(v_hi_kept, 1)

                    if rotary is not None:
                        keep_hi(PROJ - 1)
                        keep_v_t(0)
                    else:
                        keep_v_t(0)
                        act.wait_ge(sumsq_ready, g * PROJ + PROJ)
                        act.activation(rms[:, PROJ - 1, :], out_bank[:], ACT.Ln,
                                       bias=core.eps5[:]).then_inc(rms_read, 1)
                        act.wait_ge(rms_read, g * PROJ + PROJ)
                        act.activation(rms, rms, ACT.Exp, scale=-0.5).then_inc(rms_ready, 1)

                    keep_v_t(1)
                    keep_v(0)
                    if rotary is None:
                        keep_hi(0)
                        keep_hi(1)
                    keep_v_t(2)
                    keep_v(1)
                    if rotary is None:
                        for n in range(2, PROJ):
                            keep_hi(n)
                    keep_v_t(3)
                    keep_v(2)
                    keep_v(3)
                    for h in range(HG):
                        act.wait_ge(max_ready, g * 4 + h + 1)
                        act.activation(s_sb[:, h, :], s_sb[:, h, :], ACT.Exp, bias=neg_max[:, h:h + 1],
                                       scale=1.0, accum_out=row_sum[:, h:h + 1]).then_inc(exp_ready, 1)
                    for kt in range(KT):
                        act.wait_ge(turned, g * 16 + kt + 1)
                        if kt >= 4:
                            act.wait_ge(pv_done, g * 16 + kt - 3)
                        act.activation(p_hi[:, kt % 4, :], ring_bank(kt)[:], ACT.Copy).then_inc(p_hi_kept, 1)
                        if kt == 9:
                            split_w(g + 1)
                    act.wait_ge(rinv_ready, g + 1)
                    if not first:
                        act.wait_ge(o_ready, g)
                    act.activation(rinv[:], rinv_bank[:], ACT.Copy).then_inc(rinv_kept, 1)

                group(0, first=True)
                with act.Fori(1, NG) as g:
                    group(g)

            @block.vector
            def _(dve):
                norm.vector(dve)

                dve.sem_inc(x_added, 1)

                def split_w(g):
                    dve.wait_ge(w_hi_kept, g + 1)
                    dve.tensor_tensor(w_lo[:], w_kqv[:, :, 0:256], bits(w_hi[:]), ALU.subtract).then_inc(w_kept, 1)

                split_w(0)
                for n in range(NC):
                    dve.wait_ge(ctx_hi_kept, n + 1)
                    dve.tensor_tensor(ctx_lo[:, :, chunk(n)], s_sb[:, :, chunk(n)], bits(ctx_hi[:, :, chunk(n)]),
                                      ALU.subtract).then_inc(ctx_kept, 1)
                dve.wait_ge(consts_in, consts_all)
                if rotary is None:
                    dve.tensor_scalar(cols[:, 2:3], cols[:, 0:1], SCALE, None, ALU.mult).then_inc(cols_ready, 1)
                    dve.wait_ge(cols_ready, 1)
                dve.wait_ge(ctx_kept, NC)

                def group(g, first=False):
                    own_a_group = PROJ
                    steps = Steps(dve, dve_own, base=g * own_a_group)

                    def keep_lo(n):
                        dve.wait_ge(kq_hi_kept, g * PROJ + n + 1)
                        hi, lo = (k_hi[:, chunk(n)], k_lo[:, chunk(n)]) if n < NC else (q_hi[:], q_lo[:])
                        dve.tensor_tensor(lo, raw[:, n, :], bits(hi), ALU.subtract).then_inc(kq_ready, 1)

                    def keep_v(n):
                        dve.wait_ge(v_hi_kept, g * 4 + n + 1)
                        dve.tensor_tensor(v_lo[:, 4 * n:4 * n + 4, :],
                                          proj_bank(V[n])[:].rearrange("p (k d) -> p k d", k=4),
                                          bits(v_hi[:, 4 * n:4 * n + 4, :]), ALU.subtract).then_inc(v_ready, 1)

                    for n in range(PROJ):
                        dve.wait_ge(proj_read_act, g * PROJ + n + 1)
                        if rotary is not None:
                            if n < NC:
                                view = lambda t: t
                                cos, sin = (t[:, chunk(n)] for t in (cos_t, sin_t))
                            else:
                                view = lambda t: t.rearrange("p (h q) -> p h q", h=HG)
                                cos, sin = (t[:].unsqueeze(1).to_broadcast([P, HG, P]) for t in (cos_q, sin_q))
                            dve.tensor_tensor(view(raw[:, n, :]), view(proj_bank(n)[:]), cos,
                                              ALU.mult).then_inc(proj_read_dve, 1)
                            steps.then(dve.tensor_tensor(view(aux[:, n % 2, :]), view(aux[:, n % 2, :]),
                                                         sin, ALU.mult))
                            dve.wait_ge(proj_read_dve, g * PROJ + n + 1)
                            dve.tensor_tensor(raw[:, n, :], raw[:, n, :], aux[:, n % 2, :],
                                              ALU.add).then_inc(raw_ready, 1)
                            dve.wait_ge(raw_ready, g * PROJ + n + 1)
                            dve.sem_inc(aux_used, 1)
                            if n > 0:
                                keep_lo(n - 1)
                        else:
                            weight = cols[:, 1:2] if n < NC else cols[:, 2:3]
                            dve.tensor_scalar(raw[:, n, :], proj_bank(n)[:], weight, None,
                                              ALU.mult).then_inc(proj_read_dve, 1)
                    if rotary is not None:
                        keep_lo(PROJ - 1)
                        keep_v(0)
                    else:
                        dve.wait_ge(rms_ready, g + 1)
                        dve.wait_ge(proj_read_dve, g * PROJ + PROJ)
                        for n in range(PROJ):
                            dve.tensor_tensor(raw[:, n, :], raw[:, n, :], rms[:, n, :],
                                              ALU.mult).then_inc(raw_ready, 1)
                            if n == 1:
                                keep_v(0)
                        keep_lo(0)
                        keep_lo(1)
                    keep_v(1)
                    if rotary is None:
                        for n in range(2, PROJ):
                            keep_lo(n)
                    keep_v(2)
                    keep_v(3)
                    dve.wait_ge(kq_ready, g * PROJ + PROJ)
                    for h in range(HG):
                        for c in range(NC):
                            n = h * NC + c
                            dve.wait_ge(s_ready, g * 16 + n + 1)
                            dve.sem_inc(s_seen, 1)
                            dve.tensor_tensor_reduce(
                                s_sb[:, h, chunk(c)], ring_bank(n)[:], mask_sb[:, chunk(c)], 1.0, LOWEST, ALU.add,
                                ALU.max, part_max[:, h, c:c + 1]).then_inc(s_read, 1)
                        dve.wait_ge(s_read, g * 16 + h * NC + NC)
                        dve.tensor_reduce(neg_max[:, h:h + 1], part_max[:, h, :], AX.X, ALU.max,
                                          negate=True).then_inc(max_ready, 1)
                    if not first:
                        dve.wait_ge(wo_done, g)
                        dve.tensor_tensor(core.x[:], core.x[:], wo_bank[:], ALU.add).then_inc(x_added, 1)
                    for kt in range(KT):
                        dve.wait_ge(p_hi_kept, g * 16 + kt + 1)
                        dve.tensor_tensor(p_lo[:, kt % 4, :], ring_bank(kt)[:], bits(p_hi[:, kt % 4, :]),
                                          ALU.subtract).then_inc(p_ready, 1)
                        if kt == 5:
                            dve.wait_ge(exp_ready, g * 4 + 4)
                            dve.reciprocal(r_sum[:], row_sum[:]).then_inc(diag_recip, 1)
                        if kt == 6:
                            dve.wait_ge(diag_recip, g + 1)
                            for h in range(HG):
                                dve.tensor_scalar(diag[:, h, :], core.ident[:], r_sum[:, h:h + 1], None,
                                                  ALU.mult).then_inc(diag_ready, 1)
                        if kt == 9:
                            split_w(g + 1)
                    dve.wait_ge(rinv_kept, g + 1)
                    dve.wait_ge(pv_done, g * 16 + 16)
                    dve.tensor_tensor(o_t[:], out_bank[:], rinv[:], ALU.mult).then_inc(o_ready, 1)

                group(0, first=True)
                with dve.Fori(1, NG) as g:
                    group(g)
                dve.wait_ge(wo_done, NG)
                dve.tensor_tensor(core.x[:], core.x[:], wo_bank[:], ALU.add).then_inc(x_added, 1)


class ContextKeys:

    def __init__(self, core, a):
        self.core, self.a = core, a
        self.load_context = core.hold_context()
        self.st = st = Stage(core, "L1k")
        self.k_t = st.sb("k_t", [P, KT, CT, P])
        self.rstd_f = st.sb("rstd_f", [P, KT])
        self.work = work = Stage(core, "L1kw")
        self.w = work.sb("w", [P, CT, D])
        self.cols = work.sb("cols", [P, CT])
        self.row = work.sb("row", [P, D])
        self.ctx = work.sb("ctx", [P, 2, 4, D])
        self.junk = work.sb("junk", [P, D])
        self.raw = work.sb("raw", [P, 4, D])
        self.sumsq_f = work.sb("sumsq_f", [P, KT])
        self.rms_f = work.sb("rms_f", [P, KT])
        self.sumsq_k = work.sb("sumsq_k", [P, KT])
        self.rms_k = work.sb("rms_k", [P, KT])
        self.rstd_k = work.sb("rstd_k", [P, KT])
        sem = work.sem
        self.loaded = sem("loaded")
        self.context_in = sem("context_in")
        self.ctx_in = [sem(f"ctx_in{i}") for i in range(2)]
        self.folded = sem("folded")
        self.squared_f = sem("squared_f")
        self.rms_f_ready = sem("rms_f_ready")
        self.rstd_f_ready = sem("rstd_f_ready")
        self.proj = sem("proj")
        self.biased = sem("biased")
        self.squared_k = sem("squared_k")
        self.rms_k_ready = sem("rms_k_ready")
        self.rstd_k_ready = sem("rstd_k_ready")
        self.scaled = sem("scaled")
        self.turned = sem("turned")
        self.kept = sem("kept")

    def made(self):
        self.core.memory.give_back(self.work.names)
        self.st.sems += self.work.sems
        self.st.ctx = self.work.ctx

    def issue(self, sp):
        sp.dma_start(self.w[:], self.a["L1x_w"][:, :, D:]).then_inc(self.loaded, 16)
        sp.dma_start(self.cols[:], self.a["L1x_cols"]).then_inc(self.loaded, 16)
        if self.load_context:
            sp.dma_start(self.core.ctx_t[:], self.a["ctx_t"]).then_inc(self.context_in, 16)
        sp.dma_start(self.row[:], self.a["L1x_rows"][:, D:2 * D].to_broadcast([P, D])).then_inc(self.loaded, 16)
        for j in range(NC):
            if j >= 2:
                sp.wait_ge(self.squared_f, 4 * j - 4)
            sp.dma_start(self.ctx[:, j % 2], self.a["L1x_ctx"][:, 4 * j:4 * j + 4, :]).then_inc(self.ctx_in[j % 2], 16)

    def tensor(self, pe, kt):
        if kt < KT:
            if kt == 0:
                pe.wait_ge(self.folded, CT)
                if self.load_context:
                    pe.wait_ge(self.context_in, 16)
            if kt >= 2:
                pe.wait_ge(self.biased, kt - 1)
            for c in range(CT):
                mm = pe.matmul(self.core.bank[5 + kt % 2][:], self.core.ctx_t[:, c, kt * P:(kt + 1) * P],
                               self.w[:, c, :], start=(c == 0), stop=(c == CT - 1))
            mm.then_inc(self.proj, 1)
        if kt >= 3:
            pe.wait_ge(self.scaled, kt - 2)
            if kt > 3:
                pe.wait_ge(self.kept, kt - 3)
            for c in range(CT):
                mm = pe.transpose(self.core.bank[7][:, c * P:(c + 1) * P], self.raw[:, (kt - 3) % 4, c * P:(c + 1) * P],
                                  self.core.ident[:])
            mm.then_inc(self.turned, 1)

    def scalar_context(self, act, j):
        act.wait_ge(self.ctx_in[j % 2], 16 * (j // 2) + 16)
        for kt in range(4 * j, 4 * j + 4):
            if kt > 0:
                act.wait_ge(self.squared_f, kt)
            act.activation(self.junk[:], self.ctx[:, j % 2, kt % 4, :], ACT.Square,
                           accum_out=self.sumsq_f[:, kt:kt + 1]).then_inc(self.squared_f, 1)
        act.wait_ge(self.squared_f, 4 * j + 4)
        act.activation(self.rms_f[:, 4 * j:4 * j + 4], self.sumsq_f[:, 4 * j:4 * j + 4], ACT.Sqrt,
                       bias=self.core.eps6[:], scale=1.0 / D).then_inc(self.rms_f_ready, 1)

    def scalar(self, act, kt):
        if kt < KT:
            act.wait_ge(self.biased, kt + 1)
            if kt > 0:
                act.wait_ge(self.squared_k, kt)
            else:
                act.wait_ge(self.squared_f, KT)
            act.activation(self.junk[:], self.raw[:, kt % 4, :], ACT.Square,
                           accum_out=self.sumsq_k[:, kt:kt + 1]).then_inc(self.squared_k, 1)
            act.wait_ge(self.squared_k, kt + 1)
            act.activation(self.rms_k[:, kt:kt + 1], self.sumsq_k[:, kt:kt + 1], ACT.Sqrt,
                           bias=self.core.eps6[:], scale=1.0 / D).then_inc(self.rms_k_ready, 1)
        if 1 <= kt <= KT:
            act.wait_ge(self.rstd_k_ready, kt)
            act.activation(self.raw[:, (kt - 1) % 4, :], self.raw[:, (kt - 1) % 4, :], ACT.Copy,
                           scale=self.rstd_k[:, kt - 1:kt]).then_inc(self.scaled, 1)
        if kt >= 3:
            act.wait_ge(self.turned, kt - 2)
            act.activation(self.k_t[:, kt - 3, :, :], self.core.bank[7][:].rearrange("p (c k) -> p c k", c=CT),
                           ACT.Copy).then_inc(self.kept, 1)

    def vector_start(self, dve):
        dve.wait_ge(self.loaded, 48)
        for c in range(CT):
            dve.tensor_scalar(self.w[:, c, :], self.w[:, c, :], self.cols[:, c:c + 1], None,
                              ALU.mult).then_inc(self.folded, 1)

    def vector(self, dve, kt):
        if kt % 4 == 0 and kt < KT:
            j = kt // 4
            dve.wait_ge(self.rms_f_ready, j + 1)
            dve.reciprocal(self.rstd_f[:, 4 * j:4 * j + 4], self.rms_f[:, 4 * j:4 * j + 4]).then_inc(self.rstd_f_ready, 1)
            dve.wait_ge(self.rstd_f_ready, j + 1)
        if kt < KT:
            dve.wait_ge(self.proj, kt + 1)
            if kt >= 4:
                dve.wait_ge(self.turned, kt - 3)
            dve.scalar_tensor_tensor(self.raw[:, kt % 4, :], self.core.bank[5 + kt % 2][:],
                                     self.rstd_f[:, kt:kt + 1], self.row[:], ALU.mult,
                                     ALU.add).then_inc(self.biased, 1)
        if 1 <= kt <= KT:
            dve.wait_ge(self.rms_k_ready, kt)
            dve.reciprocal(self.rstd_k[:, kt - 1:kt], self.rms_k[:, kt - 1:kt]).then_inc(self.rstd_k_ready, 1)


def context_keys_alone(core, keys):
    with core.nc.Block() as block:
        @block.sync
        def _(sp):
            keys.issue(sp)

        @block.tensor
        def _(pe):
            for kt in range(KT + 3):
                keys.tensor(pe, kt)

        @block.scalar
        def _(act):
            for j in range(NC):
                keys.scalar_context(act, j)
            for kt in range(KT + 3):
                keys.scalar(act, kt)

        @block.vector
        def _(dve):
            keys.vector_start(dve)
            for kt in range(KT + 1):
                keys.vector(dve, kt)


def per_token_head_attention(core, name, w_qkvo, rows, a):
    nc = core.nc
    H, E = 32, 16
    THRESH = 0.001
    PARTS = 16
    HP = H // PARTS
    with Stage(core, name) as st:
        load_context = core.hold_context()
        context_in = st.sem("context_in")
        w = st.sb("w", [P, CT, 4 * D])
        bias = st.sb("bias", [P, 4 * D])
        w_in = st.sem("w_in")
        bias_in = st.sem("bias_in")

        def issue(sp):
            for j in range(4):
                sp.dma_start(w[:, :, j * D:(j + 1) * D], w_qkvo[:, :, j * D:(j + 1) * D]).then_inc(w_in, 16)
            sp.dma_start(bias[:], rows.to_broadcast([P, 4 * D])).then_inc(bias_in, 16)
            if load_context:
                sp.dma_start(core.ctx_t[:], a["ctx_t"]).then_inc(context_in, 16)

        following = yield issue
        norm = LayerNorm(core, st, core.bank[0])
        core.keys = keys = ContextKeys(core, a)
        qkv = st.sb("qkv", [P, 3, D])
        prod = st.sb("prod", [P, HP * H * E])
        prod_pool = st.sb("prod_pool", [P, 2, HP * H * E])
        s_sb = st.sb("s", [P, H, H])
        keep = st.sb("keep", [P, H, H])
        top = st.sb("top", [P, H])
        total = st.sb("total", [P, H])
        r_total = st.sb("r_total", [P, H])
        o_sb = st.sb("o", [P, H, E])
        o_t = st.sb("o_t", [P, CT, P])
        qkv_ready = st.sem("qkv_ready")
        own = st.sem("own")
        qkv_biased = st.sem("qkv_biased")
        prod_ready = st.sem("prod_ready")
        pool_ready = st.sem("pool_ready")
        summed = st.sem("summed")
        shifted = st.sem("shifted")
        exp_ready = st.sem("exp_ready")
        kept = st.sem("kept")
        o_ready = st.sem("o_ready")
        o_turned = st.sem("o_turned")
        o_t_ready = st.sem("o_t_ready")
        out_ready = st.sem("out_ready")
        q = qkv[:, 0, :].rearrange("p (h e) -> p h e", h=H)
        k = qkv[:, 1, :].rearrange("p (g e) -> p g e", g=H)
        v = qkv[:, 2, :].rearrange("p (g e) -> p e g", g=H)

        def factors(phase, i):
            heads = slice(i * HP, (i + 1) * HP)
            left, right = (k, q[:, heads, :]) if phase == 0 else (v, s_sb[:, heads, :])
            shape = [P, HP, H, E] if phase == 0 else [P, HP, E, H]
            return shape, left.unsqueeze(1).to_broadcast(shape), right.unsqueeze(2).to_broadcast(shape)

        with nc.Block() as block:
            @block.gpsimd
            def _(pool):
                core.clear_stale(pool)
                for phase in range(2):
                    if phase == 0:
                        pool.wait_ge(qkv_biased, 3)
                    else:
                        pool.wait_ge(kept, 1)
                    for i in range(1, PARTS, 2):
                        n = phase * PARTS + i
                        if n >= 5:
                            pool.wait_ge(summed, n - 3)
                        shape, left, right = factors(phase, i)
                        view = prod_pool[:, (n // 2) % 2, :].rearrange("p (a b c) -> p a b c", a=shape[1], b=shape[2])
                        pool.tensor_tensor(view, left, right, ALU.mult).then_inc(pool_ready, 1)

            @block.sync
            def _(sp):
                keys.issue(sp)
                following(sp)

            @block.tensor
            def _(pe):
                norm.tensor(pe)
                pe.wait_ge(w_in, 64)
                for j in range(3):
                    for c in range(CT):
                        mm = pe.matmul(core.bank[j][:], core.xn_t[:, c, :], w[:, c, j * D:(j + 1) * D],
                                       start=(c == 0), stop=(c == CT - 1))
                    mm.then_inc(qkv_ready, 1)
                if load_context:
                    pe.wait_ge(context_in, 16)
                for kt in range(KT + 3):
                    keys.tensor(pe, kt)
                pe.wait_ge(o_ready, 1)
                o_flat = o_sb[:].rearrange("p h e -> p (h e)")
                for c in range(CT):
                    mm = pe.transpose(core.bank[3][:, c * P:(c + 1) * P], o_flat[:, c * P:(c + 1) * P],
                                      core.ident[:])
                mm.then_inc(o_turned, 1)
                pe.wait_ge(o_t_ready, 1)
                for c in range(CT):
                    mm = pe.matmul(core.bank[4][:], o_t[:, c, :], w[:, c, 3 * D:], start=(c == 0),
                                   stop=(c == CT - 1))
                mm.then_inc(out_ready, 1)

            @block.scalar
            def _(act):
                norm.scalar(act)
                for j in range(NC):
                    keys.scalar_context(act, j)
                for kt in range(KT + 3):
                    if kt == 8:
                        act.wait_ge(shifted, 1)
                        act.activation(s_sb[:], s_sb[:], ACT.Exp, scale=float(E ** -0.5)).then_inc(exp_ready, 1)
                    keys.scalar(act, kt)

            @block.vector
            def _(dve):
                norm.vector(dve)
                steps = Steps(dve, own)
                keys.vector_start(dve)
                dve.wait_ge(bias_in, 16)
                for j in range(3):
                    dve.wait_ge(qkv_ready, j + 1)
                    dve.tensor_tensor(qkv[:, j, :], core.bank[j][:], bias[:, j * D:(j + 1) * D],
                                      ALU.add).then_inc(qkv_biased, 1)
                dve.wait_ge(qkv_biased, 3)
                prods, tile = 0, 0

                def sum_parts(phase, dst):
                    nonlocal prods, tile
                    for i in range(PARTS):
                        n = phase * PARTS + i
                        shape, left, right = factors(phase, i)
                        split = dict(a=shape[1], b=shape[2])
                        if i % 2 == 0:
                            if n >= 2:
                                dve.wait_ge(summed, n - 1)
                            view = prod[:].rearrange("p (a b c) -> p a b c", **split)
                            dve.tensor_tensor(view, left, right, ALU.mult).then_inc(prod_ready, 1)
                            prods += 1
                            dve.wait_ge(prod_ready, prods)
                        else:
                            view = prod_pool[:, (n // 2) % 2, :].rearrange("p (a b c) -> p a b c", **split)
                            dve.wait_ge(pool_ready, n // 2 + 1)
                        dve.tensor_reduce(dst[:, i * HP:(i + 1) * HP, :], view, AX.X, ALU.add).then_inc(summed, 1)
                        if i % 2 and tile <= KT:
                            keys.vector(dve, tile)
                            tile += 1
                    dve.wait_ge(summed, (phase + 1) * PARTS)

                sum_parts(0, s_sb)
                dve.tensor_scalar(keep[:], s_sb[:], float(E ** -0.5), THRESH, ALU.mult, ALU.is_gt)
                steps.then(dve.tensor_reduce(top[:], s_sb[:], AX.X, ALU.max))
                dve.tensor_tensor(s_sb[:], s_sb[:], top[:].unsqueeze(2).to_broadcast([P, H, H]),
                                  ALU.subtract).then_inc(shifted, 1)
                dve.wait_ge(exp_ready, 1)
                dve.tensor_tensor(s_sb[:], s_sb[:], keep[:], ALU.mult).then_inc(kept, 1)
                dve.wait_ge(kept, 1)
                steps.then(dve.tensor_reduce(total[:], s_sb[:], AX.X, ALU.add))
                steps.then(dve.reciprocal(r_total[:], total[:]))
                sum_parts(1, o_sb)
                dve.tensor_tensor(o_sb[:], o_sb[:], r_total[:].unsqueeze(2).to_broadcast([P, H, E]),
                                  ALU.mult).then_inc(o_ready, 1)
                while tile <= KT:
                    keys.vector(dve, tile)
                    tile += 1
                steps.then(dve.tensor_tensor(core.x[:], core.x[:], bias[:, 3 * D:], ALU.add))
                dve.wait_ge(o_turned, 1)
                dve.tensor_copy(o_t[:], core.bank[3][:].rearrange("p (c q) -> p c q", c=CT)).then_inc(o_t_ready, 1)
                dve.wait_ge(out_ready, 1)
                dve.tensor_tensor(core.x[:], core.x[:], core.bank[4][:], ALU.add)
        keys.made()


def adapter_ffn(core, name, w_in_dram, rows, up_dram, adapters, rank, gate=False, starts=None,
                clamp_iota=None):
    nc = core.nc
    R = adapters * rank
    WIDE = R + (adapters if gate else 0)
    with Stage(core, name) as st:
        w = st.sb("w", [P, CT, D + WIDE])
        bias = st.sb("bias", [P, D])
        up = st.sb("up", [R, D])
        iota = st.sb("iota", [P, adapters])
        start_rows = st.sb("starts", [P, 4], I32)
        w_in = st.sem("w_in")
        rows_in = st.sem("rows_in")

        def issue(sp):
            sp.dma_start(w[:], w_in_dram).then_inc(w_in, 16)
            sp.dma_start(up[:], up_dram).then_inc(w_in, 16)
            sp.dma_start(bias[:], rows.to_broadcast([P, D])).then_inc(rows_in, 16)
            sp.dma_start(iota[:], clamp_iota.to_broadcast([P, adapters])).then_inc(rows_in, 16)
            if starts is not None:
                sp.dma_start(start_rows[:], starts.to_broadcast([P, 4])).then_inc(rows_in, 16)

        following = yield issue
        norm = LayerNorm(core, st, core.bank[0])
        low = st.sb("low", [P, WIDE])
        coef = st.sb("coef", [P, adapters])
        first = st.sb("first", [P, adapters])
        second = st.sb("second", [P, adapters])
        rest = st.sb("rest", [P, adapters])
        scal = st.sb("scal", [P, 8])
        low_c = st.sb("low_c", [P, R])
        low_t = st.sb("low_t", [R, P])
        reached = st.sb("reached", [P, 4])
        own = st.sem("own")
        low_ready = st.sem("low_ready")
        scaled = st.sem("scaled")
        turned = st.sem("turned")
        low_t_ready = st.sem("low_t_ready")
        out_ready = st.sem("out_ready")
        gap_ready = st.sem("gap_ready")
        gap_exp = st.sem("gap_exp")
        with nc.Block() as block:
            @block.gpsimd
            def _(pool):
                core.clear_stale(pool)

            @block.sync
            def _(sp):
                following(sp)

            @block.tensor
            def _(pe):
                norm.tensor(pe)
                pe.wait_ge(w_in, 32)
                for c in range(CT):
                    mm = pe.matmul(core.bank[1][:, 0:WIDE], core.xn_t[:, c, :], w[:, c, D:],
                                   start=(c == 0), stop=(c == CT - 1))
                mm.then_inc(low_ready, 1)
                for c in range(CT):
                    pe.matmul(core.bank[0][:], core.xn_t[:, c, :], w[:, c, 0:D], start=(c == 0), stop=False)
                pe.wait_ge(scaled, 1)
                pe.transpose(core.bank[2][0:R, 0:P], low_c[:], core.ident[:]).then_inc(turned, 1)
                pe.wait_ge(low_t_ready, 1)
                pe.matmul(core.bank[0][:], low_t[:], up[:], start=False, stop=True).then_inc(out_ready, 1)

            @block.scalar
            def _(act):
                norm.scalar(act)
                if gate:
                    act.wait_ge(gap_ready, 1)
                    act.activation(scal[:, 3:4], scal[:, 2:3], ACT.Exp).then_inc(gap_exp, 1)

            @block.vector
            def _(dve):
                norm.vector(dve)
                steps = Steps(dve, own)
                dve.wait_ge(rows_in, 16 * (3 if starts is not None else 2))
                steps.then(dve.tensor_tensor(core.x[:], core.x[:], bias[:], ALU.add))
                if not gate:
                    steps.then(dve.tensor_scalar(reached[:], start_rows[:], 0.0, None, ALU.is_le))
                    steps.then(dve.tensor_reduce(scal[:, 0:1], reached[:], AX.X, ALU.add))
                    steps.then(dve.tensor_scalar(scal[:, 1:2], scal[:, 0:1], 2.0, 0.0, ALU.subtract, ALU.max))
                    steps.then(dve.tensor_scalar(scal[:, 2:3], scal[:, 1:2], float(adapters - 1), None, ALU.min))
                    steps.then(dve.tensor_scalar(scal[:, 3:4], scal[:, 0:1], 1.5, None, ALU.is_gt))
                    steps.then(dve.tensor_scalar(coef[:], iota[:], scal[:, 2:3], scal[:, 3:4],
                                                 ALU.is_equal, ALU.mult))
                    dve.wait_ge(low_ready, 1)
                    source = core.bank[1][:, 0:R]
                else:
                    dve.wait_ge(low_ready, 1)
                    steps.then(dve.tensor_copy(low[:], core.bank[1][:, 0:WIDE]))
                    logits = low[:, R:]

                    def pick(dst, values, peak):
                        steps.then(dve.tensor_reduce(peak, values, AX.X, ALU.max))
                        steps.then(dve.tensor_scalar(dst, values, peak, float(adapters), ALU.not_equal, ALU.mult))
                        steps.then(dve.tensor_tensor(dst, dst, iota[:], ALU.add))
                        steps.then(dve.tensor_reduce(scal[:, 6:7], dst, AX.X, ALU.min))
                        steps.then(dve.tensor_scalar(dst, iota[:], scal[:, 6:7], None, ALU.is_equal))

                    pick(first[:], logits, scal[:, 0:1])
                    steps.then(dve.scalar_tensor_tensor(rest[:], first[:], LOWEST, logits, ALU.mult, ALU.add))
                    pick(second[:], rest[:], scal[:, 1:2])
                    dve.tensor_tensor(scal[:, 2:3], scal[:, 1:2], scal[:, 0:1], ALU.subtract).then_inc(gap_ready, 1)
                    dve.wait_ge(gap_exp, 1)
                    steps.then(dve.tensor_scalar(scal[:, 4:5], scal[:, 3:4], 1.0, 0.5, ALU.add, ALU.mult))
                    steps.then(dve.reciprocal(scal[:, 5:6], scal[:, 4:5]))
                    steps.then(dve.tensor_scalar(coef[:], second[:], scal[:, 3:4], None, ALU.mult))
                    steps.then(dve.tensor_tensor(coef[:], coef[:], first[:], ALU.add))
                    steps.then(dve.tensor_scalar(coef[:], coef[:], scal[:, 5:6], None, ALU.mult))
                    source = low[:, 0:R]
                dve.tensor_tensor(low_c[:].rearrange("p (a r) -> p a r", a=adapters),
                                  source.rearrange("p (a r) -> p a r", a=adapters),
                                  coef[:].unsqueeze(2).to_broadcast([P, adapters, rank]),
                                  ALU.mult).then_inc(scaled, 1)
                dve.wait_ge(turned, 1)
                dve.tensor_copy(low_t[:], core.bank[2][0:R, 0:P]).then_inc(low_t_ready, 1)
                dve.wait_ge(out_ready, 1)
                dve.tensor_tensor(core.x[:], core.x[:], core.bank[0][:], ALU.add)


def mixed_adapter_ffn(core, name, w_dram, keys_dram, up_dram):
    nc = core.nc
    A = 8
    with Stage(core, name) as st:
        w = st.sb("w", [P, CT, 2 * D + P])
        keys = st.sb("keys", [P, A])
        up = st.sb("up", [P, CT, D])
        w_in = st.sem("w_in")

        def issue(sp):
            sp.dma_start(w[:], w_dram).then_inc(w_in, 16)
            sp.dma_start(keys[:], keys_dram).then_inc(w_in, 16)
            sp.dma_start(up[:], up_dram).then_inc(w_in, 16)

        following = yield issue
        norm = LayerNorm(core, st, core.bank[0])
        mean = st.sb("mean", [P, CT])
        q_wide = st.sb("q_wide", [P, P])
        coef = st.sb("coef", [P, A])
        coef_col = st.sb("coef_col", [P, CT])
        scal = st.sb("scal", [P, 4])
        h_t = st.sb("h_t", [P, CT, P])
        own = st.sem("own")
        mean_ready = st.sem("mean_ready")
        q_ready = st.sem("q_ready")
        q_wide_ready = st.sem("q_wide_ready")
        scores_ready = st.sem("scores_ready")
        top_ready = st.sem("top_ready")
        exp_ready = st.sem("exp_ready")
        h_ready = st.sem("h_ready")
        h_scaled = st.sem("h_scaled")
        out_ready = st.sem("out_ready")
        with nc.Block() as block:
            @block.gpsimd
            def _(pool):
                core.clear_stale(pool)

            @block.sync
            def _(sp):
                following(sp)

            @block.tensor
            def _(pe):
                norm.tensor(pe)
                pe.wait_ge(w_in, 48)
                pe.wait_ge(mean_ready, 1)
                for c in range(CT):
                    mm = pe.matmul(core.bank[1][:, 0:1], w[:, c, 2 * D:], mean[:, c:c + 1], start=(c == 0),
                                   stop=(c == CT - 1))
                mm.then_inc(q_ready, 1)
                for t in range(CT):
                    for c in range(CT):
                        mm = pe.matmul(core.bank[3][:, t * P:(t + 1) * P], w[:, c, D + t * P:D + (t + 1) * P],
                                       core.xn_t[:, c, :], start=(c == 0), stop=(c == CT - 1))
                mm.then_inc(h_ready, 1)
                pe.wait_ge(q_wide_ready, 1)
                pe.matmul(core.bank[2][:, 0:A], q_wide[:], keys[:], start=True, stop=True).then_inc(scores_ready, 1)
                for c in range(CT):
                    pe.matmul(core.bank[0][:], core.xn_t[:, c, :], w[:, c, 0:D], start=(c == 0), stop=False)
                pe.wait_ge(h_scaled, CT)
                for t in range(CT):
                    mm = pe.matmul(core.bank[0][:], h_t[:, t, :], up[:, t, :], start=False, stop=(t == CT - 1))
                mm.then_inc(out_ready, 1)

            @block.scalar
            def _(act):
                norm.scalar(act)
                act.wait_ge(top_ready, 1)
                act.activation(coef[:], core.bank[2][:, 0:A], ACT.Exp, bias=scal[:, 1:2],
                               scale=float(P ** -0.5), accum_out=scal[:, 2:3]).then_inc(exp_ready, 1)

            @block.vector
            def _(dve):
                norm.vector(dve)
                steps = Steps(dve, own)
                dve.wait_ge(norm.ready, 1)
                steps.then(dve.tensor_reduce(mean[:], core.xn_t[:], AX.X, ALU.add))
                dve.tensor_scalar(mean[:], mean[:], 1.0 / P, None, ALU.mult).then_inc(mean_ready, 1)
                dve.wait_ge(q_ready, 1)
                steps.then(dve.tensor_copy(scal[:, 3:4], core.bank[1][:, 0:1]))
                dve.tensor_scalar(q_wide[:], core.ones[:], scal[:, 3:4], None, ALU.mult).then_inc(q_wide_ready, 1)
                dve.wait_ge(scores_ready, 1)
                steps.then(dve.tensor_reduce(scal[:, 0:1], core.bank[2][:, 0:A], AX.X, ALU.max, negate=True))
                dve.tensor_scalar(scal[:, 1:2], scal[:, 0:1], float(P ** -0.5), None, ALU.mult).then_inc(top_ready, 1)
                dve.wait_ge(exp_ready, 1)
                steps.then(dve.reciprocal(scal[:, 0:1], scal[:, 2:3]))
                steps.then(dve.tensor_scalar(coef[:], coef[:], scal[:, 0:1], None, ALU.mult))
                steps.then(dve.tensor_copy(coef_col[0:64, :], coef[0:64, 0:A:2]))
                steps.then(dve.tensor_copy(coef_col[64:128, :], coef[64:128, 1:A:2]))
                dve.wait_ge(h_ready, 1)
                for t in range(CT):
                    dve.tensor_scalar(h_t[:, t, :], core.bank[3][:, t * P:(t + 1) * P], coef_col[:, t:t + 1],
                                      None, ALU.mult).then_inc(h_scaled, 1)
                dve.wait_ge(out_ready, 1)
                dve.tensor_tensor(core.x[:], core.x[:], core.bank[0][:], ALU.add)


def single_head_attention(core, name, wqkv, wo, qk_cols, rows):
    nc = core.nc
    SCALE = float(HD ** -0.5)
    with Stage(core, name) as st:
        w = st.sb("w", [P, CT, 3 * HD])
        w_o = st.sb("w_o", [P, D])
        cols = st.sb("cols", [P, 2])
        bias = st.sb("bias", [P, HD + D])
        w_in = st.sem("w_in")
        rows_in = st.sem("rows_in")

        def issue(sp):
            sp.dma_start(w[:], wqkv).then_inc(w_in, 16)
            sp.dma_start(w_o[:], wo).then_inc(w_in, 16)
            sp.dma_start(cols[:], qk_cols).then_inc(rows_in, 16)
            sp.dma_start(bias[:], rows.to_broadcast([P, HD + D])).then_inc(rows_in, 16)

        following = yield issue
        norm = LayerNorm(core, st, core.bank[0])
        qk_t = st.sb("qk_t", [P, 2, P])
        v_sb = st.sb("v", [P, HD])
        p_sb = st.sb("p", [P, P])
        p_t = st.sb("p_t", [P, P])
        o_t = st.sb("o_t", [P, P])
        scal = st.sb("scal", [P, 4])
        own = st.sem("own")
        qk_ready = st.sem("qk_ready")
        v_ready = st.sem("v_ready")
        qk_biased = st.sem("qk_biased")
        v_biased = st.sem("v_biased")
        s_ready = st.sem("s_ready")
        top_ready = st.sem("top_ready")
        exp_ready = st.sem("exp_ready")
        p_ready = st.sem("p_ready")
        p_turned = st.sem("p_turned")
        p_t_ready = st.sem("p_t_ready")
        o_ready = st.sem("o_ready")
        o_t_ready = st.sem("o_t_ready")
        out_ready = st.sem("out_ready")
        with nc.Block() as block:
            @block.gpsimd
            def _(pool):
                core.clear_stale(pool)

            @block.sync
            def _(sp):
                following(sp)

            @block.tensor
            def _(pe):
                norm.tensor(pe)
                pe.wait_ge(w_in, 32)
                for j in range(2):
                    for c in range(CT):
                        mm = pe.matmul(core.bank[0][:, j * P:(j + 1) * P], w[:, c, j * HD:(j + 1) * HD],
                                       core.xn_t[:, c, :], start=(c == 0), stop=(c == CT - 1))
                mm.then_inc(qk_ready, 1)
                for c in range(CT):
                    mm = pe.matmul(core.bank[1][:, 0:HD], core.xn_t[:, c, :], w[:, c, 2 * HD:], start=(c == 0),
                                   stop=(c == CT - 1))
                mm.then_inc(v_ready, 1)
                pe.wait_ge(qk_biased, 2)
                pe.matmul(core.bank[2][:, 0:P], qk_t[:, 0, :], qk_t[:, 1, :], start=True,
                          stop=True).then_inc(s_ready, 1)
                pe.wait_ge(p_ready, 1)
                pe.transpose(core.bank[3][:, 0:P], p_sb[:], core.ident[:]).then_inc(p_turned, 1)
                pe.wait_ge(p_t_ready, 1)
                pe.wait_ge(v_biased, 1)
                pe.matmul(core.bank[4][:, 0:P], v_sb[:], p_t[:], start=True, stop=True).then_inc(o_ready, 1)
                pe.wait_ge(o_t_ready, 1)
                pe.matmul(core.bank[5][:], o_t[:], w_o[:], start=True, stop=True).then_inc(out_ready, 1)

            @block.scalar
            def _(act):
                norm.scalar(act)
                act.wait_ge(top_ready, 1)
                act.activation(p_sb[:], core.bank[2][:, 0:P], ACT.Exp, bias=scal[:, 1:2], scale=SCALE,
                               accum_out=scal[:, 2:3]).then_inc(exp_ready, 1)

            @block.vector
            def _(dve):
                norm.vector(dve)
                steps = Steps(dve, own)
                dve.wait_ge(rows_in, 32)
                steps.then(dve.tensor_tensor(core.x[:], core.x[:], bias[:, HD:], ALU.add))
                dve.wait_ge(qk_ready, 1)
                for j in range(2):
                    dve.tensor_scalar(qk_t[:, j, :], core.bank[0][:, j * P:(j + 1) * P], cols[:, j:j + 1], None,
                                      ALU.add).then_inc(qk_biased, 1)
                dve.wait_ge(v_ready, 1)
                dve.tensor_tensor(v_sb[:], core.bank[1][:, 0:HD], bias[:, 0:HD], ALU.add).then_inc(v_biased, 1)
                dve.wait_ge(s_ready, 1)
                steps.then(dve.tensor_reduce(scal[:, 0:1], core.bank[2][:, 0:P], AX.X, ALU.max, negate=True))
                dve.tensor_scalar(scal[:, 1:2], scal[:, 0:1], SCALE, None, ALU.mult).then_inc(top_ready, 1)
                dve.wait_ge(exp_ready, 1)
                steps.then(dve.reciprocal(scal[:, 3:4], scal[:, 2:3]))
                dve.tensor_scalar(p_sb[:], p_sb[:], scal[:, 3:4], None, ALU.mult).then_inc(p_ready, 1)
                dve.wait_ge(p_turned, 1)
                dve.tensor_copy(p_t[:], core.bank[3][:, 0:P]).then_inc(p_t_ready, 1)
                dve.wait_ge(o_ready, 1)
                dve.tensor_copy(o_t[:], core.bank[4][:, 0:P]).then_inc(o_t_ready, 1)
                dve.wait_ge(out_ready, 1)
                dve.tensor_tensor(core.x[:], core.x[:], core.bank[5][:], ALU.add)


def codebook_ffn(core, name, books, codes, entry, rows):
    nc = core.nc
    N = 32
    BG = 8
    with Stage(core, name) as st:
        books_sb = st.sb("books", [P, BG, P])
        codes_sb = st.sb("codes", [P, BG, D + N], I32)
        entry_sb = st.sb("entry", [P, 1])
        bias = st.sb("bias", [P, D + N])
        loaded = st.sem("loaded")

        def issue(sp):
            sp.dma_start(books_sb[:], books).then_inc(loaded, 16)
            sp.dma_start(codes_sb[:], codes).then_inc(loaded, 16)
            sp.dma_start(entry_sb[:], entry).then_inc(loaded, 16)
            sp.dma_start(bias[:], rows.to_broadcast([P, D + N])).then_inc(loaded, 16)

        following = yield issue
        norm = LayerNorm(core, st, core.bank[7])
        hot = st.sb("hot", [P, BG, D + N])
        w_t = st.sb("w_t", [P, CT, D + N])
        dots = st.sb("dots", [P, N])
        stats = st.sb("stats", [P, 6])
        mean_var = st.sb("mean_var", [P, 2])
        scal = st.sb("scal", [P, 8])
        taken = st.sb("taken", [P, N])
        k_mask = st.sb("k_mask", [P, N])
        y_sb = st.sb("y", [P, D])
        own = st.sem("own")
        hot_ready = st.sem("hot_ready")
        w_ready = st.sem("w_ready")
        w_copied = st.sem("w_copied")
        c_copied = st.sem("c_copied")
        dots_ready = st.sem("dots_ready")
        y_ready = st.sem("y_ready")
        var_ready = st.sem("var_ready")
        std_ready = st.sem("std_ready")
        top_ready = st.sem("top_ready")
        exp_ready = st.sem("exp_ready")
        taken_ready = st.sem("taken_ready")
        count_ready = st.sem("count_ready")
        with nc.Block() as block:
            @block.gpsimd
            def _(pool):
                core.clear_stale(pool)

            @block.sync
            def _(sp):
                following(sp)

            @block.tensor
            def _(pe):
                norm.tensor(pe)
                for t in range(CT):
                    pe.wait_ge(hot_ready, 2 * t + 2)
                    big, small = core.bank[t % 2], core.bank[2 + t % 2]
                    if t >= 2:
                        pe.wait_ge(w_copied, t - 1)
                        pe.wait_ge(c_copied, t - 1)
                    for j in range(2):
                        pe.matmul(big[:], books_sb[:, 2 * t + j, :], hot[:, 2 * t + j, 0:D], start=(j == 0),
                                  stop=(j == 1))
                    for j in range(2):
                        mm = pe.matmul(small[:, 0:N], books_sb[:, 2 * t + j, :], hot[:, 2 * t + j, D:],
                                       start=(j == 0), stop=(j == 1))
                    mm.then_inc(w_ready, 1)
                pe.wait_ge(w_copied, CT)
                pe.wait_ge(c_copied, CT)
                for c in range(CT):
                    mm = pe.matmul(core.bank[4][:, 0:N], core.xn_t[:, c, :], w_t[:, c, D:], start=(c == 0),
                                   stop=(c == CT - 1))
                mm.then_inc(dots_ready, 1)
                for c in range(CT):
                    mm = pe.matmul(core.bank[5][:], core.xn_t[:, c, :], w_t[:, c, 0:D], start=(c == 0),
                                   stop=(c == CT - 1))
                mm.then_inc(y_ready, 1)
                pe.wait_ge(taken_ready, 1)
                pe.matmul(core.bank[6][:, 0:N], core.ones[:], taken[:], start=True, stop=True).then_inc(count_ready, 1)

            @block.scalar
            def _(act):
                norm.scalar(act)
                for t in range(CT):
                    act.wait_ge(w_ready, t + 1)
                    act.activation(w_t[:, t, 0:D], core.bank[t % 2][:], ACT.Copy).then_inc(w_copied, 1)
                    act.activation(w_t[:, t, D:], core.bank[2 + t % 2][:, 0:N], ACT.Copy).then_inc(c_copied, 1)
                act.wait_ge(var_ready, 1)
                act.activation(scal[:, 1:2], scal[:, 0:1], ACT.Sqrt).then_inc(std_ready, 1)
                act.wait_ge(top_ready, 1)
                act.activation(dots[:], dots[:], ACT.Exp, bias=scal[:, 3:4], scale=1.0,
                               accum_out=scal[:, 4:5]).then_inc(exp_ready, 1)

            @block.vector
            def _(dve):
                norm.vector(dve)
                steps = Steps(dve, own)
                dve.wait_ge(loaded, 64)
                for j in range(BG):
                    dve.tensor_scalar(hot[:, j, :], codes_sb[:, j, :], entry_sb[:], None,
                                      ALU.is_equal).then_inc(hot_ready, 1)
                dve.wait_ge(dots_ready, 1)
                steps.then(dve.bn_stats(stats[:], core.bank[4][:, 0:N]))
                steps.then(dve.bn_aggr(mean_var[:], stats[:]))
                dve.tensor_scalar(scal[:, 0:1], mean_var[:, 1:2], 1e-5, None, ALU.add).then_inc(var_ready, 1)
                dve.wait_ge(std_ready, 1)
                steps.then(dve.reciprocal(scal[:, 2:3], scal[:, 1:2]))
                steps.then(dve.tensor_scalar(dots[:], core.bank[4][:, 0:N], mean_var[:, 0:1], scal[:, 2:3],
                                             ALU.subtract, ALU.mult))
                steps.then(dve.tensor_tensor(dots[:], dots[:], bias[:, D:], ALU.mult))
                dve.tensor_reduce(scal[:, 3:4], dots[:], AX.X, ALU.max, negate=True).then_inc(top_ready, 1)
                dve.wait_ge(y_ready, 1)
                steps.then(dve.tensor_tensor(y_sb[:], core.bank[5][:], bias[:, 0:D], ALU.add))
                dve.wait_ge(exp_ready, 1)
                steps.then(dve.reciprocal(scal[:, 5:6], scal[:, 4:5]))
                dve.tensor_scalar(taken[:], dots[:], scal[:, 5:6], 0.5, ALU.mult, ALU.is_gt).then_inc(taken_ready, 1)
                dve.wait_ge(taken_ready, 1)
                steps.then(dve.tensor_reduce(scal[:, 6:7], taken[:], AX.X, ALU.max))
                dve.wait_ge(count_ready, 1)
                steps.then(dve.tensor_scalar(k_mask[:], core.bank[6][:, 0:N], 0.5, scal[:, 6:7], ALU.is_gt,
                                             ALU.mult))
                steps.then(dve.tensor_tensor(y_sb[:].rearrange("p (n o) -> p n o", n=N),
                                             y_sb[:].rearrange("p (n o) -> p n o", n=N),
                                             k_mask[:].unsqueeze(2).to_broadcast([P, N, D // N]), ALU.mult))
                dve.tensor_tensor(core.x[:], core.x[:], y_sb[:], ALU.add)


def feature_cross_attention(core, name, a):
    nc = core.nc
    with Stage(core, name) as st:
        w = st.sb("w", [P, CT, D])
        ctx_sb = st.sb("ctx", [P, KT, D])
        row_sb = st.sb("rows", [P, 5, D])
        w_in = st.sem("w_in")
        ctx_in = st.sem("ctx_in")
        rows_in = st.sem("rows_in")

        def issue(sp):
            sp.dma_start(w[:], a["L1x_w"][:, :, 0:D]).then_inc(w_in, 16)
            sp.dma_start(row_sb[:].rearrange("p r f -> p (r f)"), a["L1x_rows"].to_broadcast([P, 5 * D])).then_inc(rows_in, 16)
            sp.dma_start(ctx_sb[:], a["L1x_ctx"]).then_inc(ctx_in, 16)

        following = yield issue
        if core.keys is None:
            core.keys = ContextKeys(core, a)
            context_keys_alone(core, core.keys)
            core.keys.made()
        keys, k_t, rstd_f = core.keys, core.keys.k_t, core.keys.rstd_f
        norm = LayerNorm(core, st, core.bank[0])
        junk = st.sb("junk", [P, D])
        sumsq_q = st.sb("sumsq_q", [P, 1])
        rstd_q = st.sb("rstd_q", [P, 1])
        q_sb = st.sb("q", [P, D])
        q_t = st.sb("q_t", [P, CT, P])
        s_sb = st.sb("s", [P, SK])
        part_max = st.sb("part_max", [P, NC])
        neg_max = st.sb("neg_max", [P, 1])
        row_sum = st.sb("row_sum", [P, NC])
        r_sum = st.sb("r_sum", [P, 2])
        p_t = st.sb("p_t", [P, KT, P])
        o_sb = st.sb("o", [P, D])
        own = st.sem("own")
        q_proj = st.sem("q_proj")
        q_biased = st.sem("q_biased")
        q_squared = st.sem("q_squared")
        rms_q = st.sem("rms_q")
        q_ready = st.sem("q_ready")
        q_turned = st.sem("q_turned")
        q_t_ready = st.sem("q_t_ready")
        s_ready = st.sem("s_ready")
        max_ready = st.sem("max_ready")
        exp_ready = st.sem("exp_ready")
        p_turned = st.sem("p_turned")
        p_t_dve = st.sem("p_t_dve")
        p_t_act = st.sem("p_t_act")
        o_ready = st.sem("o_ready")
        with nc.Block() as block:
            @block.gpsimd
            def _(pool):
                core.clear_stale(pool)

            @block.sync
            def _(sp):
                following(sp)

            @block.tensor
            def _(pe):
                norm.tensor(pe)
                pe.wait_ge(w_in, 16)
                for c in range(CT):
                    mm = pe.matmul(core.bank[2][:], core.xn_t[:, c, :], w[:, c, :], start=(c == 0),
                                   stop=(c == CT - 1))
                mm.then_inc(q_proj, 1)
                pe.wait_ge(q_ready, 1)
                for c in range(CT):
                    mm = pe.transpose(core.bank[3][:, c * P:(c + 1) * P], q_sb[:, c * P:(c + 1) * P], core.ident[:])
                mm.then_inc(q_turned, 1)
                pe.wait_ge(q_t_ready, 1)
                for j in range(NC):
                    for c in range(CT):
                        mm = pe.matmul(core.bank[4 + j][:].rearrange("p (t k) -> p t k", t=4), q_t[:, c, :],
                                       k_t[:, 4 * j:4 * j + 4, c, :], start=(c == 0), stop=(c == CT - 1))
                    mm.then_inc(s_ready, 1)
                for j in range(NC):
                    pe.wait_ge(exp_ready, j + 1)
                    for i in range(4):
                        kt = 4 * j + i
                        mm = pe.transpose(core.bank[j][:, i * P:(i + 1) * P], s_sb[:, kt * P:(kt + 1) * P],
                                          core.ident[:])
                    mm.then_inc(p_turned, 1)
                pe.wait_ge(ctx_in, 16)
                for kt in range(KT):
                    pe.wait_ge(p_t_dve if kt // 4 % 2 else p_t_act, kt // 8 * 4 + kt % 4 + 1)
                    mm = pe.matmul(core.bank[4][:], p_t[:, kt, :], ctx_sb[:, kt, :], start=(kt == 0),
                                   stop=(kt == KT - 1))
                mm.then_inc(o_ready, 1)

            @block.scalar
            def _(act):
                norm.scalar(act)
                act.wait_ge(q_biased, 1)
                act.activation(junk[:], q_sb[:], ACT.Square, accum_out=sumsq_q[:]).then_inc(q_squared, 1)
                act.wait_ge(q_squared, 1)
                act.activation(rstd_q[:], sumsq_q[:], ACT.Sqrt, bias=core.eps6[:], scale=1.0 / D).then_inc(rms_q, 1)
                act.wait_ge(max_ready, 1)
                for j in range(NC):
                    act.activation(s_sb[:, j * 512:(j + 1) * 512], core.bank[4 + j][:], ACT.Exp, bias=neg_max[:],
                                   scale=1.0, accum_out=row_sum[:, j:j + 1]).then_inc(exp_ready, 1)
                for j in range(0, NC, 2):
                    act.wait_ge(p_turned, j + 1)
                    for kt in range(4 * j, 4 * j + 4):
                        act.activation(p_t[:, kt, :], core.bank[j][:, (kt % 4) * P:(kt % 4 + 1) * P],
                                       ACT.Copy, scale=rstd_f[:, kt:kt + 1]).then_inc(p_t_act, 1)

            @block.vector
            def _(dve):
                norm.vector(dve)
                steps = Steps(dve, own)
                dve.wait_ge(rows_in, 16)
                steps.then(dve.scalar_tensor_tensor(row_sb[:, 2, :], row_sb[:, 2, :], float(D ** -0.5),
                                                    row_sb[:, 3, :], ALU.mult, ALU.mult))
                dve.wait_ge(q_proj, 1)
                dve.tensor_tensor(q_sb[:], core.bank[2][:], row_sb[:, 0, :], ALU.add).then_inc(q_biased, 1)
                dve.wait_ge(rms_q, 1)
                steps.then(dve.reciprocal(rstd_q[:], rstd_q[:]))
                dve.scalar_tensor_tensor(q_sb[:], q_sb[:], rstd_q[:], row_sb[:, 2, :], ALU.mult,
                                         ALU.mult).then_inc(q_ready, 1)
                dve.wait_ge(q_turned, 1)
                dve.tensor_copy(q_t[:], core.bank[3][:].rearrange("p (c q) -> p c q", c=CT)).then_inc(q_t_ready, 1)
                for j in range(NC):
                    dve.wait_ge(s_ready, j + 1)
                    steps.then(dve.tensor_reduce(part_max[:, j:j + 1], core.bank[4 + j][:], AX.X, ALU.max))
                dve.tensor_reduce(neg_max[:], part_max[:], AX.X, ALU.max, negate=True).then_inc(max_ready, 1)
                for j in range(1, NC, 2):
                    dve.wait_ge(p_turned, j + 1)
                    for kt in range(4 * j, 4 * j + 4):
                        dve.tensor_scalar(p_t[:, kt, :], core.bank[j][:, (kt % 4) * P:(kt % 4 + 1) * P],
                                          rstd_f[:, kt:kt + 1], None, ALU.mult).then_inc(p_t_dve, 1)
                dve.wait_ge(exp_ready, NC)
                steps.then(dve.tensor_reduce(r_sum[:, 0:1], row_sum[:], AX.X, ALU.add))
                steps.then(dve.reciprocal(r_sum[:, 1:2], r_sum[:, 0:1]))
                dve.wait_ge(o_ready, 1)
                steps.then(dve.scalar_tensor_tensor(o_sb[:], core.bank[4][:], r_sum[:, 1:2], row_sb[:, 4, :],
                                                    ALU.mult, ALU.mult))
                dve.tensor_tensor(core.x[:], core.x[:], o_sb[:], ALU.add)
    core.end_with_last(keys.st)
    core.keys = None


def narrow_cross_attention(core, name, w_dram, w_out, mask_u8, ident_4, ctx_t):
    nc = core.nc
    E = 16
    OWN = 3 * E
    VW = 64
    LAG = 4
    MASKED = -float(2.0 ** 100)
    with Stage(core, name) as st:
        w = st.sb("w", [P, CT, 2 * P + D])
        w_o = st.sb("w_o", [P, CT, D])
        mask_b = st.sb("mask_b", [P, SK], U8)
        ident_in = st.sb("ident_in", [P, HG * P])
        w_in = st.sem("w_in")
        mask_in = st.sem("mask_in")

        def issue(sp):
            sp.dma_start(w[:], w_dram).then_inc(w_in, 16)
            sp.dma_start(mask_b[:], mask_u8).then_inc(mask_in, 16)
            sp.dma_start(ident_in[:], ident_4).then_inc(mask_in, 16)
            sp.dma_start(w_o[:], w_out).then_inc(w_in, 16)

        following = yield issue
        load_context = core.hold_context()
        norm = LayerNorm(core, st, core.bank[0])
        mask_sb = st.sb("mask", [P, SK], F32R)
        idents = st.sb("idents", [P, HG * P], F32R)
        k_hi = st.sb("k_hi", [P, SK], F32R)
        k_lo = st.sb("k_lo", [P, SK], F32R)
        q_hi = st.sb("q_hi", [P, HG * P], F32R)
        q_lo = st.sb("q_lo", [P, HG * P], F32R)
        v_hi = st.sb("v_hi", [P, KT, P], F32R)
        v_lo = st.sb("v_lo", [P, KT, P], F32R)
        k_st = [st.sb(f"k_st{b}", [P, SK], F32R) for b in range(2)]
        q_st = [st.sb(f"q_st{b}", [P, HG * P], F32R) for b in range(2)]
        v_st = [st.sb(f"v_st{b}", [P, KT, VW], F32R) for b in range(2)]
        junk = st.sb("junk", [P, 2, 512])
        part_max = st.sb("part_max", [P, HG, NC])
        neg_max = st.sb("neg_max", [P, HG])
        diag = st.sb("diag", [P, HG, P])
        o_st = [st.sb(f"o_st{b}", [VW, HG * P]) for b in range(2)]
        o_parts = st.sb("o_parts", [P, 3, HG * P])
        e_t = st.sb("e_t", [P, 4, HG * P])
        ctx = core.ctx_t
        core.drop_context()
        p_hi = st.sb("p_hi", [P, 8, HG * P], F32R)
        p_lo = st.sb("p_lo", [P, 8, HG * P], F32R)
        context_in = st.sem("context_in")
        stacks_blank = st.sem("stacks_blank")
        mask_ready = st.sem("mask_ready")
        k_proj = st.sem("k_proj")
        q_proj = st.sem("q_proj")
        v_proj = st.sem("v_proj")
        hi_kept = st.sem("hi_kept")
        lo_kept = st.sem("lo_kept")
        kq_in = [st.sem(f"kq_in{b}") for b in range(2)]
        v_kept = st.sem("v_kept")
        s_ready = st.sem("s_ready")
        s_seen = st.sem("s_seen")
        s_read = st.sem("s_read")
        max_ready = st.sem("max_ready")
        diag_ready = st.sem("diag_ready")
        m_ready = st.sem("m_ready")
        m_hi_kept = st.sem("m_hi_kept")
        m_kept = st.sem("m_kept")
        st_ready = st.sem("st_ready")
        exp_done = st.sem("exp_done")
        hi_ready = st.sem("hi_ready")
        lo_ready = [st.sem("lo_ready_even"), st.sem("lo_ready_odd")]
        pv_done = st.sem("pv_done")
        o_kept = st.sem("o_kept")
        o_in = [st.sem(f"o_in{b}") for b in range(2)]
        own = st.sem("own")
        out_ready = st.sem("out_ready")
        k_bank = lambda n: core.bank[1 + n]
        v_bank = lambda n: core.bank[(6, 7, 0, 1)[n]]
        st_bank = lambda j: core.bank[j % 4]
        s_bank = lambda n: core.bank[4 + n % 2]
        out_bank = lambda b: core.bank[6 + b]
        per_head = lambda t: t[:].rearrange("p (h q) -> p h q", h=HG)
        chunks_at = lambda j: range(min(16, max(0, j - 3) * 5 // 4), min(16, max(0, j - 2) * 5 // 4))
        bits = lambda t: t.bitcast(F32)

        with nc.Block() as block:
            @block.gpsimd
            def _(pool):
                core.clear_stale(pool)
                for b in range(2):
                    pool.memset(bits(k_st[b][:]), 1.0 / 32)
                    pool.memset(bits(q_st[b][:]), 0.0)
                    pool.memset(bits(v_st[b][:]), 1.0).then_inc(stacks_blank, 1)
                with pool.Fori(0, NG) as g:
                    for j in range(0, KT, 2):
                        pool.wait_ge(hi_ready, g * 16 + j + 1)
                        pool.tensor_tensor(p_lo[:, j % 8, :], e_t[:, j % 4, :], bits(p_hi[:, j % 8, :]),
                                           ALU.subtract).then_inc(lo_ready[0], 1)

            @block.sync
            def _(sp):
                if load_context:
                    sp.dma_start(ctx[:], ctx_t).then_inc(context_in, 16)
                following(sp)
                sp.wait_ge(stacks_blank, 2)
                sp.wait_ge(hi_kept, NC + 1)
                sp.wait_ge(lo_kept, NC + 1)
                for g in range(NG + 2):
                    if g < NG:
                        b, rows = g % 2, slice(g * E, (g + 1) * E)
                        if g >= 2:
                            sp.wait_ge(st_ready, (g - 1) * 16)
                        for i, (k, q) in enumerate(((k_hi, q_hi), (k_lo, q_hi), (k_hi, q_lo))):
                            sp.dma_start(bits(k_st[b][i * E:(i + 1) * E, :]), bits(k[rows, :])).then_inc(kq_in[b], 16)
                            sp.dma_start(bits(q_st[b][i * E:(i + 1) * E, :]), bits(q[rows, :])).then_inc(kq_in[b], 16)
                    if g >= 2:
                        sp.wait_ge(o_kept, g - 1)
                        for i in range(3):
                            sp.dma_start(o_parts[(g - 2) * E:(g - 1) * E, i, :],
                                         o_st[g % 2][i * E:(i + 1) * E, :]).then_inc(o_in[g % 2], 16)

            @block.tensor
            def _(pe):
                pe.wait_ge(w_in, 32)
                if load_context:
                    pe.wait_ge(context_in, 16)
                for n in range(NC):
                    for c in range(CT):
                        mm = pe.matmul(k_bank(n)[:], w[:, c, 0:P], ctx[:, c, n * 512:(n + 1) * 512],
                                       start=(c == 0), stop=(c == CT - 1))
                    mm.then_inc(k_proj, 1)
                norm.tensor(pe)
                for h in range(HG):
                    for c in range(CT):
                        mm = pe.matmul(core.bank[5][:, h * P:(h + 1) * P],
                                       w[:, c, 2 * P + h * P:2 * P + (h + 1) * P], core.xn_t[:, c, :],
                                       start=(c == 0), stop=(c == CT - 1))
                mm.then_inc(q_proj, 1)

                def project_v(n):
                    if n == 3:
                        pe.wait_ge(lo_kept, 1)
                    for j in range(4):
                        kt = 4 * n + j
                        for c in range(CT):
                            mm = pe.matmul(v_bank(n)[:, j * P:(j + 1) * P], ctx[:, c, kt * P:(kt + 1) * P],
                                           w[:, c, P:2 * P], start=(c == 0), stop=(c == CT - 1))
                    mm.then_inc(v_proj, 1)

                def score(g, b, n):
                    h, c = n // NC, n % NC
                    if not (isinstance(g, int) and n < 2):
                        pe.wait_ge(s_read, g * 16 + n - 1)
                    pe.matmul(s_bank(n)[:], q_st[b][0:64, h * P:(h + 1) * P], k_st[b][0:64, c * 512:(c + 1) * 512],
                              start=True, stop=True).then_inc(s_ready, 1)

                def spread_max(g):
                    pe.wait_ge(diag_ready, g * 4 + 4)
                    pe.matmul(core.bank[4][:], core.ones[:], diag[:].rearrange("p h q -> p (h q)"),
                              start=True, stop=True).then_inc(m_ready, 1)

                def weigh(g, b, j):
                    pe.wait_ge(lo_ready[j % 2], g * 8 + j // 2 + 1 + 2)
                    if j == 0:
                        pe.wait_ge(v_kept, g + 1)
                    for p in (p_hi, p_lo):
                        mm = pe.matmul(out_bank(b)[0:VW, :], v_st[b][:, j, :], p[:, j % 8, :],
                                       start=(j == 0 and p is p_hi), stop=(j == KT - 1 and p is p_lo))
                    mm.then_inc(pv_done, 1)

                def step(g, b, pair, before=True, this=True, after=True):
                    if this:
                        pe.wait_ge(m_kept, g + 1)
                    for j in range(KT if this else LAG):
                        if this:
                            pe.wait_ge(exp_done, g * 16 + j + 1)
                            keys = slice(j * P, (j + 1) * P)
                            pe.matmul(st_bank(j)[:], k_st[b][:, keys], q_st[b][:], start=True, stop=False)
                            pe.matmul(st_bank(j)[:], mask_sb[:, keys], idents[:], start=False,
                                      stop=True).then_inc(st_ready, 1)
                            if after:
                                if j == 0:
                                    pe.wait_ge(kq_in[1 - b], 96 * (pair + 1 + b))
                                for n in chunks_at(j):
                                    score(g + 1, 1 - b, n)
                                if j == 15:
                                    spread_max(g + 1)
                        if j >= LAG:
                            weigh(g, b, j - LAG)
                        elif before:
                            weigh(g - 1, 1 - b, KT - LAG + j)

                project_v(0)
                project_v(1)
                pe.wait_ge(lo_kept, NC + 1)
                pe.wait_ge(kq_in[0], 96)
                for n in range(16):
                    score(0, 0, n)
                    if n == 7:
                        project_v(2)
                project_v(3)
                spread_max(0)
                pe.wait_ge(lo_kept, 2 * NC + 1)
                pe.wait_ge(mask_ready, 2)
                step(0, 0, 0, before=False)
                with pe.Fori(0, NG // 2 - 1) as i:
                    step(i * 2 + 1, 1, i)
                    step(i * 2 + 2, 0, i + 1)
                step(NG - 1, 1, NG // 2 - 1, after=False)
                step(NG, 0, 0, this=False)
                pe.wait_ge(own, 3)
                for h in range(HG):
                    mm = pe.matmul(core.bank[1][:], o_parts[:, 0, h * P:(h + 1) * P], w_o[:, h, :], start=(h == 0),
                                   stop=(h == HG - 1))
                mm.then_inc(out_ready, 1)

            @block.scalar
            def _(act):
                norm.scalar(act)
                for n in range(NC):
                    act.wait_ge(k_proj, n + 1)
                    act.activation(k_hi[:, n * 512:(n + 1) * 512], k_bank(n)[:], ACT.Copy).then_inc(hi_kept, 1)
                act.wait_ge(q_proj, 1)
                act.activation(q_hi[:], core.bank[5][:], ACT.Copy, scale=float(E ** -0.5)).then_inc(hi_kept, 1)
                for n in range(4):
                    act.wait_ge(v_proj, n + 1)
                    act.activation(v_hi[:, 4 * n:4 * n + 4, :], v_bank(n)[:].rearrange("p (k d) -> p k d", k=4),
                                   ACT.Copy).then_inc(hi_kept, 1)

                def keep_max(g, b):
                    act.wait_ge(m_ready, g + 1)
                    act.activation(q_st[b][64:128, :], core.bank[4][64:128, :], ACT.Copy).then_inc(m_hi_kept, 1)

                def keep_output(g, b, earlier):
                    act.wait_ge(pv_done, g * 16 + 16 + 8)
                    act.wait_ge(o_in[b], earlier * 48 + 48)
                    act.activation(o_st[b][:], out_bank(b)[0:VW, :], ACT.Copy).then_inc(o_kept, 1)

                def keep_v(g, b):
                    for half, v in enumerate((v_hi, v_lo)):
                        copy = act.activation(v_st[b][:, :, half * E:(half + 1) * E],
                                              bits(v[:, :, bass.ds(g * E, E)]), ACT.Copy)
                    copy.then_inc(v_kept, 1)

                def round_p(g, j):
                    act.wait_ge(exp_done, g * 16 + j + 1 + 4)
                    act.wait_ge(pv_done, g * 16 + j + 1)
                    act.activation(p_hi[:, j % 8, :], e_t[:, j % 4, :], ACT.Copy).then_inc(hi_ready, 1)

                def step(g, b, before=None, after=True):
                    for j in range(KT):
                        act.wait_ge(st_ready, g * 16 + j + 1)
                        act.wait_ge(lo_ready[j % 2], g * 8 + j // 2 + 1)
                        act.activation(e_t[:, j % 4, :], st_bank(j)[:], ACT.Exp).then_inc(exp_done, 1)
                        if j > 0:
                            round_p(g, j - 1)
                        if before is not None and j == LAG + 1:
                            keep_output(g - 1, 1 - b, before)
                        if after and j == 8:
                            keep_v(g + 1, 1 - b)
                        if after and j == 15:
                            keep_max(g + 1, 1 - b)
                    round_p(g, KT - 1)

                keep_max(0, 0)
                act.wait_ge(stacks_blank, 2)
                act.wait_ge(lo_kept, 2 * NC + 1)
                keep_v(0, 0)
                step(0, 0)
                with act.Fori(0, NG // 2 - 1) as i:
                    step(i * 2 + 1, 1, before=i)
                    step(i * 2 + 2, 0, before=i)
                step(NG - 1, 1, before=NG // 2 - 1, after=False)
                keep_output(NG - 1, 1, NG // 2 - 1)

            @block.vector
            def _(dve):
                norm.vector(dve)
                for ahead, by in ((exp_done, 4), (lo_ready[0], 2), (lo_ready[1], 2), (pv_done, 8), (o_in[0], 48), (o_in[1], 48)):
                    dve.sem_inc(ahead, by)
                dve.wait_ge(mask_in, 32)
                dve.tensor_scalar(mask_sb[:], mask_b[:], 1.0, -MASKED, ALU.subtract, ALU.mult).then_inc(mask_ready, 1)
                for n in range(NC):
                    dve.wait_ge(hi_kept, n + 1)
                    at = slice(n * 512, (n + 1) * 512)
                    dve.tensor_tensor(k_lo[:, at], k_bank(n)[:], bits(k_hi[:, at]), ALU.subtract).then_inc(lo_kept, 1)
                dve.wait_ge(hi_kept, NC + 1)
                dve.scalar_tensor_tensor(q_lo[:], core.bank[5][:], float(E ** -0.5), bits(q_hi[:]), ALU.mult,
                                         ALU.subtract).then_inc(lo_kept, 1)
                dve.tensor_copy(idents[:], ident_in[:]).then_inc(mask_ready, 1)
                dve.wait_ge(mask_ready, 2)

                def split_v(n):
                    dve.wait_ge(hi_kept, NC + 2 + n)
                    at = slice(4 * n, 4 * n + 4)
                    dve.tensor_tensor(v_lo[:, at, :], v_bank(n)[:].rearrange("p (k d) -> p k d", k=4),
                                      bits(v_hi[:, at, :]), ALU.subtract).then_inc(lo_kept, 1)

                def take_max(g, n):
                    h, c = n // NC, n % NC
                    dve.wait_ge(s_ready, g * 16 + n + 1)
                    dve.sem_inc(s_seen, 1)
                    if not (isinstance(g, int) and n < 2):
                        dve.wait_ge(s_read, g * 16 + n - 1)
                        dve.sem_inc(s_seen, 1)
                    dve.tensor_tensor_reduce(junk[:, n % 2, :], s_bank(n)[:], bits(mask_sb[:, c * 512:(c + 1) * 512]), 1.0,
                                             LOWEST, ALU.add, ALU.max, part_max[:, h, c:c + 1]).then_inc(s_read, 1)
                    if c == NC - 1:
                        dve.wait_ge(s_read, g * 16 + n + 1)
                        dve.tensor_reduce(neg_max[:, h:h + 1], part_max[:, h, :], AX.X, ALU.max,
                                          negate=True).then_inc(max_ready, 1)
                        dve.wait_ge(max_ready, g * 4 + h + 1)
                        dve.tensor_scalar(diag[:, h, :], core.ident[:], neg_max[:, h:h + 1], None,
                                          ALU.mult).then_inc(diag_ready, 1)

                def keep_max(g, b):
                    dve.wait_ge(m_hi_kept, g + 1)
                    rows = slice(96, 128)
                    dve.tensor_tensor(q_st[b][rows, :], core.bank[4][rows, :], bits(q_st[b][rows, :]),
                                      ALU.subtract).then_inc(m_kept, 1)

                def low_half(g, j):
                    dve.wait_ge(hi_ready, g * 16 + j + 1)
                    dve.tensor_tensor(p_lo[:, j % 8, :], e_t[:, j % 4, :], bits(p_hi[:, j % 8, :]),
                                      ALU.subtract).then_inc(lo_ready[1], 1)

                def step(g, b, after=True):
                    for j in range(KT):
                        if after:
                            for n in chunks_at(j):
                                take_max(g + 1, n)
                        if j % 2 and j > 1:
                            low_half(g, j - 2)
                    if after:
                        keep_max(g + 1, 1 - b)
                    low_half(g, KT - 1)

                split_v(0)
                split_v(1)
                for n in range(16):
                    take_max(0, n)
                    if n == 7:
                        split_v(2)
                split_v(3)
                keep_max(0, 0)
                step(0, 0)
                with dve.Fori(0, NG // 2 - 1) as i:
                    step(i * 2 + 1, 1)
                    step(i * 2 + 2, 0)
                step(NG - 1, 1, after=False)
                steps = Steps(dve, own)
                for b in range(2):
                    dve.wait_ge(o_in[b], 3 * 16 * (NG // 2) + 48)
                steps.then(dve.tensor_tensor(o_parts[:, 0, :], o_parts[:, 0, :], o_parts[:, 1, :], ALU.add))
                steps.then(dve.reciprocal(o_parts[:, 2, :], o_parts[:, 2, :]))
                steps.then(dve.tensor_tensor(o_parts[:, 0, :], o_parts[:, 0, :], o_parts[:, 2, :], ALU.mult))
                dve.wait_ge(out_ready, 1)
                dve.tensor_tensor(core.x[:], core.x[:], core.bank[1][:], ALU.add)


def latent_attention(core, name, a, causal, eps_inside):
    nc = core.nc
    QR, KR, RD = 192, 64, 64
    LO = QR - P
    PE_W = HG * RD
    SCALE = float((HD + RD) ** -0.5)
    with Stage(core, name) as st:
        w_a = st.sb("w_a", [P, CT, QR + KR + RD])
        row_sb = st.sb("rows", [P, QR + KR])
        rot = st.sb("rot", [P, 2, RD])
        masked = st.sb("mask", [P, P])
        w_hi = [st.sb(f"w_hi{b}", [P, HG * HD + PE_W]) for b in range(2)]
        w_lo = [st.sb(f"w_lo{b}", [LO, HG * HD + PE_W + 2 * HG * HD]) for b in range(2)]
        w_o = [st.sb(f"w_o{b}", [P, HG, D]) for b in range(2)]
        w_a_in = st.sem("w_a_in")
        rows_in = st.sem("rows_in")
        w_in = [st.sem(f"w_in{b}") for b in range(2)]
        o_in = [st.sem(f"o_in{b}") for b in range(2)]

        def issue(sp):
            sp.dma_start(w_a[:], a["w_a"]).then_inc(w_a_in, 16)
            sp.dma_start(row_sb[:], a["rows"].to_broadcast([P, QR + KR])).then_inc(rows_in, 16)
            sp.dma_start(rot[:], a["rot"]).then_inc(rows_in, 16)
            sp.dma_start(masked[:], a["causal"]).then_inc(rows_in, 16)
            for b in range(2):
                sp.dma_start(w_hi[b][:], a["hi"][b]).then_inc(w_in[b], 16)
                sp.dma_start(w_lo[b][:], a["lo"][b]).then_inc(w_in[b], 16)
                sp.dma_start(w_o[b][:], a["o"][b]).then_inc(o_in[b], 16)

        following = yield issue
        norm = LayerNorm(core, st, core.bank[0])
        junk = st.sb("junk", [P, QR])
        sumsq = st.sb("sumsq", [P, 2])
        rstd = st.sb("rstd", [P, 2])
        lat = st.sb("lat", [P, QR + KR])
        k_pe = st.sb("k_pe", [P, RD])
        k_sw = st.sb("k_sw", [P, RD])
        lat_hi = st.sb("lat_hi", [P, P])
        lat_lo = st.sb("lat_lo", [LO, 3, P])
        q_t = st.sb("q_t", [P, HG, P])
        k_t = st.sb("k_t", [P, HG, P])
        v_sb = [st.sb(f"v{b}", [P, HG, HD]) for b in range(2)]
        q_pe = st.sb("q_pe", [P, HG, RD])
        q_sw = st.sb("q_sw", [P, HG, RD])
        q_pe_t = st.sb("q_pe_t", [RD, HG, P])
        s_sb = [st.sb(f"s{b}", [P, HG, P]) for b in range(2)]
        neg_max = st.sb("neg_max", [P, HG])
        row_sum = st.sb("row_sum", [P, HG])
        r_sum = st.sb("r_sum", [P, HG])
        p_t = st.sb("p_t", [P, HG, P])
        o_t = st.sb("o_t", [P, HG, P])
        own = st.sem("own")
        rows_scaled = st.sem("rows_scaled")
        lat_proj = st.sem("lat_proj")
        squared = st.sem("squared")
        rms_ready = st.sem("rms_ready")
        lat_ready = st.sem("lat_ready")
        lat_turned = st.sem("lat_turned")
        lat_t_ready = st.sem("lat_t_ready")
        q_proj = st.sem("q_proj")
        k_proj = st.sem("k_proj")
        v_proj = st.sem("v_proj")
        pe_proj = st.sem("pe_proj")
        q_copied = st.sem("q_copied")
        v_copied = st.sem("v_copied")
        k_copied = st.sem("k_copied")
        pe_read = st.sem("pe_read")
        pe_ready = st.sem("pe_ready")
        pe_turned = st.sem("pe_turned")
        pe_copied = st.sem("pe_copied")
        s_ready = st.sem("s_ready")
        s_masked = st.sem("s_masked")
        max_ready = st.sem("max_ready")
        exp_ready = st.sem("exp_ready")
        recip_ready = st.sem("recip_ready")
        p_ready = st.sem("p_ready")
        p_turned = st.sem("p_turned")
        p_t_ready = st.sem("p_t_ready")
        o_ready = st.sem("o_ready")
        o_t_ready = st.sem("o_t_ready")
        wo_done = st.sem("wo_done")
        x_added = st.sem("x_added")
        banks = core.bank
        per_head = lambda bank: bank[:].rearrange("p (h q) -> p h q", h=HG)

        with nc.Block() as block:
            @block.gpsimd
            def _(pool):
                core.clear_stale(pool)

            @block.sync
            def _(sp):
                following(sp)
                def load_projections(n, b):
                    sp.wait_ge(v_proj, n - 1)
                    sp.dma_start(w_hi[b][:], a["hi"][n]).then_inc(w_in[b], 16)
                    sp.dma_start(w_lo[b][:], a["lo"][n]).then_inc(w_in[b], 16)

                def load_output(n, b):
                    sp.wait_ge(wo_done, n - 1)
                    sp.dma_start(w_o[b][:], a["o"][n]).then_inc(o_in[b], 16)

                load_projections(2, 0)
                load_projections(3, 1)
                with sp.Fori(0, NG // 2 - 2) as i:
                    for b in range(2):
                        load_output(i * 2 + (2 + b), b)
                        load_projections(i * 2 + (4 + b), b)
                load_output(NG - 2, 0)
                load_output(NG - 1, 1)

            @block.tensor
            def _(pe):
                norm.tensor(pe)
                pe.wait_ge(w_a_in, 16)
                for c in range(CT):
                    mm = pe.matmul(banks[0][:, 0:QR + KR + RD], core.xn_t[:, c, :], w_a[:, c, :], start=(c == 0),
                                   stop=(c == CT - 1))
                mm.then_inc(lat_proj, 1)
                pe.wait_ge(lat_ready, 1)
                pe.transpose(banks[1][:, 0:P], lat[:, 0:P], core.ident[:])
                pe.transpose(banks[1][0:LO, P:2 * P], lat[:, P:QR], core.ident[:])
                pe.transpose(banks[1][0:KR, 2 * P:3 * P], lat[:, QR:], core.ident[:])
                pe.transpose(banks[1][0:RD, 3 * P:4 * P], k_pe[:], core.ident[:]).then_inc(lat_turned, 1)
                pe.wait_ge(lat_t_ready, 2)

                KO = HG * HD + PE_W

                def project(g, b, i):
                    pe.wait_ge(w_in[b], i * 32 + 32)
                    pe.wait_ge(pe_read, g + 1)
                    pe.matmul(banks[3][:, 0:PE_W], lat_hi[:], w_hi[b][:, HG * HD:], start=True, stop=False)
                    pe.matmul(banks[3][:, 0:PE_W], lat_lo[:, 0, :], w_lo[b][:, HG * HD:KO], start=False,
                              stop=True).then_inc(pe_proj, 1)
                    pe.wait_ge(q_copied, g + 1)
                    for h in range(HG):
                        pe.matmul(banks[0][:, h * P:(h + 1) * P], w_hi[b][:, h * HD:(h + 1) * HD], lat_hi[:],
                                  start=True, stop=False)
                        mm = pe.matmul(banks[0][:, h * P:(h + 1) * P], w_lo[b][:, h * HD:(h + 1) * HD],
                                       lat_lo[:, 0, :], start=False, stop=True)
                    mm.then_inc(q_proj, 1)
                    pe.wait_ge(k_copied, g + 1)
                    for h in range(HG):
                        mm = pe.matmul(banks[1][:, h * P:(h + 1) * P], w_lo[b][:, KO + h * HD:KO + (h + 1) * HD],
                                       lat_lo[:, 1, :], start=True, stop=True)
                    mm.then_inc(k_proj, 1)
                    pe.wait_ge(v_copied, g + 1)
                    pe.matmul(banks[2][:], lat_lo[:, 1, :], w_lo[b][:, KO + HG * HD:], start=True,
                              stop=True).then_inc(v_proj, 1)

                def turn_rotary(g):
                    pe.wait_ge(pe_ready, g + 1)
                    pe.wait_ge(pe_copied, g + 1)
                    for j in range(HG // 2):
                        mm = pe.transpose(banks[4][:, j * P:(j + 1) * P],
                                          q_pe[:, 2 * j:2 * j + 2, :].rearrange("p h e -> p (h e)"),
                                          core.ident[:])
                    mm.then_inc(pe_turned, 1)

                def score(g):
                    pe.wait_ge(q_copied, g + 2)
                    pe.wait_ge(k_copied, g + 2)
                    pe.wait_ge(pe_copied, g + 2)
                    pe.wait_ge(s_masked, g + 1)
                    for h in range(HG):
                        pe.matmul(banks[5][:, h * P:(h + 1) * P], q_t[:, h, :], k_t[:, h, :], start=True, stop=False)
                        mm = pe.matmul(banks[5][:, h * P:(h + 1) * P], q_pe_t[:, h, :], lat_lo[:, 2, :],
                                       start=False, stop=True)
                    mm.then_inc(s_ready, 1)

                def turn_probabilities(g, b):
                    pe.wait_ge(p_ready, g + 1)
                    pe.wait_ge(x_added, g + 1)
                    for h in range(HG):
                        mm = pe.transpose(banks[6][:, h * P:(h + 1) * P], s_sb[b][:, h, :], core.ident[:])
                    mm.then_inc(p_turned, 1)

                def weigh(g, b):
                    pe.wait_ge(p_t_ready, g + 1)
                    pe.wait_ge(v_copied, g + 2)
                    pe.wait_ge(o_t_ready, g + 1)
                    for h in range(HG):
                        mm = pe.matmul(banks[7][:, h * P:(h + 1) * P], v_sb[b][:, h, :], p_t[:, h, :], start=True,
                                       stop=True)
                    mm.then_inc(o_ready, 1)

                def project_out(g, b, i):
                    pe.wait_ge(o_t_ready, g + 2)
                    pe.wait_ge(o_in[b], i * 16 + 16)
                    for h in range(HG):
                        mm = pe.matmul(banks[6][:], o_t[:, h, :], w_o[b][:, h, :], start=(h == 0),
                                       stop=(h == HG - 1))
                    mm.then_inc(wo_done, 1)

                def step(g, b, i, before=True, this=True, after=True):
                    prev_i, next_i = (i, i + 1) if b else (i - 1, i)
                    if this:
                        score(g)
                    if before:
                        turn_probabilities(g - 1, 1 - b)
                    if after:
                        project(g + 1, 1 - b, next_i)
                    if before:
                        weigh(g - 1, 1 - b)
                    if after:
                        turn_rotary(g + 1)
                    if before:
                        project_out(g - 1, 1 - b, prev_i)

                project(0, 0, 0)
                turn_rotary(0)
                step(0, 0, 0, before=False)
                with pe.Fori(0, NG // 2 - 1) as i:
                    step(i * 2 + 1, 1, i)
                    step(i * 2 + 2, 0, i + 1)
                step(NG - 1, 1, NG // 2 - 1, after=False)
                step(NG, 0, NG // 2, this=False, after=False)

            @block.scalar
            def _(act):
                norm.scalar(act)
                for one_ahead in (q_copied, v_copied, o_t_ready):
                    act.sem_inc(one_ahead, 1)
                act.wait_ge(lat_proj, 1)
                act.activation(junk[:], banks[0][:, 0:QR], ACT.Square, accum_out=sumsq[:, 0:1]).then_inc(squared, 1)
                act.wait_ge(squared, 1)
                act.activation(junk[:, 0:KR], banks[0][:, QR:QR + KR], ACT.Square,
                               accum_out=sumsq[:, 1:2]).then_inc(squared, 1)
                act.wait_ge(squared, 2)
                bias = core.eps5[:] if eps_inside else core.zero[:]
                act.activation(rstd[:, 0:1], sumsq[:, 0:1], ACT.Sqrt, bias=bias, scale=1.0 / QR).then_inc(rms_ready, 1)
                act.activation(rstd[:, 1:2], sumsq[:, 1:2], ACT.Sqrt, bias=bias, scale=1.0 / KR).then_inc(rms_ready, 1)

                def keep_q(g):
                    act.wait_ge(q_proj, g + 1)
                    if not (isinstance(g, int) and g == 0):
                        act.wait_ge(s_ready, g)
                    act.activation(q_t[:], per_head(banks[0]), ACT.Copy).then_inc(q_copied, 1)

                def keep_v(g, b, used=True):
                    act.wait_ge(v_proj, g + 1)
                    if used:
                        act.wait_ge(o_ready, g - 1)
                    act.activation(v_sb[b][:], per_head(banks[2]), ACT.Copy).then_inc(v_copied, 1)

                def step(g, b, before=True, this=True, after=True):
                    if before:
                        act.wait_ge(p_turned, g)
                        act.activation(p_t[:], per_head(banks[6]), ACT.Copy).then_inc(p_t_ready, 1)
                    if this:
                        act.wait_ge(max_ready, g + 1)
                        for h in range(HG):
                            act.activation(s_sb[b][:, h, :], s_sb[b][:, h, :], ACT.Exp, bias=neg_max[:, h:h + 1],
                                           scale=1.0, accum_out=row_sum[:, h:h + 1]).then_inc(exp_ready, 1)
                    if after:
                        keep_q(g + 1)
                    if before:
                        act.wait_ge(o_ready, g)
                        act.activation(o_t[:], per_head(banks[7]), ACT.Copy).then_inc(o_t_ready, 1)
                    if after:
                        keep_v(g + 1, 1 - b, used=before)

                keep_q(0)
                keep_v(0, 0, used=False)
                step(0, 0, before=False)
                with act.Fori(0, NG // 2 - 1) as i:
                    step(i * 2 + 1, 1)
                    step(i * 2 + 2, 0)
                step(NG - 1, 1, after=False)
                step(NG, 0, this=False, after=False)

            @block.vector
            def _(dve):
                norm.vector(dve)
                for one_ahead in (k_copied, pe_read, pe_copied, s_masked, x_added):
                    dve.sem_inc(one_ahead, 1)
                steps = Steps(dve, own)
                dve.wait_ge(rows_in, 48)
                dve.tensor_scalar(row_sb[:, 0:QR], row_sb[:, 0:QR], SCALE, None, ALU.mult).then_inc(rows_scaled, 1)
                dve.wait_ge(rms_ready, 2)
                if not eps_inside:
                    steps.then(dve.tensor_scalar(rstd[:], rstd[:], 1e-6, None, ALU.add))
                steps.then(dve.reciprocal(rstd[:], rstd[:]))
                dve.wait_ge(rows_scaled, 1)
                steps.then(dve.scalar_tensor_tensor(lat[:, 0:QR], banks[0][:, 0:QR], rstd[:, 0:1], row_sb[:, 0:QR],
                                                    ALU.mult, ALU.mult))
                steps.then(dve.scalar_tensor_tensor(lat[:, QR:], banks[0][:, QR:QR + KR], rstd[:, 1:2],
                                                    row_sb[:, QR:], ALU.mult, ALU.mult))
                half = RD // 2
                src = banks[0][:, QR + KR:QR + KR + RD]
                steps.then(dve.tensor_tensor(k_pe[:], src, rot[:, 0, :], ALU.mult))
                steps.then(dve.tensor_tensor(k_sw[:, 0:half], src[:, half:], rot[:, 1, 0:half], ALU.mult))
                steps.then(dve.tensor_tensor(k_sw[:, half:], src[:, 0:half], rot[:, 1, half:], ALU.mult))
                dve.tensor_tensor(k_pe[:], k_pe[:], k_sw[:], ALU.add).then_inc(lat_ready, 1)
                dve.wait_ge(lat_turned, 1)
                dve.tensor_copy(lat_hi[:], banks[1][:, 0:P]).then_inc(lat_t_ready, 1)
                dve.tensor_copy(lat_lo[:], banks[1][0:LO, P:].rearrange("p (t q) -> p t q", t=3)).then_inc(lat_t_ready, 1)

                def keep(g):
                    dve.wait_ge(pe_proj, g + 1)
                    if not (isinstance(g, int) and g == 0):
                        dve.wait_ge(pe_turned, g)
                    src = banks[3][:, 0:PE_W].rearrange("p (h e) -> p h e", h=HG)
                    wide, thin = [P, HG, RD], [P, HG, half]
                    cos = rot[:, 0, :].unsqueeze(1).to_broadcast(wide)
                    lo = rot[:, 1, 0:half].unsqueeze(1).to_broadcast(thin)
                    hi = rot[:, 1, half:].unsqueeze(1).to_broadcast(thin)
                    dve.tensor_tensor(q_pe[:], src, cos, ALU.mult)
                    dve.tensor_tensor(q_sw[:, :, 0:half], src[:, :, half:], lo, ALU.mult)
                    dve.tensor_tensor(q_sw[:, :, half:], src[:, :, 0:half], hi, ALU.mult).then_inc(pe_read, 1)
                    dve.wait_ge(pe_read, g + 2)
                    dve.tensor_tensor(q_pe[:], q_pe[:], q_sw[:], ALU.add).then_inc(pe_ready, 1)
                    dve.wait_ge(k_proj, g + 1)
                    if not (isinstance(g, int) and g == 0):
                        dve.wait_ge(s_ready, g)
                    dve.tensor_copy(k_t[:], per_head(banks[1])).then_inc(k_copied, 1)

                def turn_rotary(g):
                    dve.wait_ge(pe_turned, g + 1)
                    if not (isinstance(g, int) and g == 0):
                        dve.wait_ge(s_ready, g)
                    for odd in range(2):
                        copy = dve.tensor_copy(
                            q_pe_t[:, odd:HG:2, :],
                            banks[4][odd * RD:(odd + 1) * RD, 0:2 * P].rearrange("p (h q) -> p h q", h=HG // 2))
                    copy.then_inc(pe_copied, 1)

                def step(g, b, before=True, this=True, after=True):
                    if this:
                        dve.wait_ge(s_ready, g + 1)
                        if causal:
                            dve.tensor_tensor(s_sb[b][:], per_head(banks[5]),
                                              masked[:].unsqueeze(1).to_broadcast([P, HG, P]),
                                              ALU.add).then_inc(s_masked, 1)
                        else:
                            dve.tensor_copy(s_sb[b][:], per_head(banks[5])).then_inc(s_masked, 1)
                        dve.wait_ge(s_masked, g + 2)
                        dve.tensor_reduce(neg_max[:], s_sb[b][:], AX.X, ALU.max, negate=True).then_inc(max_ready, 1)
                    if after:
                        keep(g + 1)
                    if this:
                        dve.wait_ge(exp_ready, g * 4 + 4)
                        dve.reciprocal(r_sum[:], row_sum[:]).then_inc(recip_ready, 1)
                        dve.wait_ge(recip_ready, g + 1)
                        dve.tensor_tensor(s_sb[b][:], s_sb[b][:], r_sum[:].unsqueeze(2).to_broadcast([P, HG, P]),
                                          ALU.mult).then_inc(p_ready, 1)
                    if after:
                        turn_rotary(g + 1)
                    if before:
                        dve.wait_ge(wo_done, g)
                        dve.tensor_tensor(core.x[:], core.x[:], banks[6][:], ALU.add).then_inc(x_added, 1)

                keep(0)
                turn_rotary(0)
                step(0, 0, before=False)
                with dve.Fori(0, NG // 2 - 1) as i:
                    step(i * 2 + 1, 1)
                    step(i * 2 + 2, 0)
                step(NG - 1, 1, after=False)
                step(NG, 0, this=False, after=False)


def latent_inputs(a, name):
    return {"w_a": a[f"{name}_w"], "rows": a[f"{name}_rows"], "rot": a["latent_rot"], "causal": a["causal"],
            "hi": a[f"{name}_hi"], "lo": a[f"{name}_lo"], "o": a[f"{name}_o"]}


STAGE_OF = {
    "L0x": lambda core, name, a: wide_cross_attention(
        core, name, a["L0x_kqv"], a["L0x_o"], a["L0x_mask"], a["ctx_t"],
        rotary=(a["L0x_cos"], a["L0x_sin"], a["L0x_cos_q"], a["L0x_sin_q"])),
    "L0a": lambda core, name, a: per_token_head_attention(core, name, a["L0a_w"], a["L0a_rows"], a),
    "L0f": lambda core, name, a: adapter_ffn(core, name, a["L0f_w"], a["L0f_rows"], a["L0f_up"], 3, 16,
                                             starts=a["L0f_starts"], clamp_iota=a["iota8"][:, 0:3]),
    "L1f": lambda core, name, a: adapter_ffn(core, name, a["L1f_w"], a["L1f_rows"], a["L1f_up"], 8, 16,
                                             gate=True, clamp_iota=a["iota8"]),
    "L1x": lambda core, name, a: feature_cross_attention(core, name, a),
    "L1a": lambda core, name, a: latent_attention(core, name, latent_inputs(a, "L1a"), True, True),
    "L2x": lambda core, name, a: narrow_cross_attention(core, name, a["L2x_w"], a["L2x_o"], a["L2x_mask"],
                                                        a["ident_4"], a["ctx_t"]),
    "L2a": lambda core, name, a: latent_attention(core, name, latent_inputs(a, "L2a"), False, False),
    "L2f": lambda core, name, a: mixed_adapter_ffn(core, name, a["L2f_w"], a["L2f_keys"], a["L2f_up"]),
    "L3a": lambda core, name, a: single_head_attention(core, name, a["L3a_w"], a["L3a_o"], a["L3a_cols"],
                                                       a["L3a_rows"]),
    "L3f": lambda core, name, a: codebook_ffn(core, name, a["L3f_books"], a["L3f_codes"], a["L3f_entry"],
                                              a["L3f_rows"]),
    "L3x": lambda core, name, a: wide_cross_attention(
        core, name, a["L3x_kqv"], a["L3x_o"], a["L3x_mask"], a["ctx_t"], norm_cols=a["L3x_cols"]),
}
STAGES = ("L0x", "L0a", "L0f", "L1x", "L1a", "L1f", "L2x", "L2a", "L2f", "L3x", "L3a", "L3f")


def load_start(core, a, following):
    nc = core.nc
    with Stage(core, "start") as st:
        loaded = st.sem("loaded")
        with nc.Block() as block:
            @block.sync
            def _(sp):
                sp.dma_start(core.x[:], a["x"]).then_inc(loaded, 16)
                sp.dma_start(core.ident[:], a["ident"]).then_inc(loaded, 16)
                following(sp)
                sp.wait_ge(loaded, 32)

            @block.gpsimd
            def _(pool):
                pool.memset(core.ones[:], 1.0)
                pool.memset(core.ones_r[:].bitcast(F32), 1.0)
                pool.memset(core.zero[:], 0.0)
                pool.memset(core.eps5[:], 1e-5)
                pool.memset(core.eps6[:], 1e-6)


def store_result(core, out):
    nc = core.nc
    with Stage(core, "end") as st:
        stored = st.sem("stored")
        with nc.Block() as block:
            @block.gpsimd
            def _(pool):
                core.clear_stale(pool)

            @block.sync
            def _(sp):
                sp.dma_start(out, core.x[:]).then_inc(stored, 16)
                sp.wait_ge(stored, 16)

        with nc.Block() as block:
            @block.gpsimd
            def _(pool):
                pool.sem_clear(stored)


def perceiver(nc, a, out, stages=STAGES):
    with ExitStack() as ctx:
        core = Core(nc, ctx)
        stage = STAGE_OF[stages[0]](core, stages[0], a)
        load_start(core, a, next(stage))
        for name in (*stages[1:], None):
            coming = STAGE_OF[name](core, name, a) if name else None
            following = next(coming) if coming else (lambda sp: None)
            try:
                stage.send(following)
            except StopIteration:
                pass
            stage = coming
        store_result(core, out)
        core.freed.close()


def by_feature(w):
    return w.reshape(CT, P, -1).transpose(1, 0, 2)


def grouped(w_q, w_k, w_v, w_o):
    per_group = []
    for g in range(NG):
        cols = [w_k[:, g * HD:(g + 1) * HD], w_v[:, g * HD:(g + 1) * HD], w_q[:, g * HG * HD:(g + 1) * HG * HD]]
        per_group.append(by_feature(np.concatenate(cols, axis=1)))
    return np.stack(per_group), w_o.reshape(NG, HG, HD, D).transpose(0, 2, 1, 3)


def rotary_angles(width, positions):
    inv = (1.0 / 10000.0 ** (np.arange(0, width, 2, dtype=np.float32) / np.float32(width))).astype(np.float32)
    return np.arange(positions, dtype=np.float32)[:, None] * inv[None, :]


def layouts(i):
    f = np.float32
    a = {"x": i["x"][0], "ident": np.eye(P, dtype=f), "ctx_t": by_feature(i["ctx_4096"][0].T)}
    a["L0x_kqv"], a["L0x_o"] = grouped(i["L0_xattn_wq"], i["L0_xattn_wk"], i["L0_xattn_wv"], i["L0_xattn_wo"])
    a["L0x_mask"] = i["mask_BxSxS2_ff0"][0]
    ang = rotary_angles(HD, SK).T
    cos, sin = np.cos(ang).astype(f), np.sin(ang).astype(f)
    scale = f(1.0) / np.sqrt(f(HD))
    a["L0x_cos"] = np.concatenate([cos, cos])
    a["L0x_sin"] = np.concatenate([-sin, sin])
    a["L0x_cos_q"] = a["L0x_cos"][:, :P] * scale
    a["L0x_sin_q"] = a["L0x_sin"][:, :P] * scale
    a["L3x_kqv"], a["L3x_o"] = grouped(i["L3_xattn_q_proj_w"].T, i["L3_xattn_k_proj_w"].T,
                                       i["L3_xattn_v_proj_w"].T, i["L3_xattn_o_proj_w"].T)
    a["L3x_mask"] = i["mask_1x1xSxS2_ff0"][0, 0]
    a["L3x_cols"] = np.stack([i["L3_xattn_q_norm_w"], i["L3_xattn_k_norm_w"]], axis=1)
    row = lambda *parts: np.concatenate(parts)[None, :]
    beside = lambda *parts: by_feature(np.concatenate(parts, axis=1))
    a["iota8"] = np.arange(8, dtype=f)[None, :]
    a["L0a_w"] = beside(*(i[f"L0_attn_W{n}"].T for n in "qkvo"))
    a["L0a_rows"] = row(*(i[f"L0_attn_b{n}"] for n in "qkvo"))
    a["L0f_w"] = beside(i["L0_ffn_weight"].T, i["L0_ffn_lora_A"].reshape(48, D).T)
    a["L0f_rows"] = row(i["L0_ffn_bias"])
    a["L0f_up"] = i["L0_ffn_lora_B"].transpose(0, 2, 1).reshape(48, D)
    a["L0f_starts"] = i["L0_ffn_lora_start_indices"][None, :]
    a["L1f_w"] = beside(i["L1_ffn_base_w"].T, i["L1_ffn_lora_A"].reshape(P, D).T, i["L1_ffn_gate_w"].T)
    a["L1f_rows"] = row(i["L1_ffn_base_b"])
    a["L1f_up"] = i["L1_ffn_lora_B"].transpose(0, 2, 1).reshape(P, D)
    a["L2f_w"] = beside(i["L2_ffn_W_org"].T, i["L2_ffn_lora_down"].transpose(1, 0, 2).reshape(D, D),
                        i["L2_ffn_Wq"].T)
    a["L2f_keys"] = i["L2_ffn_lora_keys"].T
    a["L2f_up"] = by_feature(i["L2_ffn_lora_up"].reshape(D, D))
    a["L3a_w"] = by_feature(i["L3_attn_Wqkv"])
    a["L3a_o"] = i["L3_attn_Wo"]
    a["L3a_cols"] = i["L3_attn_bqkv"][:2 * HD].reshape(2, HD).T
    a["L3a_rows"] = row(i["L3_attn_bqkv"][2 * HD:], i["L3_attn_bo"])
    books = np.zeros((4, 32, 8, 2, 4, 16), f)
    for group in range(8):
        for book in range(4):
            books[book, :, group, group % 2, book] = i["L3_ffn_codebooks"][4 * group + book]
    a["L3f_books"] = books.reshape(P, 8, P)
    codes = np.concatenate([i["L3_ffn_codes"], i["L3_ffn_centroids"]], axis=1)
    codes = np.broadcast_to(codes.reshape(8, 4, 1, D + 32), (8, 4, 32, D + 32))
    a["L3f_codes"] = codes.transpose(1, 2, 0, 3).reshape(P, 8, D + 32)
    a["L3f_entry"] = np.tile(np.arange(32, dtype=f), 4)[:, None]
    a["L3f_rows"] = row(i["L3_ffn_bias"], i["L3_ffn_ln_weight"])
    a["L1x_w"] = beside(i["L1_xattn_Wq_w"].T, i["L1_xattn_Wk_w"].T)
    a["L1x_ctx"] = i["ctx_4096"][0].reshape(KT, P, D).transpose(1, 0, 2)
    a["L1x_cols"] = i["L1_xattn_fn_w"].reshape(CT, P).T
    a["L1x_rows"] = row(*(i[f"L1_xattn_{n}"] for n in ("Wq_b", "Wk_b", "qn_w", "kn_w", "fn_w")))
    ang = rotary_angles(64, P)
    cos, sin = np.cos(ang).astype(f), np.sin(ang).astype(f)
    a["latent_rot"] = np.stack([np.concatenate([cos, cos], 1), np.concatenate([-sin, sin], 1)], axis=1)
    a["causal"] = np.triu(np.full((P, P), LOWEST, f), 1)
    halves = np.r_[0:64:2, 1:64:2]
    a.update(latent_layouts("L1a", i["L1_attn_q_a_w"], i["L1_attn_kv_a_w"], i["L1_attn_q_a_norm_w"],
                            i["L1_attn_kv_a_norm_w"], i["L1_attn_q_b_w"], i["L1_attn_kv_b_w"],
                            i["L1_attn_o_w"], halves))
    a.update(latent_layouts("L2a", i["L2_attn_w_qa"], i["L2_attn_w_kva"], i["L2_attn_g_qa"],
                            i["L2_attn_g_kva"], i["L2_attn_w_qb"], i["L2_attn_w_kvb"], i["L2_attn_w_o"],
                            np.arange(64)))
    q_by_place = i["L2_xattn_w_q"].reshape(NG, HG, 16, D).transpose(1, 0, 2, 3).reshape(D, D)
    a["L2x_w"] = beside(i["L2_xattn_w_k"].T, i["L2_xattn_w_v"].T, q_by_place.T)
    a["L2x_o"] = i["L2_xattn_w_out"].T.reshape(NG, HG, 16, D).transpose(0, 2, 1, 3).reshape(P, HG, D)
    a["L2x_mask"] = i["mask_SxS2_bk0"]
    a["ident_4"] = np.tile(a["ident"], (1, HG))
    return a


def latent_layouts(name, q_a, kv_a, g_q, g_kv, q_b, kv_b, o, order):
    kv_a = np.concatenate([kv_a[:, :64], kv_a[:, 64:][:, order]], axis=1)
    q_b = q_b.reshape(192, NG, HG, 192).transpose(1, 0, 2, 3)
    q_b = np.concatenate([q_b[..., :128].reshape(NG, 192, 512), q_b[..., 128:][..., order].reshape(NG, 192, 256)], 2)
    kv_b = kv_b.reshape(64, NG, HG, 2, 128).transpose(1, 0, 3, 2, 4).reshape(NG, 64, 1024)
    return {f"{name}_w": by_feature(np.concatenate([q_a, kv_a], axis=1)),
            f"{name}_rows": np.concatenate([g_q, g_kv])[None, :],
            f"{name}_hi": q_b[:, :128], f"{name}_lo": np.concatenate([q_b[:, 128:], kv_b], axis=2),
            f"{name}_o": o.reshape(NG, HG, HD, D).transpose(0, 2, 1, 3)}


def kernel(**inputs):
    import concourse.bacc as bacc
    from concourse.bass_utils import run_bass_kernel_spmd

    laid = {k: np.ascontiguousarray(v) for k, v in layouts({k: np.asarray(v) for k, v in inputs.items()}).items()}
    nc = bacc.Bacc("TRN2", target_bir_lowering=False, num_devices=1)
    aps = {k: nc.dram_tensor(f"in_{k}", v.shape, mybir.dt.from_np(v.dtype), kind="ExternalInput").ap()
           for k, v in laid.items()}
    out = nc.dram_tensor("out", (P, D), F32, kind="ExternalOutput").ap()
    perceiver(nc, aps, out)
    result = run_bass_kernel_spmd(nc, [{f"in_{k}": v for k, v in laid.items()}], core_ids=[0])
    return result.results[0]["out"].reshape(1, P, D)
```
